# Optimizing a Trainium2 kernel written in Bass

```python
import numpy as np
import jax
import jax.numpy as jnp

def _softmax(x, axis=-1):
    return jax.nn.softmax(x, axis=axis)

def _gelu(x):
    return jax.nn.gelu(x, approximate=True)

def _silu(x):
    return jax.nn.silu(x)

def _sigmoid(x):
    return jax.nn.sigmoid(x)

def _layernorm(x, axis=-1, eps=1e-05):
    m = jnp.mean(x, axis=axis, keepdims=True)
    v = jnp.var(x, axis=axis, keepdims=True)
    return (x - m) / jnp.sqrt(v + eps)

def _scatter_add(tgt, idx, src, axis=0):
    return tgt.at[idx].add(src)

def _segment_sum(src, seg, n):
    return jax.ops.segment_sum(src, seg, n)
kernel_name = 'mk_macaron_d2_jaxref_r4_a6fd8c'

def setup_inputs(seed: int=0):
    np.random.seed(seed)
    _w = jnp.asarray

    def _L0_attn_setup():
        import jax, jax.numpy as jnp
        import numpy as np
        from jax import lax
        H = 256
        EXPAND = 2
        I = EXPAND * H
        N = 16
        K = 4
        R = 64
        EPS = 1e-06
        B_SZ, L = (2, 256)

        def rmsnorm(x, w):
            v = jnp.mean(x.astype(jnp.float32) ** 2, axis=-1, keepdims=True)
            return w * (x * jax.lax.rsqrt(v + EPS)).astype(x.dtype)
        key = jax.random.key(seed)
        ks = jax.random.split(key, 10)
        s = 0.02
        inp = {'hidden_states': jax.random.normal(ks[0], (B_SZ, L, H), jnp.float32), 'in_proj_w': jax.random.normal(ks[1], (2 * I, H), jnp.float32) * s, 'conv_w': jax.random.normal(ks[2], (I, 1, K), jnp.float32) * s, 'conv_b': jnp.zeros((I,), jnp.float32), 'x_proj_w': jax.random.normal(ks[3], (R + 2 * N, I), jnp.float32) * s, 'dt_proj_w': jax.random.normal(ks[4], (I, R), jnp.float32) * s, 'dt_proj_b': jax.random.normal(ks[5], (I,), jnp.float32) * 0.1, 'dt_ln_w': jnp.ones((R,), jnp.float32), 'b_ln_w': jnp.ones((N,), jnp.float32), 'c_ln_w': jnp.ones((N,), jnp.float32), 'A_log': jnp.log(jnp.broadcast_to(jnp.arange(1, N + 1, dtype=jnp.float32)[None, :], (I, N))), 'D': jnp.ones((I,), jnp.float32), 'out_proj_w': jax.random.normal(ks[6], (H, I), jnp.float32) * s}
        return inp
    _L0_attn_in = _L0_attn_setup()

    def _L0_ffn_setup():
        import jax, jax.numpy as jnp
        import numpy as np
        D_MODEL = 256
        EXPANSION = 4
        D_HIDDEN = D_MODEL * EXPANSION
        NUM_STAGES = int(np.log2(D_HIDDEN))

        def butterfly(y, weights, dim):
            lead = y.shape[:-1]
            for stage in range(weights.shape[0]):
                s = 2 ** stage
                nb = dim // (2 * s)
                yr = y.reshape(*lead, nb, 2, s)
                a = yr[..., 0, :]
                b = yr[..., 1, :]
                w = weights[stage].reshape(nb, s, 2, 2)
                na = w[..., 0, 0] * a + w[..., 0, 1] * b
                nb2 = w[..., 1, 0] * a + w[..., 1, 1] * b
                y = jnp.stack([na, nb2], axis=-2).reshape(*lead, dim)
            return y
        key = jax.random.key(seed)
        ks = jax.random.split(key, 6)
        B, S = (4, 512)
        x = jax.random.normal(ks[0], (B, S, D_MODEL), jnp.float32)
        W_exp = jax.random.normal(ks[1], (D_MODEL, D_HIDDEN), jnp.float32) * 0.02
        b_exp = jnp.zeros((D_HIDDEN,), jnp.float32)
        up_weights = jax.random.normal(ks[2], (NUM_STAGES, D_HIDDEN // 2, 2, 2), jnp.float32) * 0.02
        up_bias = jnp.zeros((D_HIDDEN,), jnp.float32)
        down_weights = jax.random.normal(ks[3], (NUM_STAGES, D_HIDDEN // 2, 2, 2), jnp.float32) * 0.02
        W_con = jax.random.normal(ks[4], (D_HIDDEN, D_MODEL), jnp.float32) * 0.02
        b_con = jnp.zeros((D_MODEL,), jnp.float32)
        down_bias = jnp.zeros((D_MODEL,), jnp.float32)
        return dict(x=x, W_exp=W_exp, b_exp=b_exp, up_weights=up_weights, up_bias=up_bias, down_weights=down_weights, W_con=W_con, b_con=b_con, down_bias=down_bias)
    _L0_ffn_in = _L0_ffn_setup()

    def _L1_attn_setup():
        import jax, jax.numpy as jnp
        import numpy as np
        D_MODEL = 256
        N_HEADS = 16
        HEAD_DIM = D_MODEL // N_HEADS
        WINDOW = 128
        STRIDE = 64

        def build_sparse_mask(T: int) -> jnp.ndarray:
            rows = jnp.arange(T)[:, None]
            cols = jnp.arange(T)[None, :]
            causal = cols <= rows
            local = jnp.abs(rows - cols) <= WINDOW
            strided = cols % STRIDE == 0
            return causal & (local | strided)
        key = jax.random.key(seed)
        k_x, k_qkv, k_out = jax.random.split(key, 3)
        B, T = (2, 512)
        x = jax.random.normal(k_x, (B, T, D_MODEL), dtype=jnp.float32)
        s_in = 1.0 / np.sqrt(D_MODEL)
        w_qkv = jax.random.uniform(k_qkv, (3 * D_MODEL, D_MODEL), dtype=jnp.float32, minval=-s_in, maxval=s_in)
        w_out = jax.random.uniform(k_out, (D_MODEL, D_MODEL), dtype=jnp.float32, minval=-s_in, maxval=s_in)
        return {'x': x, 'w_qkv': w_qkv, 'w_out': w_out}
    _L1_attn_in = _L1_attn_setup()

    def _L1_ffn_setup():
        import jax, jax.numpy as jnp
        import numpy as np
        E = 8
        K = 2
        D = 256
        H = 1024
        CAP_FACTOR = 1.0
        key = jax.random.key(seed)
        ks = jax.random.split(key, 5)
        x = jax.random.normal(ks[0], (4, 512, D), jnp.float32)
        gate_w = jax.random.normal(ks[1], (E, D), jnp.float32) * 0.02
        fc1_w = jax.random.normal(ks[2], (E, H, D), jnp.float32) * 0.02
        fc1_b = jnp.zeros((E, 1, H), jnp.float32)
        fc2_w = jax.random.normal(ks[3], (E, H, D), jnp.float32) * 0.02
        fc2_b = jnp.zeros((E, 1, D), jnp.float32)
        return {'x': x, 'gate_w': gate_w, 'fc1_w': fc1_w, 'fc1_b': fc1_b, 'fc2_w': fc2_w, 'fc2_b': fc2_b}
    _L1_ffn_in = _L1_ffn_setup()
    _d = {'L0_attn_hidden_states': _L0_attn_in['hidden_states'], 'L0_attn_in_proj_w': _L0_attn_in['in_proj_w'], 'L0_attn_conv_w': _L0_attn_in['conv_w'], 'L0_attn_conv_b': _L0_attn_in['conv_b'], 'L0_attn_x_proj_w': _L0_attn_in['x_proj_w'], 'L0_attn_dt_proj_w': _L0_attn_in['dt_proj_w'], 'L0_attn_dt_proj_b': _L0_attn_in['dt_proj_b'], 'L0_attn_dt_ln_w': _L0_attn_in['dt_ln_w'], 'L0_attn_b_ln_w': _L0_attn_in['b_ln_w'], 'L0_attn_c_ln_w': _L0_attn_in['c_ln_w'], 'L0_attn_A_log': _L0_attn_in['A_log'], 'L0_attn_D': _L0_attn_in['D'], 'L0_attn_out_proj_w': _L0_attn_in['out_proj_w'], 'L0_ffn_W_exp': _L0_ffn_in['W_exp'], 'L0_ffn_b_exp': _L0_ffn_in['b_exp'], 'L0_ffn_up_weights': _L0_ffn_in['up_weights'], 'L0_ffn_up_bias': _L0_ffn_in['up_bias'], 'L0_ffn_down_weights': _L0_ffn_in['down_weights'], 'L0_ffn_W_con': _L0_ffn_in['W_con'], 'L0_ffn_b_con': _L0_ffn_in['b_con'], 'L0_ffn_down_bias': _L0_ffn_in['down_bias'], 'L1_attn_w_qkv': _L1_attn_in['w_qkv'], 'L1_attn_w_out': _L1_attn_in['w_out'], 'L1_ffn_gate_w': _L1_ffn_in['gate_w'], 'L1_ffn_fc1_w': _L1_ffn_in['fc1_w'], 'L1_ffn_fc1_b': _L1_ffn_in['fc1_b'], 'L1_ffn_fc2_w': _L1_ffn_in['fc2_w'], 'L1_ffn_fc2_b': _L1_ffn_in['fc2_b']}
    _x0 = _d['L0_attn_hidden_states']
    _d['L0_attn_hidden_states'] = jax.random.normal(jax.random.fold_in(jax.random.key(seed), 1), (2, 2048, 256), dtype=_x0.dtype)
    del _x0
    return _d

def reference(L0_attn_hidden_states, L0_attn_in_proj_w, L0_attn_conv_w, L0_attn_conv_b, L0_attn_x_proj_w, L0_attn_dt_proj_w, L0_attn_dt_proj_b, L0_attn_dt_ln_w, L0_attn_b_ln_w, L0_attn_c_ln_w, L0_attn_A_log, L0_attn_D, L0_attn_out_proj_w, L0_ffn_W_exp, L0_ffn_b_exp, L0_ffn_up_weights, L0_ffn_up_bias, L0_ffn_down_weights, L0_ffn_W_con, L0_ffn_b_con, L0_ffn_down_bias, L1_attn_w_qkv, L1_attn_w_out, L1_ffn_gate_w, L1_ffn_fc1_w, L1_ffn_fc1_b, L1_ffn_fc2_w, L1_ffn_fc2_b):

    def _L0_attn_ref(hidden_states, in_proj_w, conv_w, conv_b, x_proj_w, dt_proj_w, dt_proj_b, dt_ln_w, b_ln_w, c_ln_w, A_log, D, out_proj_w):
        import jax, jax.numpy as jnp
        import numpy as np
        from jax import lax
        H = 256
        EXPAND = 2
        I = EXPAND * H
        N = 16
        K = 4
        R = 64
        EPS = 1e-06
        B_SZ, L = (2, 256)

        def rmsnorm(x, w):
            v = jnp.mean(x.astype(jnp.float32) ** 2, axis=-1, keepdims=True)
            return w * (x * jax.lax.rsqrt(v + EPS)).astype(x.dtype)
        b, l, _ = hidden_states.shape
        proj = hidden_states @ in_proj_w.T
        hs, gate = (proj[..., :I], proj[..., I:])
        x = jnp.transpose(hs, (0, 2, 1))
        x = lax.conv_general_dilated(x, conv_w, (1,), [(1, 2)], feature_group_count=I, dimension_numbers=('NCH', 'OIH', 'NCH'))
        x = x + conv_b[None, :, None]
        u = jax.nn.silu(jnp.transpose(x, (0, 2, 1)))
        x_dbl = u @ x_proj_w.T
        dt = rmsnorm(x_dbl[..., :R], dt_ln_w)
        Bm = rmsnorm(x_dbl[..., R:R + N], b_ln_w)
        Cm = rmsnorm(x_dbl[..., R + N:], c_ln_w)
        dt = jax.nn.softplus(dt @ dt_proj_w.T + dt_proj_b)
        A = -jnp.exp(A_log)
        dA = jnp.exp(dt[..., None] * A)
        dBu = (dt * u)[..., None] * Bm[:, :, None, :]

        def step(h, inp):
            dA_t, dBu_t = inp
            h = dA_t * h + dBu_t
            return (h, h)
        h0 = jnp.zeros((b, I, N), jnp.float32)
        _, h_seq = lax.scan(step, h0, (jnp.transpose(dA, (1, 0, 2, 3)), jnp.transpose(dBu, (1, 0, 2, 3))))
        y = jnp.einsum('lbin,bln->bli', h_seq, Cm)
        y = y + u * D
        y = y * jax.nn.silu(gate)
        return y @ out_proj_w.T

    def _L0_ffn_ref(x, W_exp, b_exp, up_weights, up_bias, down_weights, W_con, b_con, down_bias):
        import jax, jax.numpy as jnp
        import numpy as np
        D_MODEL = 256
        EXPANSION = 4
        D_HIDDEN = D_MODEL * EXPANSION
        NUM_STAGES = int(np.log2(D_HIDDEN))

        def butterfly(y, weights, dim):
            lead = y.shape[:-1]
            for stage in range(weights.shape[0]):
                s = 2 ** stage
                nb = dim // (2 * s)
                yr = y.reshape(*lead, nb, 2, s)
                a = yr[..., 0, :]
                b = yr[..., 1, :]
                w = weights[stage].reshape(nb, s, 2, 2)
                na = w[..., 0, 0] * a + w[..., 0, 1] * b
                nb2 = w[..., 1, 0] * a + w[..., 1, 1] * b
                y = jnp.stack([na, nb2], axis=-2).reshape(*lead, dim)
            return y
        h = jnp.einsum('bsd,dh->bsh', x, W_exp) + b_exp
        h = butterfly(h, up_weights, D_HIDDEN)
        h = jax.nn.gelu(h + up_bias, approximate=False)
        h = butterfly(h, down_weights, D_HIDDEN)
        y = jnp.einsum('bsh,hd->bsd', h, W_con) + b_con
        return y + down_bias

    def _L1_attn_ref(x, w_qkv, w_out):
        import jax, jax.numpy as jnp
        import numpy as np
        D_MODEL = 256
        N_HEADS = 16
        HEAD_DIM = D_MODEL // N_HEADS
        WINDOW = 128
        STRIDE = 64

        def build_sparse_mask(T: int) -> jnp.ndarray:
            rows = jnp.arange(T)[:, None]
            cols = jnp.arange(T)[None, :]
            causal = cols <= rows
            local = jnp.abs(rows - cols) <= WINDOW
            strided = cols % STRIDE == 0
            return causal & (local | strided)
        B, T, C = x.shape
        qkv = jnp.einsum('btc,dc->btd', x, w_qkv)
        q, k, v = jnp.split(qkv, 3, axis=-1)
        q = q.reshape(B, T, N_HEADS, HEAD_DIM).transpose(0, 2, 1, 3)
        k = k.reshape(B, T, N_HEADS, HEAD_DIM).transpose(0, 2, 1, 3)
        v = v.reshape(B, T, N_HEADS, HEAD_DIM).transpose(0, 2, 1, 3)
        mask = build_sparse_mask(T)
        scale = HEAD_DIM ** (-0.5)
        attn = jnp.einsum('bhqd,bhkd->bhqk', q, k) * scale
        attn = jnp.where(mask[None, None], attn, -jnp.inf)
        attn = jax.nn.softmax(attn, axis=-1)
        attn = jnp.nan_to_num(attn, nan=0.0)
        out = jnp.einsum('bhqk,bhkd->bhqd', attn, v)
        out = out.transpose(0, 2, 1, 3).reshape(B, T, C)
        return jnp.einsum('btc,dc->btd', out, w_out)

    def _L1_ffn_ref(x, gate_w, fc1_w, fc1_b, fc2_w, fc2_b):
        import jax, jax.numpy as jnp
        import numpy as np
        E = 8
        K = 2
        D = 256
        H = 1024
        CAP_FACTOR = 1.0
        B, S, Dm = x.shape
        xf = x.reshape(-1, Dm)
        N = xf.shape[0]
        cap = int(K * CAP_FACTOR * ((N + E - 1) // E))
        logits = xf @ gate_w.T
        scores = jax.nn.softmax(logits, axis=-1)
        topv, topi = jax.lax.top_k(scores, K)
        gates = topv / jnp.sum(topv, axis=-1, keepdims=True)
        offset = jnp.zeros((E,), jnp.int32)
        locs = []
        for j in range(K):
            mask = jax.nn.one_hot(topi[:, j], E, dtype=jnp.int32)
            loc_in = jnp.cumsum(mask, axis=0) - 1 + offset[None, :]
            locs.append(jnp.take_along_axis(loc_in, topi[:, j:j + 1], axis=1)[:, 0])
            offset = offset + mask.sum(axis=0)
        loc = jnp.stack(locs, axis=1)
        valid = loc < cap
        flat_idx = jnp.where(valid, topi * cap + loc, 0)
        w = valid.astype(xf.dtype)
        disp = jnp.zeros((E * cap, Dm), xf.dtype)
        disp = disp.at[flat_idx.reshape(-1)].add((xf[:, None, :] * w[:, :, None]).reshape(-1, Dm))
        de = disp.reshape(E, cap, Dm)
        h = jax.nn.relu(jnp.einsum('ecd,ehd->ech', de, fc1_w) + fc1_b)
        eo = jnp.einsum('ech,ehd->ecd', h, fc2_w) + fc2_b
        gathered = eo.reshape(E * cap, Dm)[flat_idx]
        out = jnp.sum(gathered * (gates * w)[:, :, None], axis=1)
        return out.reshape(B, S, Dm)
    x = L0_attn_hidden_states
    x = x + 0.5 * _L0_ffn_ref(_layernorm(x, axis=-1), L0_ffn_W_exp, L0_ffn_b_exp, L0_ffn_up_weights, L0_ffn_up_bias, L0_ffn_down_weights, L0_ffn_W_con, L0_ffn_b_con, L0_ffn_down_bias)
    x = x + _L0_attn_ref(_layernorm(x, axis=-1), L0_attn_in_proj_w, L0_attn_conv_w, L0_attn_conv_b, L0_attn_x_proj_w, L0_attn_dt_proj_w, L0_attn_dt_proj_b, L0_attn_dt_ln_w, L0_attn_b_ln_w, L0_attn_c_ln_w, L0_attn_A_log, L0_attn_D, L0_attn_out_proj_w)
    x = x + 0.5 * _L0_ffn_ref(_layernorm(x, axis=-1), L0_ffn_W_exp, L0_ffn_b_exp, L0_ffn_up_weights, L0_ffn_up_bias, L0_ffn_down_weights, L0_ffn_W_con, L0_ffn_b_con, L0_ffn_down_bias)
    x = x + 0.5 * _L1_ffn_ref(_layernorm(x, axis=-1), L1_ffn_gate_w, L1_ffn_fc1_w, L1_ffn_fc1_b, L1_ffn_fc2_w, L1_ffn_fc2_b)
    x = x + _L1_attn_ref(_layernorm(x, axis=-1), L1_attn_w_qkv, L1_attn_w_out)
    x = x + 0.5 * _L1_ffn_ref(_layernorm(x, axis=-1), L1_ffn_gate_w, L1_ffn_fc1_w, L1_ffn_fc1_b, L1_ffn_fc2_w, L1_ffn_fc2_b)
    return x

_drawn_inputs = setup_inputs


def setup_inputs(seed=0):
    import zlib

    import numpy as np

    out = dict(_drawn_inputs(seed))
    spreads = {'L0_attn_conv_b': (0.0, 0.8),
     'L0_attn_dt_ln_w': (1.0, 0.6),
     'L0_attn_b_ln_w': (1.0, 0.6),
     'L0_attn_c_ln_w': (1.0, 0.6),
     'L0_attn_D': (1.0, 0.6),
     'L0_ffn_b_exp': (0.0, 0.1),
     'L0_ffn_up_bias': (0.0, 0.1),
     'L0_ffn_b_con': (0.0, 0.1),
     'L0_ffn_down_bias': (0.0, 0.1),
     'L1_ffn_fc1_b': (0.0, 2.0),
     'L1_ffn_fc2_b': (0.0, 0.8)}
    factors = {'L0_attn_in_proj_w': 8.0,
     'L0_attn_conv_w': 8.0,
     'L0_attn_x_proj_w': 3.151,
     'L0_attn_dt_proj_w': 8.0,
     'L0_attn_dt_proj_b': 8.0,
     'L0_attn_A_log': 7.287,
     'L0_attn_out_proj_w': 8.0,
     'L1_attn_w_qkv': 8.0,
     'L1_attn_w_out': 8.0,
     'L1_ffn_gate_w': 8.0,
     'L1_ffn_fc1_w': 8.0,
     'L1_ffn_fc2_w': 8.0}
    for name, (base, spread) in spreads.items():
        noise = np.random.default_rng([zlib.crc32(name.encode()), seed]).standard_normal(out[name].shape)
        drawn = base * np.exp(spread * noise) if base else spread * noise
        out[name] = jnp.asarray(drawn.astype(out[name].dtype))
    for name, factor in factors.items():
        out[name] = (out[name] * factor).astype(out[name].dtype)
    return out
```

```python
from contextlib import ExitStack

import concourse.bass as bass
from concourse import mybir

F32 = mybir.dt.float32
BF16 = mybir.dt.bfloat16
I32 = mybir.dt.int32
ALU = mybir.AluOpType
ACT = mybir.ActivationFunctionType
AX = mybir.AxisListType

P = 128
BATCH, SEQ, D = 2, 2048, 256
TOK = BATCH * SEQ
KD = D // P
BLK = 512
NBLK = TOK // BLK
TPB = BLK // P
NT = TOK // P
LN_EPS = 1e-5
RMS_EPS = 1e-6
FH = 1024
FM = FH // P
STAGES = 10
INNER, STATE, TAPS, RANK = 512, 16, 4, 64
IB = INNER // P
XD = RANK + 2 * STATE
HPAD = SEQ + TAPS - 1
HEADS, HD = 16, 16
HPB = P // HD
SPARSE = 64
NSTR = SEQ // SPARSE
QT = SEQ // P
NEG = -1.0e30
NE, EH, CAP, TOPK = 8, 1024, 1024, 2
EM = EH // P
HALF = 512
HPE = CAP // HALF


class Room:

    def __init__(self, nc, ctx, tag):
        self.nc, self.ctx, self.tag = nc, ctx, tag

    def sb(self, name, shape, dt=F32):
        return self.ctx.enter_context(self.nc.sbuf_tensor(f"{self.tag}_{name}", shape, dt))

    def ps(self, name, shape, dt=F32):
        return self.ctx.enter_context(self.nc.psum_tensor(f"{self.tag}_{name}", shape, dt))

    def sem(self, name):
        sem = self.nc.alloc_semaphore(f"{self.tag}_{name}")
        Room.sems.append(sem)
        return sem

    sems = []


def recycle_semaphores(nc):
    nc.clear_and_free_semaphores(Room.sems)
    Room.sems = []
    nc.all_engine_barrier()


def tiles(dram, i, n=TPB):
    return dram[bass.ds(i * (n * P), n * P), :].rearrange("(j p) d -> p j d", p=P)



LN_OPS = 3 * TPB + 2


def ln_vector(nc, dve, i, x, xn, stat, mv, s, n=TPB):
    ops = 3 * n + 2
    dve.wait_ge(s["x_loaded"], 16 * (i + 1))
    for j in range(n):
        nc.vector.bn_stats(stat[:, j, :], x[:, j, :]).then_inc(s["ln"], 1)
    dve.wait_ge(s["ln"], i * ops + n)
    nc.vector.tensor_copy(mv[:, n, :], stat[:, n - 1, 0:2]).then_inc(s["ln"], 1)
    for j in range(n):
        nc.vector.bn_aggr(mv[:, j, :], stat[:, j, :]).then_inc(s["ln"], 1)
    dve.wait_ge(s["ln"], i * ops + 2 * n + 1)
    nc.vector.tensor_scalar(mv[:, 0:n, 1], mv[:, 0:n, 1], LN_EPS, None, ALU.add).then_inc(s["ln"], 1)
    dve.wait_ge(s["rstd_ready"], i + 1)
    dve.wait_ge(s["xT_ps_ready"], KD * i)
    for j in range(n):
        nc.vector.tensor_scalar(xn[:, j, :], x[:, j, :], mv[:, j, 0:1], s["rstd"][:, j:j + 1],
                                ALU.subtract, ALU.mult).then_inc(s["ln"], 1)


def ln_gpsimd(nc, pool, i, mv, s, n=TPB):
    pool.wait_ge(s["ln"], i * (3 * n + 2) + 2 * n + 2)
    nc.gpsimd.tensor_tensor(s["rstd"][:, 0:n], mv[:, 0:n, 1], s["minus_half"][:, 0:n], ALU.pow)\
        .then_inc(s["rstd_ready"], 1)


def ln_transpose(nc, pe, i, xn, xT_ps, ident, s, n=TPB):
    pe.wait_ge(s["ln"], (i + 1) * (3 * n + 2))
    pe.wait_ge(s["xT_ready"], KD * i)
    for k in range(KD):
        for j in range(n):
            t = nc.tensor.transpose(xT_ps[k][:, j * P:(j + 1) * P], xn[:, j, k * P:(k + 1) * P], ident[:])
        t.then_inc(s["xT_ps_ready"], 1)


def ln_room(r, n=TPB):
    x = r.sb("x", [P, n, D])
    xn = r.sb("xn", [P, n, D])
    stat = r.sb("stat", [P, n, 6])
    mv = r.sb("mv", [P, n + 1, 2])
    xT_ps = [r.ps(f"xT_ps{k}", [P, n * P]) for k in range(KD)]
    xT = r.sb("xT", [P, KD, n * P])
    s = {k: r.sem(k) for k in ("x_loaded", "ln", "rstd_ready", "xT_ps_ready", "xT_ready")}
    s["rstd"] = r.sb("rstd", [P, n])
    return x, xn, stat, mv, xT_ps, xT, s



def fold_block(nc, g, a):
    with ExitStack() as ctx:
        r = Room(nc, ctx, "fold")
        mats = [[r.sb(f"m{m}_{b}", [P, KD, FH]) for b in range(2)] for m in range(2)]
        w = [[r.sb(f"w{m}_{b}", [P, 2 * FH]) for b in range(2)] for m in range(2)]
        prod = [r.sb(f"prod{t}", [P, FH]) for t in range(4)]
        row = [r.sb(f"row{b}", [1, FH]) for b in range(2)]
        rprod = [r.sb(f"rprod{t}", [1, FH]) for t in range(2)]
        up_bias = r.sb("up_bias", [1, FH])
        con_bias = r.sb("con_bias", [P, 2, D])
        alog = r.sb("alog", [P, IB, STATE])
        ps = [r.ps(f"ps{i}", [P, BLK]) for i in range(4)]
        bias_ps = r.ps("bias_ps", [P, FM])
        base_in = r.sem("base_in")
        const_in = r.sem("const_in")
        w_in = [[r.sem(f"w_{n}_in{b}") for b in range(2)] for n in ("up", "down")]
        dv = r.sem("dv")
        rows = r.sem("rows")
        turned = r.sem("turned")
        biased = r.sem("biased")
        taken = r.sem("taken")
        block = ctx.enter_context(nc.Block())
        PER = 2 * KD * 3

        @block.sync
        def _(sp):
            sp.dma_start(mats[0][0][:], a["w_exp"].rearrange("(k p) h -> p k h", p=P)).then_inc(base_in, 16)
            sp.dma_start(mats[1][0][:], a["w_con_T"].rearrange("(k p) h -> p k h", p=P)).then_inc(base_in, 16)
            sp.dma_start(row[0][:], a["b_exp"]).then_inc(base_in, 16)
            for st in range(STAGES):
                for m, name in enumerate(("up_w", "down_w")):
                    if st >= 2:
                        sp.wait_ge(dv, (st - 1) * PER)
                        sp.wait_ge(rows, (st - 1) * 3)
                    sp.dma_start(w[m][st % 2][:], a[name][st, :].partition_broadcast(P)).then_inc(w_in[m][st % 2], 16)
            sp.dma_start(up_bias[:], a["up_bias"]).then_inc(const_in, 16)
            sp.dma_start(g["ident"][:], a["ident"]).then_inc(const_in, 16)
            sp.dma_start(con_bias[:, 0, :], a["b_con"].partition_broadcast(P)).then_inc(const_in, 16)
            sp.dma_start(con_bias[:, 1, :], a["down_bias"].partition_broadcast(P)).then_inc(const_in, 16)
            sp.dma_start(alog[:], a["A_log"].rearrange("(k p) n -> p k n", p=P)).then_inc(const_in, 16)

        def stage(src, dst, wt, s, q0, q1):
            si = src.rearrange("p (n t s) -> p t n s", t=2, s=s)
            do = dst.rearrange("p (n t s) -> p t n s", t=2, s=s)
            wi = wt.rearrange("p (i o n s) -> p i o n s", i=2, o=2, s=s)
            return si, do, wi, [q.rearrange("p (o n s) -> p o n s", o=2, s=s) for q in (q0, q1)]

        @block.vector
        def _(dve):
            dve.wait_ge(base_in, 48)
            for st in range(STAGES):
                for m in range(2):
                    s = 2 ** st if m == 0 else 2 ** (STAGES - 1 - st)
                    dve.wait_ge(w_in[m][st % 2], 16 * (st // 2 + 1))
                    for k in range(KD):
                        n0 = st * PER + (m * KD + k) * 3
                        si, do, wi, q = stage(mats[m][st % 2][:, k, :], mats[m][1 - st % 2][:, k, :],
                                              w[m][st % 2][:], s, prod[2 * k][:], prod[2 * k + 1][:])
                        if n0:
                            dve.wait_ge(dv, n0)
                        for i in range(2):
                            nc.vector.tensor_tensor(q[i], wi[:, i], si[:, i:i + 1].to_broadcast(list(q[i].shape)),
                                                    ALU.mult).then_inc(dv, 1)
                        dve.wait_ge(dv, n0 + 2)
                        nc.vector.tensor_tensor(do, q[0], q[1], ALU.add).then_inc(dv, 1)
            dve.wait_ge(dv, STAGES * PER)
            nc.vector.tensor_copy(g["w_up"][:], mats[0][0][:]).then_inc(dv, 1)
            dve.wait_ge(const_in, 80)
            nc.vector.tensor_tensor(con_bias[:, 0, :], con_bias[:, 0, :], con_bias[:, 1, :], ALU.add).then_inc(dv, 1)
            dve.wait_ge(dv, STAGES * PER + 2)
            nc.vector.tensor_scalar(g["half_bias"][:], con_bias[:, 0, :], 0.5, None, ALU.mult).then_inc(dv, 1)
            dve.wait_ge(biased, 1)
            nc.vector.tensor_copy(g["b_up"][:], bias_ps[:]).then_inc(dv, 1)

        @block.gpsimd
        def _(pool):
            nc.gpsimd.memset(g["minus_half"][:], -0.5)
            nc.gpsimd.memset(g["zeros"][:], 0.0)
            pool.wait_ge(base_in, 48)
            for st in range(STAGES):
                pool.wait_ge(w_in[0][st % 2], 16 * (st // 2 + 1))
                if st:
                    pool.wait_ge(rows, st * 3)
                si, do, wi, q = stage(row[st % 2][:], row[1 - st % 2][:], w[0][st % 2][0:1, :], 2 ** st,
                                      rprod[0][:], rprod[1][:])
                for i in range(2):
                    nc.gpsimd.tensor_tensor(q[i], wi[:, i], si[:, i:i + 1].to_broadcast(list(q[i].shape)),
                                            ALU.mult).then_inc(rows, 1)
                pool.wait_ge(rows, st * 3 + 2)
                nc.gpsimd.tensor_tensor(do, q[0], q[1], ALU.add).then_inc(rows, 1)
            pool.wait_ge(rows, STAGES * 3)
            pool.wait_ge(const_in, 80)
            nc.gpsimd.tensor_tensor(row[1][:], row[0][:], up_bias[:], ALU.add).then_inc(rows, 1)

        @block.tensor
        def _(pe):
            pe.wait_ge(const_in, 80)
            pe.wait_ge(rows, STAGES * 3 + 1)
            for m in range(FM):
                t = nc.tensor.matmul(bias_ps[:, m:m + 1], row[1][0:1, m * P:(m + 1) * P], g["ident"][0:1, 0:1],
                                     start=True, stop=True)
            t.then_inc(biased, 1)
            pe.wait_ge(dv, STAGES * PER)
            for m in range(FM):
                if m >= 4 and m % 2 == 0:
                    pe.wait_ge(taken, m // 2 - 1)
                for k in range(KD):
                    t = nc.tensor.transpose(ps[m // 2 % 2][:, m % 2 * D + k * P:m % 2 * D + (k + 1) * P],
                                            mats[1][0][:, k, m * P:(m + 1) * P], g["ident"][:])
                if m % 2:
                    t.then_inc(turned, 1)

        @block.scalar
        def _(act):
            for m2 in range(FM // 2):
                act.wait_ge(turned, m2 + 1)
                nc.scalar.copy(g["w_down"][:, 2 * m2:2 * m2 + 2, :].rearrange("p m d -> p (m d)"), ps[m2 % 2][:])\
                    .then_inc(taken, 1)
            act.wait_ge(const_in, 80)
            nc.scalar.activation(alog[:], alog[:], ACT.Exp).then_inc(taken, 1)
            act.wait_ge(taken, FM // 2 + 1)
            nc.scalar.mul(g["neg_A"][:], alog[:], -1.0).then_inc(taken, 1)



def ffn_block(nc, tag, g, x_in, x_out):
    with ExitStack() as ctx:
        r = Room(nc, ctx, tag)
        x, xn, stat, mv, xT_ps, xT, s = ln_room(r)
        s["minus_half"] = g["minus_half"]
        xb = r.sb("xb", [P, TPB, D])
        hid = r.sb("hid", [P, FM, BLK])
        y = r.sb("y", [P, TPB, D])
        h_ps = [r.ps(f"h_ps{i}", [P, BLK]) for i in range(3)]
        y_ps = [r.ps(f"y_ps{i}", [P, BLK])[:, 0:D] for i in range(3)]
        xb_ready, h_ps_ready, hid_ready, y_ps_ready, y_ready, stored = (
            r.sem(n) for n in ("xb_ready", "h_ps_ready", "hid_ready", "y_ps_ready", "y_ready", "stored"))
        block = ctx.enter_context(nc.Block())
        LAST = NBLK - 1

        @block.sync
        def _(sp):
            def load(i):
                sp.dma_start(x[:], tiles(x_in, i)).then_inc(s["x_loaded"], 16)

            def store(i):
                sp.wait_ge(y_ready, TPB * (i + 1))
                sp.dma_start(tiles(x_out, i), y[:]).then_inc(stored, 16)

            load(0)
            with sp.Fori(0, LAST) as i:
                sp.wait_ge(s["ln"], LN_OPS * (i + 1))
                sp.wait_ge(xb_ready, i + 1)
                load(i + 1)
                store(i)
            store(LAST)
            sp.wait_ge(stored, 16 * NBLK)

        @block.gpsimd
        def _(pool):
            def biased(i):
                pool.wait_ge(s["x_loaded"], 16 * (i + 1))
                pool.wait_ge(y_ready, TPB * i)
                nc.gpsimd.tensor_tensor(xb[:], x[:], g["half_bias"][:].unsqueeze(1).to_broadcast([P, TPB, D]),
                                        ALU.add).then_inc(xb_ready, 1)

            with pool.Fori(0, NBLK) as i:
                ln_gpsimd(nc, pool, i, mv, s)
                biased(i)

        @block.vector
        def _(dve):
            def take_y(i):
                dve.wait_ge(xb_ready, i + 1)
                dve.wait_ge(stored, 16 * i)
                for j in range(TPB):
                    dve.wait_ge(y_ps_ready, TPB * i + j + 1)
                    nc.vector.scalar_tensor_tensor(out=y[:, j, :], in0=y_ps[j % 3], scalar=0.5,
                                                   in1=xb[:, j, :], op0=ALU.mult, op1=ALU.add)\
                        .then_inc(y_ready, 1)

            ln_vector(nc, dve, 0, x, xn, stat, mv, s)
            with dve.Fori(0, LAST) as i:
                ln_vector(nc, dve, i + 1, x, xn, stat, mv, s)
                take_y(i)
            take_y(LAST)

        @block.scalar
        def _(act):
            def take_xT(i):
                for k in range(KD):
                    act.wait_ge(s["xT_ps_ready"], KD * i + k + 1)
                    act.wait_ge(h_ps_ready, FM * i)
                    nc.scalar.copy(xT[:, k, :], xT_ps[k][:]).then_inc(s["xT_ready"], 1)

            def gelu(i):
                act.wait_ge(y_ps_ready, TPB * i)
                for m in range(FM):
                    act.wait_ge(h_ps_ready, FM * i + m + 1)
                    nc.scalar.activation(hid[:, m, :], h_ps[m % 3][:], ACT.Gelu, bias=g["b_up"][:, m:m + 1],
                                         scale=1.0).then_inc(hid_ready, 1)

            take_xT(0)
            with act.Fori(0, LAST) as i:
                gelu(i)
                take_xT(i + 1)
            gelu(LAST)

        @block.tensor
        def _(pe):
            def up(i):
                pe.wait_ge(s["xT_ready"], KD * (i + 1))
                for m in range(FM):
                    if m >= 3:
                        pe.wait_ge(hid_ready, FM * i + m - 2)
                    else:
                        pe.wait_ge(hid_ready, FM * i)
                    for k in range(KD):
                        t = nc.tensor.matmul(h_ps[m % 3][:], g["w_up"][:, k, m * P:(m + 1) * P], xT[:, k, :],
                                             start=(k == 0), stop=(k == KD - 1))
                    t.then_inc(h_ps_ready, 1)

            def down(i):
                pe.wait_ge(hid_ready, FM * (i + 1))
                for j in range(TPB):
                    if j >= 3:
                        pe.wait_ge(y_ready, TPB * i + j - 2)
                    else:
                        pe.wait_ge(y_ready, TPB * i)
                    for m in range(FM):
                        t = nc.tensor.matmul(y_ps[j % 3], hid[:, m, j * P:(j + 1) * P], g["w_down"][:, m, :],
                                             start=(m == 0), stop=(m == FM - 1))
                    t.then_inc(y_ps_ready, 1)

            ln_transpose(nc, pe, 0, xn, xT_ps, g["ident"], s)
            with pe.Fori(0, LAST) as i:
                up(i)
                ln_transpose(nc, pe, i + 1, xn, xT_ps, g["ident"], s)
                down(i)
            up(LAST)
            down(LAST)



def inproj_block(nc, g, a, x_in, proj_T):
    with ExitStack() as ctx:
        r = Room(nc, ctx, "inp")
        x, xn, stat, mv, xT_ps, xT, s = ln_room(r)
        s["minus_half"] = g["minus_half"]
        NM = 2 * INNER // P
        w = r.sb("w", [P, KD, 2 * INNER])
        o = [r.sb(f"o{i}", [P, IB, BLK]) for i in range(2)]
        p_ps = [r.ps(f"p_ps{i}", [P, BLK]) for i in range(4)]
        w_in, p_ps_ready, o_ready, padded = (r.sem(n) for n in ("w_in", "p_ps_ready", "o_ready", "padded"))
        stored = [r.sem(f"stored{h}") for h in range(2)]
        block = ctx.enter_context(nc.Block())
        LAST = NBLK - 1
        BPB = NBLK // BATCH
        PARTS = [(0, BPB, 0), (BPB, LAST, 1)]

        @block.sync
        def _(sp):
            out3 = proj_T.rearrange("(k p) t -> p k t", p=P)

            def load(i):
                sp.dma_start(x[:], tiles(x_in, i)).then_inc(s["x_loaded"], 16)

            def store(i, b):
                for h in range(2):
                    sp.wait_ge(o_ready, NM * i + (h + 1) * IB)
                    sp.dma_start(out3[:, h * IB:(h + 1) * IB, bass.ds(i * BLK + (b * (TAPS - 1) + 1), BLK)], o[h][:])\
                        .then_inc(stored[h], 16)

            load(0)
            sp.dma_start(w[:], a["in_proj_T"].rearrange("(k p) n -> p k n", p=P)).then_inc(w_in, 16)
            for b in range(BATCH):
                z = g["zeros"][:, 0:IB * 2].rearrange("p (k t) -> p k t", k=IB)
                sp.dma_start(out3[:, 0:IB, b * HPAD:b * HPAD + 1], z[:, :, 0:1],
                             allow_slow_non_contiguous=True).then_inc(padded, 16)
                sp.dma_start(out3[:, 0:IB, b * HPAD + SEQ + 1:(b + 1) * HPAD], z).then_inc(padded, 16)
            for lo, hi, b in PARTS:
                with sp.Fori(lo, hi) as i:
                    sp.wait_ge(s["ln"], LN_OPS * (i + 1))
                    load(i + 1)
                    store(i, b)
            store(LAST, 1)
            sp.wait_ge(padded, 16 * 2 * BATCH)
            sp.wait_ge(stored[0], 16 * NBLK)
            sp.wait_ge(stored[1], 16 * NBLK)

        @block.gpsimd
        def _(pool):
            with pool.Fori(0, NBLK) as i:
                ln_gpsimd(nc, pool, i, mv, s)

        @block.vector
        def _(dve):
            with dve.Fori(0, NBLK) as i:
                ln_vector(nc, dve, i, x, xn, stat, mv, s)

        @block.scalar
        def _(act):
            def take_xT(i):
                for k in range(KD):
                    act.wait_ge(s["xT_ps_ready"], KD * i + k + 1)
                    act.wait_ge(p_ps_ready, NM * i)
                    nc.scalar.copy(xT[:, k, :], xT_ps[k][:]).then_inc(s["xT_ready"], 1)

            def take(i):
                for m in range(NM):
                    if m % IB == 0:
                        act.wait_ge(stored[m // IB], 16 * i)
                    act.wait_ge(p_ps_ready, NM * i + m + 1)
                    if m < IB:
                        t = nc.scalar.copy(o[0][:, m, :], p_ps[m % 4][:])
                    else:
                        t = nc.scalar.activation(o[1][:, m - IB, :], p_ps[m % 4][:], ACT.Silu)
                    t.then_inc(o_ready, 1)

            take_xT(0)
            with act.Fori(0, LAST) as i:
                take(i)
                take_xT(i + 1)
            take(LAST)

        @block.tensor
        def _(pe):
            def project(i):
                pe.wait_ge(s["xT_ready"], KD * (i + 1))
                for m in range(NM):
                    pe.wait_ge(o_ready, NM * i + max(m - 3, 0))
                    for k in range(KD):
                        t = nc.tensor.matmul(p_ps[m % 4][:], w[:, k, m * P:(m + 1) * P], xT[:, k, :],
                                             start=(k == 0), stop=(k == KD - 1))
                    t.then_inc(p_ps_ready, 1)

            pe.wait_ge(w_in, 16)
            ln_transpose(nc, pe, 0, xn, xT_ps, g["ident"], s)
            with pe.Fori(0, LAST) as i:
                project(i)
                ln_transpose(nc, pe, i + 1, xn, xT_ps, g["ident"], s)
            project(LAST)




def mamba_block(nc, g, a, x_in, proj_T, bc_T, x_out):
    with ExitStack() as ctx:
        r = Room(nc, ctx, "mam")
        QS = 4
        NQ = STATE // QS
        NG = NQ * IB
        conv_w = r.sb("conv_w", [P, IB, TAPS])
        conv_b = r.sb("conv_b", [P, IB])
        diag = r.sb("diag", [P, IB, TAPS, P])
        w_x = r.sb("w_x", [P, IB, XD])
        w_dt = r.sb("w_dt", [RANK, INNER])
        b_dt = r.sb("b_dt", [P, IB])
        ln_w = r.sb("ln_w", [XD, 1])
        skip = r.sb("skip", [P, IB])
        keep = r.sb("keep", [P, NBLK + 1])
        w_out = r.sb("w_out", [P, IB, D])
        hs = r.sb("hs", [P, IB, BLK + TAPS - 1])
        u = [r.sb(f"u{b}", [P, IB, BLK]) for b in range(2)]
        dt = [r.sb(f"dt{b}", [P, IB, BLK]) for b in range(2)]
        dtu = [r.sb(f"dtu{b}", [P, IB, BLK]) for b in range(2)]
        soft = r.sb("soft", [P, IB, BLK])
        gate = r.sb("gate", [P, IB, BLK])
        xd = r.sb("xd", [P, TPB, XD])
        xsq = r.sb("xsq", [P, TPB, XD])
        ms = r.sb("ms", [P, 3, TPB])
        rms = r.sb("rms", [P, 3, TPB])
        xdT = r.sb("xdT", [XD, BLK])
        Bq = [r.sb(f"Bq{b}", [P, QS, BLK]) for b in range(2)]
        Cq = [r.sb(f"Cq{b}", [P, QS, BLK]) for b in range(2)]
        dA = [r.sb(f"dA{b}", [P, QS, BLK]) for b in range(2)]
        dBu = [r.sb(f"dBu{b}", [P, QS, BLK]) for b in range(2)]
        h = [r.sb(f"h{b}", [P, QS, BLK]) for b in range(2)]
        h_last = r.sb("h_last", [P, NG, QS])
        xr = r.sb("xr", [P, TPB, D])
        o = r.sb("o", [P, TPB, D])
        y_ps = [r.ps(f"y_ps{k}", [P, BLK]) for k in range(IB)]
        rot_ps = [r.ps(f"rot_ps{k}", [P, BLK]) for k in range(2)]
        xd_ps = r.ps("xd_ps", [P, TPB, P])
        xT_ps = r.ps("xT_ps", [P, BLK])
        names = ("w_in hs_in gate_in x_loaded conv_ps_ready u_ready xd_ps_ready norm rms_ready xT_ps_ready "
                 "xdT_ready bc_stored dt_ps_ready softened dtu_ready dA_ready dBu_ready scanned kept hC_ready "
                 "y_summed y_ready o_ps_ready o_ready stored diags").split()
        s = {n: r.sem(n) for n in names}
        B_in = [r.sem(f"B_in{b}") for b in range(2)]
        C_in = [r.sem(f"C_in{b}") for b in range(2)]
        block = ctx.enter_context(nc.Block())
        LAST = NBLK - 1
        NORM = 9
        SOFT = 2 * IB + 2
        FIN = 2
        W_IN = 16 * 9
        proj3 = proj_T.rearrange("(k p) t -> p k t", p=P)

        def wait(eng, name, value):
            if not (isinstance(value, int) and value <= 0):
                eng.wait_ge(s[name], value)

        def all_steps(eng, step, end):
            step(0, 0, True, False)
            with eng.Fori(0, (NBLK - 2) // 2) as i:
                step(i * 2 + 1, 1, False, False)
                step(i * 2 + 2, 0, False, False)
            step(LAST, LAST % 2, False, True)
            if end:
                end()

        @block.sync
        def _(sp):
            BPB = NBLK // BATCH

            def load_hs(n, b):
                wait(sp, "conv_ps_ready", IB * n)
                sp.dma_start(hs[:], proj3[:, 0:IB, bass.ds(n * BLK + b * (TAPS - 1), BLK + TAPS - 1)])\
                    .then_inc(s["hs_in"], 16)

            def load_quad(c, quad):
                G = c * NG + (quad - 2) * IB
                b = quad % 2
                rows = bc_T[quad * QS:quad * QS + QS, bass.ds(c * BLK + BLK, BLK)]
                wait(sp, "dBu_ready", G + IB)
                sp.dma_start(Bq[b][:], rows.partition_broadcast(P)).then_inc(B_in[b], 16)
                rows = bc_T[STATE + quad * QS:STATE + quad * QS + QS, bass.ds(c * BLK + BLK, BLK)]
                wait(sp, "hC_ready", G + IB)
                sp.dma_start(Cq[b][:], rows.partition_broadcast(P)).then_inc(C_in[b], 16)

            def store_bc(n):
                sp.wait_ge(s["xdT_ready"], n + 1)
                sp.dma_start(bc_T[:, bass.ds(n * BLK + BLK, BLK)], xdT[RANK:XD, :]).then_inc(s["bc_stored"], 16)

            def store_out(c):
                sp.wait_ge(s["o_ready"], TPB * (c + 1))
                sp.dma_start(tiles(x_out, c), o[:]).then_inc(s["stored"], 16)

            def step(c, q, first, last, b, bn):
                if not last:
                    load_hs(c + 1, bn)
                wait(sp, "y_ready", FIN * IB * c)
                sp.dma_start(gate[:], proj3[:, IB:2 * IB, bass.ds(c * BLK + b * (TAPS - 1) + 1, BLK)])\
                    .then_inc(s["gate_in"], 16)
                load_quad(c, 2)
                if not first:
                    store_out(c - 1)
                wait(sp, "o_ready", TPB * c)
                sp.dma_start(xr[:], tiles(x_in, c)).then_inc(s["x_loaded"], 16)
                load_quad(c, 3)
                if not last:
                    store_bc(c + 1)
                    sp.wait_ge(s["bc_stored"], 16 * (c + 2))
                    load_quad(c + 1, 0)
                    load_quad(c + 1, 1)

            for dst, name in ((conv_w, "conv_w"), (w_x, "x_proj_T"), (w_out, "out_proj_T")):
                sp.dma_start(dst[:], a[name].rearrange("(k p) n -> p k n", p=P)).then_inc(s["w_in"], 16)
            for dst, name in ((conv_b, "conv_b"), (b_dt, "dt_bias"), (skip, "D")):
                sp.dma_start(dst[:], a[name]).then_inc(s["w_in"], 16)
            sp.dma_start(w_dt[:], a["dt_proj_T"]).then_inc(s["w_in"], 16)
            sp.dma_start(ln_w[:], a["xd_ln_w"]).then_inc(s["w_in"], 16)
            sp.dma_start(keep[:], a["keep"]).then_inc(s["w_in"], 16)
            load_hs(0, 0)
            store_bc(0)
            sp.wait_ge(s["bc_stored"], 16)
            load_quad(0, 0)
            load_quad(0, 1)
            step(0, 0, True, False, 0, 0)
            with sp.Fori(1, BPB - 1) as c:
                step(c, 0, False, False, 0, 0)
            step(BPB - 1, 0, False, False, 0, 1)
            with sp.Fori(BPB, LAST) as c:
                step(c, 0, False, False, 1, 1)
            step(LAST, 0, False, True, 1, 1)
            store_out(LAST)
            sp.wait_ge(s["stored"], 16 * NBLK)

        @block.gpsimd
        def _(pool):
            def norms(n):
                pool.wait_ge(s["norm"], NORM * n + 7)
                nc.gpsimd.tensor_tensor(rms[:].rearrange("p g j -> p (g j)"), ms[:].rearrange("p g j -> p (g j)"),
                                        g["minus_half"][:, 0:3 * TPB], ALU.pow).then_inc(s["rms_ready"], 1)

            def make_dt(n, p):
                pool.wait_ge(s["softened"], SOFT * (n + 1))
                nc.gpsimd.tensor_tensor(dt[p][:], dt[p][:], soft[:], ALU.add).then_inc(s["dtu_ready"], 1)
                wait(pool, "dBu_ready", NG * (n - 1))
                pool.wait_ge(s["dtu_ready"], 2 * n + 1)
                nc.gpsimd.tensor_tensor(dtu[p][:], dt[p][:], u[p][:], ALU.mult).then_inc(s["dtu_ready"], 1)

            def step(c, q, first, last):
                for gi in range(NG):
                    k, quad, G = gi % IB, gi // IB, c * NG + gi
                    if gi % IB == 0:
                        pool.wait_ge(B_in[quad % 2], 16 * (2 * c + quad // 2 + 1))
                    if gi == 0:
                        pool.wait_ge(s["dtu_ready"], 2 * (c + 1))
                    wait(pool, "scanned", QS * (G - 1))
                    nc.gpsimd.tensor_tensor(dBu[gi % 2][:], Bq[quad % 2][:],
                                            dtu[q][:, k:k + 1, :].to_broadcast([P, QS, BLK]), ALU.mult)\
                        .then_inc(s["dBu_ready"], 1)
                    if gi == 7 and not last:
                        norms(c + 1)
                    if gi == 13 and not last:
                        make_dt(c + 1, 1 - q)

            norms(0)
            make_dt(0, 0)
            all_steps(pool, step, None)

        @block.scalar
        def _(act):
            def make_u(n, p):
                wait(act, "o_ps_ready", TPB * (n - 1))
                for k in range(IB):
                    act.wait_ge(s["conv_ps_ready"], IB * n + k + 1)
                    nc.scalar.activation(u[p][:, k, :], rot_ps[k % 2][:], ACT.Silu, bias=conv_b[:, k:k + 1],
                                         scale=1.0).then_inc(s["u_ready"], 1)

            def take_xdT(n):
                act.wait_ge(s["xT_ps_ready"], n + 1)
                wait(act, "dt_ps_ready", IB * n)
                wait(act, "bc_stored", 16 * n)
                nc.scalar.activation(xdT[:], xT_ps[0:XD, :], ACT.Copy, scale=ln_w[:, 0:1]).then_inc(s["xdT_ready"], 1)

            def softplus(n, p):
                wait(act, "dtu_ready", 2 * n)
                for k in range(IB):
                    act.wait_ge(s["dt_ps_ready"], IB * n + k + 1)
                    nc.scalar.activation(soft[:, k, :], rot_ps[k % 2][:], ACT.Abs, bias=b_dt[:, k:k + 1], scale=1.0)\
                        .then_inc(s["softened"], 1)
                    nc.scalar.activation(dt[p][:, k, :], rot_ps[k % 2][:], ACT.Relu, bias=b_dt[:, k:k + 1], scale=1.0)\
                        .then_inc(s["softened"], 1)
                act.wait_ge(s["softened"], SOFT * n + 2 * IB)
                nc.scalar.activation(soft[:], soft[:], ACT.Exp, scale=-1.0).then_inc(s["softened"], 1)
                act.wait_ge(s["softened"], SOFT * n + 2 * IB + 1)
                nc.scalar.activation(soft[:], soft[:], ACT.Ln, bias=1.0).then_inc(s["softened"], 1)

            def step(c, q, first, last):
                for gi in range(NG):
                    k, quad, G = gi % IB, gi // IB, c * NG + gi
                    if gi == 0:
                        act.wait_ge(s["dtu_ready"], 2 * (c + 1))
                    wait(act, "scanned", QS * (G - 1))
                    for m in range(QS):
                        n = quad * QS + m
                        nc.scalar.activation(dA[gi % 2][:, m, :], dt[q][:, k, :], ACT.Exp,
                                             scale=g["neg_A"][:, k, n:n + 1]).then_inc(s["dA_ready"], 1)
                    if gi == 3 and not last:
                        make_u(c + 1, 1 - q)
                    if gi == 9 and not last:
                        take_xdT(c + 1)
                    if gi == 11 and not last:
                        softplus(c + 1, 1 - q)

            act.wait_ge(s["w_in"], W_IN)
            make_u(0, 0)
            take_xdT(0)
            softplus(0, 0)
            all_steps(act, step, None)

        @block.vector
        def _(dve):
            def norms(n):
                dve.wait_ge(s["xd_ps_ready"], n + 1)
                wait(dve, "xT_ps_ready", n)
                nc.vector.tensor_copy(xd[:], xd_ps[:, :, 0:XD]).then_inc(s["norm"], 1)
                dve.wait_ge(s["norm"], NORM * n + 1)
                nc.vector.tensor_tensor(xsq[:], xd[:], xd[:], ALU.mult).then_inc(s["norm"], 1)
                dve.wait_ge(s["norm"], NORM * n + 2)
                for i, (lo, hi) in enumerate(((0, RANK), (RANK, RANK + STATE), (RANK + STATE, XD))):
                    nc.vector.tensor_reduce(ms[:, i, :], xsq[:, :, lo:hi], AX.X, ALU.add).then_inc(s["norm"], 1)
                dve.wait_ge(s["norm"], NORM * n + 5)
                nc.vector.tensor_scalar(ms[:, 0, :], ms[:, 0, :], 1.0 / RANK, RMS_EPS, ALU.mult, ALU.add)\
                    .then_inc(s["norm"], 1)
                nc.vector.tensor_scalar(ms[:, 1:3, :], ms[:, 1:3, :], 1.0 / STATE, RMS_EPS, ALU.mult, ALU.add)\
                    .then_inc(s["norm"], 1)

            def scale(n):
                dve.wait_ge(s["rms_ready"], n + 1)
                nc.vector.tensor_tensor(xd[:, :, 0:RANK], xd[:, :, 0:RANK],
                                        rms[:, 0, :].unsqueeze(2).to_broadcast([P, TPB, RANK]), ALU.mult)\
                    .then_inc(s["norm"], 1)
                bc = xd[:, :, RANK:XD].rearrange("p j (g n) -> p j g n", g=2)
                nc.vector.tensor_tensor(bc, bc, rms[:, 1:3, :].rearrange("p g j -> p j g").unsqueeze(3)
                                        .to_broadcast([P, TPB, 2, STATE]), ALU.mult).then_inc(s["norm"], 1)

            def finish(c, q, k):
                dve.wait_ge(s["y_summed"], NG * c + NG - IB + k + 1)
                nc.vector.scalar_tensor_tensor(out=u[q][:, k, :], in0=u[q][:, k, :], scalar=skip[:, k:k + 1],
                                               in1=y_ps[k][:], op0=ALU.mult, op1=ALU.add).then_inc(s["y_ready"], 1)
                dve.wait_ge(s["y_ready"], FIN * (IB * c + k) + 1)
                dve.wait_ge(s["gate_in"], 16 * (c + 1))
                nc.vector.tensor_tensor(u[q][:, k, :], u[q][:, k, :], gate[:, k, :], ALU.mult)\
                    .then_inc(s["y_ready"], 1)

            def take_out(c):
                dve.wait_ge(s["x_loaded"], 16 * (c + 1))
                wait(dve, "stored", 16 * c)
                for j in range(TPB):
                    dve.wait_ge(s["o_ps_ready"], TPB * c + j + 1)
                    nc.vector.tensor_tensor(o[:, j, :], rot_ps[j % 2][:, 0:D], xr[:, j, :], ALU.add)\
                        .then_inc(s["o_ready"], 1)

            def step(c, q, first, last):
                for gi in range(NG):
                    k, quad, G = gi % IB, gi // IB, c * NG + gi
                    hb = h[gi % 2]
                    dve.wait_ge(s["dBu_ready"], G + 1)
                    wait(dve, "y_summed", G - 1)
                    wait(dve, "kept", G)
                    for m in range(QS):
                        dve.wait_ge(s["dA_ready"], QS * G + m + 1)
                        nc.vector.tensor_tensor_scan(hb[:, m, :], dA[gi % 2][:, m, :], dBu[gi % 2][:, m, :],
                                                     h_last[:, gi, m:m + 1], ALU.mult, ALU.add)\
                            .then_inc(s["scanned"], 1)
                    dve.wait_ge(s["scanned"], QS * (G + 1))
                    nc.vector.tensor_tensor(h_last[:, gi, :], hb[:, :, BLK - 1], keep[:, bass.ds(c + 1, 1)]
                                            .to_broadcast([P, QS]), ALU.mult).then_inc(s["kept"], 1)
                    dve.wait_ge(s["kept"], G + 1)
                    dve.wait_ge(C_in[quad % 2], 16 * (2 * c + quad // 2 + 1))
                    nc.vector.tensor_tensor(hb[:], hb[:], Cq[quad % 2][:], ALU.mult).then_inc(s["hC_ready"], 1)
                    if gi == 0 and not first:
                        finish(c - 1, 1 - q, IB - 1)
                    if gi == 3 and not first:
                        take_out(c - 1)
                    if gi == 6 and not last:
                        norms(c + 1)
                    if gi == 8 and not last:
                        scale(c + 1)
                    if gi >= NG - 3:
                        finish(c, q, gi - (NG - 3))

            def end():
                finish(LAST, LAST % 2, IB - 1)
                take_out(LAST)

            dve.wait_ge(s["w_in"], W_IN)
            nc.vector.memset(h_last[:], 0.0).then_inc(s["diags"], 1)
            for k in range(IB):
                for tap in range(TAPS):
                    nc.vector.tensor_scalar(diag[:, k, tap, :], g["ident"][:], conv_w[:, k, tap:tap + 1], None,
                                            ALU.mult).then_inc(s["diags"], 1)
            dve.wait_ge(s["diags"], 1 + IB * TAPS)
            norms(0)
            scale(0)
            all_steps(dve, step, end)

        @block.tensor
        def _(pe):
            def convolve(n):
                pe.wait_ge(s["hs_in"], 16 * (n + 1))
                for k in range(IB):
                    if k >= 2:
                        pe.wait_ge(s["u_ready"], IB * n + k - 1)
                    else:
                        wait(pe, "o_ready", TPB * (n - 1))
                    if k < 2:
                        wait(pe, "softened", SOFT * n)
                    for tap in range(TAPS):
                        t = nc.tensor.matmul(rot_ps[k % 2][:], diag[:, k, tap, :], hs[:, k, tap:tap + BLK],
                                             start=(tap == 0), stop=(tap == TAPS - 1))
                    t.then_inc(s["conv_ps_ready"], 1)

            def project_x(n, p):
                pe.wait_ge(s["u_ready"], IB * (n + 1))
                wait(pe, "norm", NORM * (n - 1) + 1)
                for j in range(TPB):
                    for k in range(IB):
                        t = nc.tensor.matmul(xd_ps[:, j, 0:XD], u[p][:, k, j * P:(j + 1) * P], w_x[:, k, :],
                                             start=(k == 0), stop=(k == IB - 1))
                t.then_inc(s["xd_ps_ready"], 1)

            def turn(n):
                pe.wait_ge(s["norm"], NORM * (n + 1))
                wait(pe, "xdT_ready", n)
                for j in range(TPB):
                    t = nc.tensor.transpose(xT_ps[0:XD, j * P:(j + 1) * P], xd[:, j, :], g["ident"][:])
                t.then_inc(s["xT_ps_ready"], 1)

            def project_dt(n):
                pe.wait_ge(s["xdT_ready"], n + 1)
                for k in range(IB):
                    if k < 2:
                        pe.wait_ge(s["u_ready"], IB * n + k + 3)
                    else:
                        pe.wait_ge(s["softened"], SOFT * n + 2 * (k - 1))
                    nc.tensor.matmul(rot_ps[k % 2][:], w_dt[:, k * P:(k + 1) * P], xdT[0:RANK, :],
                                     start=True, stop=True).then_inc(s["dt_ps_ready"], 1)

            def project_out(c, q, last=False):
                pe.wait_ge(s["y_ready"], FIN * IB * (c + 1))
                for j in range(TPB):
                    if not last and j < 2:
                        pe.wait_ge(s["softened"], SOFT * (c + 2))
                    wait(pe, "o_ready", TPB * c + max(j - 1, 0))
                    for k in range(IB):
                        t = nc.tensor.matmul(rot_ps[j % 2][:, 0:D], u[q][:, k, j * P:(j + 1) * P], w_out[:, k, :],
                                             start=(k == 0), stop=(k == IB - 1))
                    t.then_inc(s["o_ps_ready"], 1)

            def step(c, q, first, last):
                for gi in range(NG):
                    k, quad, G = gi % IB, gi // IB, c * NG + gi
                    pe.wait_ge(s["hC_ready"], G + 1)
                    if quad == 0:
                        wait(pe, "y_ready", FIN * (IB * (c - 1) + k) + 1)
                    for m in range(QS):
                        t = nc.tensor.matmul(y_ps[k][:], g["ident"][:], h[gi % 2][:, m, :],
                                             start=(quad == 0 and m == 0), stop=(quad == NQ - 1 and m == QS - 1))
                    t.then_inc(s["y_summed"], 1)
                    if gi == 1 and not first:
                        project_out(c - 1, 1 - q)
                    if gi == 2 and not last:
                        convolve(c + 1)
                    if gi == 5 and not last:
                        project_x(c + 1, 1 - q)
                    if gi == 8 and not last:
                        turn(c + 1)
                    if gi == 10 and not last:
                        project_dt(c + 1)

            pe.wait_ge(s["diags"], 1 + IB * TAPS)
            convolve(0)
            project_x(0, 0)
            turn(0)
            project_dt(0)
            all_steps(pe, step, lambda: project_out(LAST, LAST % 2, True))



def route_block(nc, tag, g, a, x_in, slots_dram):
    with ExitStack() as ctx:
        r = Room(nc, ctx, tag)
        x, xn, stat, mv, xT_ps, xT, s = ln_room(r)
        s["minus_half"] = g["minus_half"]
        NL = NT * NE
        w = r.sb("w", [P, KD, NE])
        xn_all = r.sb("xn_all", [P, NT, D])
        logits = r.sb("logits", [P, NT, NE])
        e = r.sb("e", [P, NT, NE])
        t = r.sb("t", [P, NT, NE])
        hot = r.sb("hot", [P, TOPK, NT, NE])
        best = r.sb("best", [P, TOPK, NT])
        m = r.sb("m", [P, NT])
        rank = r.sb("rank", [P, NE])
        first_slot = r.sb("first_slot", [P, NE])
        outside = r.sb("outside", [P, TOPK * NT])
        earlier = r.sb("earlier", [P, P])
        ones = r.sb("ones", [P, P])
        total = r.sb("total", [P, TOPK * NT, NE])
        upto = r.sb("upto", [P, TOPK * NT, NE])
        place = r.sb("place", [P, TOPK * NT, NE])
        pick = r.sb("pick", [P, TOPK * NT, NE])
        loc = r.sb("loc", [P, TOPK * NT])
        slot = r.sb("slot", [P, TOPK * NT])
        fits = r.sb("fits", [P, TOPK * NT])
        put = r.sb("put", [P, TOPK * NT], I32)
        l_ps = r.ps("l_ps", [P, TPB, NE])
        before_ps = r.ps("before_ps", [P, BLK])
        total_ps = r.ps("total_ps", [P, BLK])
        w_in, kept, l_ps_ready, l_ready, cleared, rt, exped, counted, scattered = (
            r.sem(n) for n in "w_in kept l_ps_ready l_ready cleared rt exped counted scattered".split())
        block = ctx.enter_context(nc.Block())
        W_IN = 16 * 6
        ROUTED = 33

        @block.sync
        def _(sp):
            def load(i):
                sp.dma_start(x[:], tiles(x_in, i)).then_inc(s["x_loaded"], 16)

            def keep(i):
                sp.wait_ge(s["ln"], LN_OPS * (i + 1))
                sp.dma_start(xn_all[:, bass.ds(i * TPB, TPB), :], xn[:]).then_inc(kept, 16)

            load(0)
            for dst, name in ((rank, "rank"), (first_slot, "first_slot"), (outside, "outside"),
                              (earlier, "earlier"), (ones, "ones")):
                sp.dma_start(dst[:], a[name]).then_inc(w_in, 16)
            sp.dma_start(w[:], a["gate_T"].rearrange("(k p) e -> p k e", p=P)).then_inc(w_in, 16)
            rows = slots_dram.rearrange("(c p q) d -> c p (q d)", p=P, q=4)
            for c in range(rows.shape[0]):
                sp.dma_start(rows[c], g["zeros"][:]).then_inc(cleared, 16)
            with sp.Fori(0, NBLK - 1) as i:
                keep(i)
                load(i + 1)
            keep(NBLK - 1)

        @block.gpsimd
        def _(pool):
            with pool.Fori(0, NBLK) as i:
                ln_gpsimd(nc, pool, i, mv, s)
            pool.wait_ge(kept, 16 * NBLK)
            pool.wait_ge(cleared, 16 * (NE * CAP // (4 * P)))
            pool.wait_ge(rt, ROUTED)
            for j in range(TOPK):
                for i in range(NT):
                    c = j * NT + i
                    nc.gpsimd.indirect_dma_start(
                        out=slots_dram, out_offset=bass.IndirectOffsetOnAxis(ap=put[:, c:c + 1], axis=0),
                        in_=xn_all[:, i, :], in_offset=None, bounds_check=NE * CAP - 1, oob_is_err=False)\
                        .then_inc(scattered, 16)
            pool.wait_ge(scattered, 16 * TOPK * NT)

        @block.vector
        def _(dve):
            with dve.Fori(0, NBLK) as i:
                if True:
                    dve.wait_ge(kept, 16 * i)
                    ln_vector(nc, dve, i, x, xn, stat, mv, s)
                    dve.wait_ge(l_ps_ready, i + 1)
                    nc.vector.tensor_copy(logits[:, bass.ds(i * TPB, TPB), :], l_ps[:]).then_inc(l_ready, 1)

            n = [0]

            def done(ins):
                ins.then_inc(rt, 1)
                n[0] += 1
                dve.wait_ge(rt, n[0])

            def over(v, k):
                return v.unsqueeze(2).to_broadcast([P, k, NE])

            dve.wait_ge(l_ready, NBLK)
            dve.wait_ge(w_in, W_IN)
            done(nc.vector.tensor_reduce(m[:], logits[:], AX.X, ALU.max))
            done(nc.vector.tensor_tensor(e[:], logits[:], over(m[:], NT), ALU.subtract))
            dve.wait_ge(exped, 1)
            done(nc.vector.tensor_reduce(m[:], e[:], AX.X, ALU.add))
            done(nc.vector.reciprocal(m[:], m[:]))
            done(nc.vector.tensor_tensor(e[:], e[:], over(m[:], NT), ALU.mult))
            for j in range(TOPK):
                done(nc.vector.tensor_reduce(best[:, j, :], e[:], AX.X, ALU.max))
                done(nc.vector.tensor_tensor(t[:], e[:], over(best[:, j, :], NT), ALU.is_equal))
                done(nc.vector.tensor_tensor(t[:], t[:], rank[:].unsqueeze(1).to_broadcast([P, NT, NE]), ALU.mult))
                done(nc.vector.tensor_reduce(m[:], t[:], AX.X, ALU.max))
                done(nc.vector.tensor_tensor(hot[:, j], t[:], over(m[:], NT), ALU.is_equal))
                if j == 0:
                    done(nc.vector.scalar_tensor_tensor(out=e[:], in0=hot[:, 0], scalar=-2.0, in1=e[:],
                                                        op0=ALU.mult, op1=ALU.add))
            done(nc.vector.tensor_tensor(m[:], best[:, 0, :], best[:, 1, :], ALU.add))
            done(nc.vector.reciprocal(m[:], m[:]))
            dve.wait_ge(counted, 2)
            total_f = total[:].rearrange("p c e -> p (c e)")
            done(nc.vector.tensor_copy(total_f, total_ps[:]))
            for ex in range(NE):
                ins = nc.vector.tensor_tensor_scan(upto[:, :, ex], ones[:, 0:TOPK * NT], total[:, :, ex], 0.0,
                                                   ALU.mult, ALU.add)
                if ex == NE - 1:
                    done(ins)
            done(nc.vector.tensor_tensor(upto[:], upto[:], total[:], ALU.subtract))
            done(nc.vector.tensor_tensor(place[:].rearrange("p c e -> p (c e)"),
                                         upto[:].rearrange("p c e -> p (c e)"), before_ps[:], ALU.add))
            hot_f = hot[:].rearrange("p j t e -> p (j t) e")
            done(nc.vector.tensor_tensor(pick[:], place[:], hot_f, ALU.mult))
            done(nc.vector.tensor_reduce(loc[:], pick[:], AX.X, ALU.add))
            done(nc.vector.tensor_tensor(pick[:], hot_f, first_slot[:].unsqueeze(1)
                                         .to_broadcast([P, TOPK * NT, NE]), ALU.mult))
            done(nc.vector.tensor_reduce(slot[:], pick[:], AX.X, ALU.add))
            done(nc.vector.tensor_tensor(slot[:], slot[:], loc[:], ALU.add))
            done(nc.vector.tensor_scalar(fits[:], loc[:], float(CAP), None, ALU.is_lt))
            done(nc.vector.tensor_tensor(slot[:], slot[:], fits[:], ALU.mult))
            nc.vector.tensor_copy(g["take"][:], slot[:])
            done(nc.vector.tensor_scalar(loc[:], fits[:], -1.0, 1.0, ALU.mult, ALU.add))
            done(nc.vector.tensor_tensor(loc[:], loc[:], outside[:], ALU.mult))
            done(nc.vector.tensor_tensor(loc[:], loc[:], slot[:], ALU.add))
            done(nc.vector.tensor_copy(put[:], loc[:]))
            assert n[0] == ROUTED, n[0]
            share = g["share"][:].rearrange("p (j t) -> p j t", j=TOPK)
            done(nc.vector.tensor_tensor(share, best[:], m[:].unsqueeze(1).to_broadcast([P, TOPK, NT]), ALU.mult))
            done(nc.vector.scalar_tensor_tensor(out=g["share"][:], in0=g["share"][:], scalar=0.5, in1=fits[:],
                                                op0=ALU.mult, op1=ALU.mult))

        @block.scalar
        def _(act):
            with act.Fori(0, NBLK) as i:
                for k in range(KD):
                    act.wait_ge(s["xT_ps_ready"], KD * i + k + 1)
                    act.wait_ge(l_ps_ready, i)
                    nc.scalar.copy(xT[:, k, :], xT_ps[k][:]).then_inc(s["xT_ready"], 1)
            act.wait_ge(rt, 2)
            nc.scalar.activation(e[:], e[:], ACT.Exp).then_inc(exped, 1)

        @block.tensor
        def _(pe):
            pe.wait_ge(w_in, W_IN)
            with pe.Fori(0, NBLK) as i:
                ln_transpose(nc, pe, i, xn, xT_ps, g["ident"], s)
                pe.wait_ge(s["xT_ready"], KD * (i + 1))
                pe.wait_ge(l_ready, i)
                for j in range(TPB):
                    for k in range(KD):
                        t = nc.tensor.matmul(l_ps[:, j, :], xT[:, k, j * P:(j + 1) * P], w[:, k, :],
                                             start=(k == 0), stop=(k == KD - 1))
                t.then_inc(l_ps_ready, 1)
            pe.wait_ge(rt, 16)
            hot_f = hot[:].rearrange("p j t e -> p (j t e)")
            nc.tensor.matmul(before_ps[:], earlier[:], hot_f, start=True, stop=True).then_inc(counted, 1)
            nc.tensor.matmul(total_ps[:], ones[:], hot_f, start=True, stop=True).then_inc(counted, 1)


def expert_block(nc, tag, g, a, slots_dram, done_dram):
    with ExitStack() as ctx:
        r = Room(nc, ctx, tag)
        w1 = r.sb("w1", [P, KD, EH])
        w2 = r.sb("w2", [P, EM, D])
        b1 = r.sb("b1", [P, EM])
        b2 = r.sb("b2", [P, D])
        x = r.sb("x", [P, TPB, D])
        xT = r.sb("xT", [P, KD, HALF])
        hid = r.sb("hid", [P, EM, HALF])
        y = r.sb("y", [P, TPB, D])
        xT_ps = [r.ps(f"xT_ps{k}", [P, HALF]) for k in range(KD)]
        h_ps = [r.ps(f"h_ps{i}", [P, HALF]) for i in range(3)]
        y_ps = [r.ps(f"y_ps{i}", [P, BLK])[:, 0:D] for i in range(3)]
        names = "w1_in w2_in x_in xT_ps_ready xT_ready h_ps_ready hid_ready y_ps_ready y_ready stored".split()
        s = {n: r.sem(n) for n in names}
        block = ctx.enter_context(nc.Block())
        STEPS = NE * HPE

        def on(eng, name, value):
            if not (isinstance(value, int) and value <= 0):
                eng.wait_ge(s[name], value)

        @block.sync
        def _(sp):
            w1_v = a["fc1_T"].rearrange("(k p) n -> p k n", p=P)
            w2_v = a["fc2"].rearrange("(m p) d -> p m d", p=P)

            def load_w1(e):
                on(sp, "h_ps_ready", EM * HPE * e)
                sp.dma_start(w1[:], w1_v[:, :, bass.ds(e * EH, EH)]).then_inc(s["w1_in"], 16)
                on(sp, "hid_ready", EM * HPE * e)
                sp.dma_start(b1[:], a["b1"][:, bass.ds(e * EM, EM)]).then_inc(s["w1_in"], 16)

            def load_w2(e):
                on(sp, "y_ps_ready", TPB * HPE * e)
                sp.dma_start(w2[:], w2_v[:, bass.ds(e * EM, EM), :]).then_inc(s["w2_in"], 16)
                on(sp, "y_ready", TPB * HPE * e)
                sp.dma_start(b2[:], a["b2"][bass.ds(e * D, D)].partition_broadcast(P)).then_inc(s["w2_in"], 16)

            def load_x(i):
                on(sp, "xT_ps_ready", KD * i)
                sp.dma_start(x[:], tiles(slots_dram, i)).then_inc(s["x_in"], 16)

            def store(i):
                sp.wait_ge(s["y_ready"], TPB * (i + 1))
                sp.dma_start(tiles(done_dram, i), y[:]).then_inc(s["stored"], 16)

            load_x(0)
            load_w1(0)
            load_w2(0)
            with sp.Fori(0, NE - 1) as e:
                load_x(e * HPE + 1)
                store(e * HPE)
                load_x(e * HPE + 2)
                load_w1(e + 1)
                store(e * HPE + 1)
                load_w2(e + 1)
            load_x(STEPS - 1)
            store(STEPS - 2)
            store(STEPS - 1)
            sp.wait_ge(s["stored"], 16 * STEPS)

        @block.tensor
        def _(pe):
            def turn(i):
                pe.wait_ge(s["x_in"], 16 * (i + 1))
                on(pe, "xT_ready", KD * i)
                for k in range(KD):
                    for j in range(TPB):
                        t = nc.tensor.transpose(xT_ps[k][:, j * P:(j + 1) * P], x[:, j, k * P:(k + 1) * P],
                                                g["ident"][:])
                    t.then_inc(s["xT_ps_ready"], 1)

            def up(i, e):
                pe.wait_ge(s["xT_ready"], KD * (i + 1))
                pe.wait_ge(s["w1_in"], 32 * (e + 1))
                for m in range(EM):
                    on(pe, "hid_ready", EM * i + max(m - 2, 0))
                    for k in range(KD):
                        t = nc.tensor.matmul(h_ps[m % 3][:], w1[:, k, m * P:(m + 1) * P], xT[:, k, :],
                                             start=(k == 0), stop=(k == KD - 1))
                    t.then_inc(s["h_ps_ready"], 1)

            def down(i, e):
                pe.wait_ge(s["hid_ready"], EM * (i + 1))
                pe.wait_ge(s["w2_in"], 32 * (e + 1))
                for j in range(TPB):
                    on(pe, "y_ready", TPB * i + max(j - 2, 0))
                    for m in range(EM):
                        t = nc.tensor.matmul(y_ps[j % 3], hid[:, m, j * P:(j + 1) * P], w2[:, m, :],
                                             start=(m == 0), stop=(m == EM - 1))
                    t.then_inc(s["y_ps_ready"], 1)

            def expert(e, last):
                up(e * HPE, e)
                turn(e * HPE + 1)
                down(e * HPE, e)
                up(e * HPE + 1, e)
                if not last:
                    turn(e * HPE + 2)
                down(e * HPE + 1, e)

            turn(0)
            with pe.Fori(0, NE - 1) as e:
                expert(e, False)
            expert(NE - 1, True)

        @block.scalar
        def _(act):
            def relu(i, e):
                on(act, "y_ps_ready", TPB * i)
                act.wait_ge(s["w1_in"], 32 * (e + 1))
                for m in range(EM):
                    act.wait_ge(s["h_ps_ready"], EM * i + m + 1)
                    nc.scalar.activation(hid[:, m, :], h_ps[m % 3][:], ACT.Relu, bias=b1[:, m:m + 1], scale=1.0)\
                        .then_inc(s["hid_ready"], 1)

            with act.Fori(0, NE) as e:
                for h in range(HPE):
                    relu(e * HPE + h, e)

        @block.vector
        def _(dve):
            def take_xT(i):
                for k in range(KD):
                    dve.wait_ge(s["xT_ps_ready"], KD * i + k + 1)
                    on(dve, "h_ps_ready", EM * i)
                    nc.vector.tensor_copy(xT[:, k, :], xT_ps[k][:]).then_inc(s["xT_ready"], 1)

            def take_y(i, e):
                dve.wait_ge(s["w2_in"], 32 * (e + 1))
                on(dve, "stored", 16 * i)
                for j in range(TPB):
                    dve.wait_ge(s["y_ps_ready"], TPB * i + j + 1)
                    nc.vector.tensor_tensor(y[:, j, :], y_ps[j % 3], b2[:], ALU.add).then_inc(s["y_ready"], 1)

            def expert(e, last):
                take_xT(e * HPE + 1)
                take_y(e * HPE, e)
                if not last:
                    take_xT(e * HPE + 2)
                take_y(e * HPE + 1, e)

            take_xT(0)
            with dve.Fori(0, NE - 1) as e:
                expert(e, False)
            expert(NE - 1, True)


def combine_block(nc, tag, g, x_in, done_dram, x_out):
    with ExitStack() as ctx:
        r = Room(nc, ctx, tag)
        NB = 4
        x = [r.sb(f"x{b}", [P, TPB, D]) for b in range(2)]
        got = [[r.sb(f"got{j}_{b}", [P, D]) for b in range(NB)] for j in range(TOPK)]
        x_loaded = [r.sem(f"x_loaded{b}") for b in range(2)]
        stored = [r.sem(f"stored{b}") for b in range(2)]
        fetched = [r.sem(f"fetched{b}") for b in range(NB)]
        added = r.sem("added")
        block = ctx.enter_context(nc.Block())

        @block.sync
        def _(sp):
            def load(i):
                if i >= 2:
                    sp.wait_ge(stored[i % 2], 16 * (i // 2))
                sp.dma_start(x[i % 2][:], tiles(x_in, i)).then_inc(x_loaded[i % 2], 16)

            load(0)
            load(1)
            for i in range(NBLK):
                sp.wait_ge(added, 2 * TPB * (i + 1))
                sp.dma_start(tiles(x_out, i), x[i % 2][:]).then_inc(stored[i % 2], 16)
                if i + 2 < NBLK:
                    load(i + 2)
            for b in range(2):
                sp.wait_ge(stored[b], 16 * (NBLK // 2))

        @block.gpsimd
        def _(pool):
            for i in range(NT):
                if i >= NB:
                    pool.wait_ge(added, 2 * (i - NB + 1))
                for j in range(TOPK):
                    c = j * NT + i
                    nc.gpsimd.indirect_dma_start(
                        out=got[j][i % NB][:], out_offset=None, in_=done_dram,
                        in_offset=bass.IndirectOffsetOnAxis(ap=g["take"][:, c:c + 1], axis=0),
                        bounds_check=NE * CAP - 1, oob_is_err=True).then_inc(fetched[i % NB], 16)

        @block.vector
        def _(dve):
            for i in range(NT):
                b, t = i // TPB % 2, i % TPB
                dve.wait_ge(x_loaded[b], 16 * (i // TPB // 2 + 1))
                dve.wait_ge(fetched[i % NB], 32 * (i // NB + 1))
                for j in range(TOPK):
                    c = j * NT + i
                    if j:
                        dve.wait_ge(added, 2 * i + 1)
                    nc.vector.scalar_tensor_tensor(out=x[b][:, t, :], in0=got[j][i % NB][:],
                                                   scalar=g["share"][:, c:c + 1], in1=x[b][:, t, :],
                                                   op0=ALU.mult, op1=ALU.add).then_inc(added, 1)



SPAD = SEQ + P
GH = 4
NGR = HEADS // GH


def qkv_block(nc, g, a, qkv, x_in):
    with ExitStack() as ctx:
        r = Room(nc, ctx, "qkv")
        x, xn, stat, mv, xT_ps, xT, s = ln_room(r)
        s["minus_half"] = g["minus_half"]
        w = {n: r.sb(n, [P, KD, D]) for n in ("wq_T", "wk_T", "wv_T")}
        qk_ps = [r.ps(f"qk_ps{i}", [P, BLK]) for i in range(2 * KD)]
        v_ps = [r.ps(f"v_ps{i}", [P, 2, D]) for i in range(TPB // 2)]
        w_in, qk_full, qk_taken, v_full, v_taken, padded = (
            r.sem(n) for n in ("w_in", "qk_full", "qk_taken", "v_full", "v_taken", "padded"))
        block = ctx.enter_context(nc.Block())
        LAST = NBLK - 1
        BPB = NBLK // BATCH
        PARTS = [(0, BPB, 0), (BPB, LAST, 1)]
        NV = TPB // 2

        @block.sync
        def _(sp):
            sp.dma_start(x[:], tiles(x_in, 0)).then_inc(s["x_loaded"], 16)
            for name, t in w.items():
                sp.dma_start(t[:], a[name].rearrange("(k p) n -> p k n", p=P)).then_inc(w_in, 16)
            with sp.Fori(0, LAST) as i:
                sp.wait_ge(s["ln"], LN_OPS * (i + 1))
                sp.dma_start(x[:], tiles(x_in, i + 1)).then_inc(s["x_loaded"], 16)

        @block.gpsimd
        def _(pool):
            for b in range(BATCH):
                nc.gpsimd.memset(qkv["kT"][:, :, b * SPAD:b * SPAD + P], 0.0).then_inc(padded, 1)
                nc.gpsimd.memset(qkv["v"][:, b * (QT + 1), :], 0.0).then_inc(padded, 1)
            with pool.Fori(0, NBLK) as i:
                ln_gpsimd(nc, pool, i, mv, s)
            pool.wait_ge(padded, 2 * BATCH)

        @block.vector
        def _(dve):
            def take_v(i, b):
                for m in range(NV):
                    dve.wait_ge(v_full, NV * i + m + 1)
                    nc.vector.tensor_copy(qkv["v"][:, bass.ds(i * TPB + (b + 1 + 2 * m), 2), :], v_ps[m][:])\
                        .then_inc(v_taken, 1)

            ln_vector(nc, dve, 0, x, xn, stat, mv, s)
            for lo, hi, b in PARTS:
                with dve.Fori(lo, hi) as i:
                    ln_vector(nc, dve, i + 1, x, xn, stat, mv, s)
                    take_v(i, b)
            take_v(LAST, 1)

        @block.scalar
        def _(act):
            def take_xT(i):
                for k in range(KD):
                    act.wait_ge(s["xT_ps_ready"], KD * i + k + 1)
                    if not (isinstance(i, int) and i == 0):
                        act.wait_ge(v_full, NV * i)
                    nc.scalar.copy(xT[:, k, :], xT_ps[k][:]).then_inc(s["xT_ready"], 1)

            def take_qk(i, b):
                for m in range(2 * KD):
                    act.wait_ge(qk_full, 2 * KD * i + m + 1)
                    name, pad = ("qT", 0) if m < KD else ("kT", (b + 1) * P)
                    nc.scalar.copy(qkv[name][:, m % KD, bass.ds(i * BLK + pad, BLK)], qk_ps[m][:])\
                        .then_inc(qk_taken, 1)

            take_xT(0)
            for lo, hi, b in PARTS:
                with act.Fori(lo, hi) as i:
                    take_qk(i, b)
                    take_xT(i + 1)
            take_qk(LAST, 1)

        @block.tensor
        def _(pe):
            def project(i, first):
                pe.wait_ge(s["xT_ready"], KD * (i + 1))
                for m in range(2 * KD):
                    if not first:
                        pe.wait_ge(qk_taken, 2 * KD * (i - 1) + m + 1)
                    name, f = ("wq_T", "wk_T")[m // KD], m % KD
                    for k in range(KD):
                        t = nc.tensor.matmul(qk_ps[m][:], w[name][:, k, f * P:(f + 1) * P], xT[:, k, :],
                                             start=(k == 0), stop=(k == KD - 1))
                    t.then_inc(qk_full, 1)
                for m in range(NV):
                    if not first:
                        pe.wait_ge(v_taken, NV * (i - 1) + m + 1)
                    for j in range(2):
                        c = 2 * m + j
                        for k in range(KD):
                            t = nc.tensor.matmul(v_ps[m][:, j, :], xT[:, k, c * P:(c + 1) * P], w["wv_T"][:, k, :],
                                                 start=(k == 0), stop=(k == KD - 1))
                    t.then_inc(v_full, 1)

            pe.wait_ge(w_in, 16 * 3)
            ln_transpose(nc, pe, 0, xn, xT_ps, g["ident"], s)
            project(0, True)
            with pe.Fori(1, NBLK) as i:
                ln_transpose(nc, pe, i, xn, xT_ps, g["ident"], s)
                project(i, False)


def attend_block(nc, g, a, qkv, x_in, x_out):
    with ExitStack() as ctx:
        r = Room(nc, ctx, "att")
        W2 = 2 * P
        wo_T = r.sb("wo_T", [P, KD, D])
        hmask = r.sb("hmask", [P, HPB])
        vmask = r.sb("vmask", [P, GH * HD])
        identb = r.sb("identb", [P, P], BF16)
        wmask = r.sb("wmask", [P, 2, 2 * W2], BF16)
        smask = r.sb("smask", [P, QT * BLK], BF16)
        ones = r.sb("ones", [P, P], BF16)
        xr = r.sb("xr", [P, D])
        q = [r.sb(f"q{b}", [P, KD, P]) for b in range(2)]
        qm = [r.sb(f"qm{b}", [P, HEADS, P]) for b in range(2)]
        Ks = [r.sb(f"Ks{b}", [P, KD, HPB, NSTR]) for b in range(BATCH)]
        vrows = [r.sb(f"vrows{b}", [P, NGR, GH * HD]) for b in range(BATCH)]
        Vs = [r.sb(f"Vs{b}", [P, NGR, GH * HD]) for b in range(BATCH)]
        top_s = r.sb("top_s", [P, HEADS])
        top_w = r.sb("top_w", [P, HEADS])
        shift_s = r.sb("shift_s", [P, HEADS])
        shift = r.sb("shift", [P, HEADS])
        den = [r.sb(f"den{b}", [P, HEADS]) for b in range(2)]
        den_s = r.sb("den_s", [P, HEADS])
        rden = r.sb("rden", [P, HEADS])
        probs = [r.sb(f"probs{b}", [P, GH, W2]) for b in range(2)]
        str_in = r.sb("str_in", [P, HEADS * NSTR])
        probs_s = r.sb("probs_s", [P, HEADS * NSTR])
        PT = [r.sb(f"PT{b}", [P, 2, GH, P]) for b in range(2)]
        PTs = r.sb("PTs", [P, NGR, P])
        on = r.sb("on", [P, D])
        OT = r.sb("OT", [P, KD, P])
        o = r.sb("o", [P, D])
        S_ps = [r.ps(f"S_ps{b}", [P, GH, W2]) for b in range(2)]
        Ss_ps = r.ps("Ss_ps", [P, BLK])
        T_ps = [r.ps(f"T_ps{b}", [P, BLK]) for b in range(2)]
        O_ps = r.ps("O_ps", [P, BLK])
        names = ("w_in vrows_in Ks_ready Vs_ready q_ready qm_ready Ss_ready S_ready top_s_ready shift_s_ready "
                 "tops shifts exp_done str_shifted str_exp str_turned PTs_taken turned0 turned1 PT0_taken "
                 "PT1_taken PV_done O_ready sums dens on_ready O_turned OT_taken out_ready o_ready xr_in "
                 "stored").split()
        s = {n: r.sem(n) for n in names}
        block = ctx.enter_context(nc.Block())
        LAST = NT - 1
        N_IN = 7

        def wait(eng, name, value):
            if not (isinstance(value, int) and value <= 0):
                eng.wait_ge(s[name], value)

        def all_tiles(eng, tile):
            for b in range(BATCH):
                tile(b * QT, 0, b)
                with eng.Fori(0, QT // 2 - 1) as i:
                    tile(i * 2 + (b * QT + 1), 1, b)
                    tile(i * 2 + (b * QT + 2), 0, b)
                tile(b * QT + QT - 1, 1, b)

        def is_first(t):
            return isinstance(t, int) and t == 0

        def is_last(t):
            return isinstance(t, int) and t == LAST

        @block.sync
        def _(sp):
            for b in range(BATCH):
                for c in range(GH):
                    for h in range(2):
                        dst = vrows[b][c * NSTR + h:(c + 1) * NSTR:2, :, :].rearrange("p g d -> p (g d)")
                        sp.dma_start(dst, qkv["v"][h * SPARSE:h * SPARSE + 1, b * (QT + 1) + 1:(b + 1) * (QT + 1), :])\
                            .then_inc(s["vrows_in"], 16)
            for dst, src in ((hmask[:], a["hmask"]), (identb[:], a["identb"]), (ones[0:1, :], a["ones_row"]),
                             (smask[0:1, :], a["strided_masks"]),
                             (wmask[:].rearrange("p a c -> p (a c)"), a["window_masks"]), (vmask[:], a["vmask"]),
                             (wo_T[:], a["wo_T"].rearrange("(k p) n -> p k n", p=P))):
                sp.dma_start(dst, src).then_inc(s["w_in"], 16)

            def tile(t, p, b):
                wait(sp, "o_ready", t)
                sp.dma_start(xr[:], x_in[bass.ds(t * P, P), :]).then_inc(s["xr_in"], 16)
                if not is_first(t):
                    sp.dma_start(x_out[bass.ds((t - 1) * P, P), :], o[:]).then_inc(s["stored"], 16)

            all_tiles(sp, tile)
            sp.wait_ge(s["o_ready"], NT)
            sp.dma_start(x_out[LAST * P:NT * P, :], o[:]).then_inc(s["stored"], 16)
            sp.wait_ge(s["stored"], 16 * NT)

        @block.gpsimd
        def _(pool):
            pool.wait_ge(s["w_in"], 16 * N_IN)

            def mask_q(t, p, b):
                pool.wait_ge(s["q_ready"], t + 1)
                wait(pool, "S_ready", NGR * (t - 1))
                for f in range(KD):
                    nc.gpsimd.tensor_tensor(qm[p][:, f * HPB:(f + 1) * HPB, :],
                                            q[p][:, f:f + 1, :].to_broadcast([P, HPB, P]),
                                            hmask[:].unsqueeze(2).to_broadcast([P, HPB, P]), ALU.mult)\
                        .then_inc(s["qm_ready"], 1)

            all_tiles(pool, mask_q)

        @block.vector
        def _(dve):
            def strided_keys(b):
                kT = qkv["kT"]
                for f in range(KD):
                    keys = kT[:, f, b * SPAD + P:(b + 1) * SPAD:SPARSE]
                    nc.vector.tensor_tensor(Ks[b][:, f, :, :], keys.unsqueeze(1).to_broadcast([P, HPB, NSTR]),
                                            hmask[:].unsqueeze(2).to_broadcast([P, HPB, NSTR]), ALU.mult)\
                        .then_inc(s["Ks_ready"], 1)
                nc.vector.tensor_tensor(Vs[b][:], vrows[b][:], vmask[:].unsqueeze(1).to_broadcast([P, NGR, GH * HD]),
                                        ALU.mult).then_inc(s["Vs_ready"], 1)

            def strided_tops(t):
                dve.wait_ge(s["Ss_ready"], t + 1)
                nc.vector.tensor_reduce(top_s[:], Ss_ps[:].rearrange("p (h k) -> p h k", h=HEADS), AX.X, ALU.max)\
                    .then_inc(s["top_s_ready"], 1)
                dve.wait_ge(s["top_s_ready"], t + 1)
                nc.vector.tensor_scalar(shift_s[:], top_s[:], -0.25, None, ALU.mult).then_inc(s["shift_s_ready"], 1)

            def maxima(t, gr):
                h = slice(gr * GH, (gr + 1) * GH)
                dve.wait_ge(s["S_ready"], t * NGR + gr + 1)
                nc.vector.tensor_reduce(top_w[:, h], S_ps[gr % 2][:], AX.X, ALU.max).then_inc(s["tops"], 1)
                dve.wait_ge(s["tops"], t * NGR + gr + 1)
                dve.wait_ge(s["shift_s_ready"], t + 1)
                wait(dve, "exp_done", GH * ((t - 1) * NGR + gr + 1))
                nc.vector.scalar_tensor_tensor(out=shift[:, h], in0=top_w[:, h], scalar=-0.25, in1=shift_s[:, h],
                                               op0=ALU.mult, op1=ALU.min).then_inc(s["shifts"], 1)

            def shift_strided(t):
                wait(dve, "str_exp", t)
                dve.wait_ge(s["shifts"], (t + 1) * NGR)
                nc.vector.scalar_tensor_tensor(
                    out=str_in[:].rearrange("p (h k) -> p h k", h=HEADS),
                    in0=Ss_ps[:].rearrange("p (h k) -> p h k", h=HEADS), scalar=0.25,
                    in1=shift[:].unsqueeze(2).to_broadcast([P, HEADS, NSTR]),
                    op0=ALU.mult, op1=ALU.add).then_inc(s["str_shifted"], 1)

            def take_PT0(t, gr):
                dve.wait_ge(s["turned0"], t * NGR + gr + 1)
                wait(dve, "PV_done", t * NGR + gr - 1)
                nc.vector.tensor_copy(PT[gr % 2][:, 0].rearrange("p h c -> p (h c)"), T_ps[0][:])\
                    .then_inc(s["PT0_taken"], 1)

            def denominators(t, p):
                dve.wait_ge(s["str_exp"], t + 1)
                nc.vector.tensor_reduce(den_s[:], probs_s[:].rearrange("p (h k) -> p h k", h=HEADS), AX.X, ALU.add)\
                    .then_inc(s["sums"], 1)
                dve.wait_ge(s["sums"], 2 * t + 1)
                dve.wait_ge(s["exp_done"], GH * NGR * (t + 1))
                nc.vector.tensor_tensor(den_s[:], den_s[:], den[p][:], ALU.add).then_inc(s["sums"], 1)
                dve.wait_ge(s["sums"], 2 * t + 2)
                wait(dve, "on_ready", t)
                nc.vector.reciprocal(rden[:], den_s[:]).then_inc(s["dens"], 1)

            def normalise(t):
                dve.wait_ge(s["O_ready"], t + 1)
                dve.wait_ge(s["dens"], t + 1)
                wait(dve, "O_turned", t)
                nc.vector.tensor_tensor(on[:].rearrange("p (h d) -> p h d", h=HEADS),
                                        O_ps[:, 0:D].rearrange("p (h d) -> p h d", h=HEADS),
                                        rden[:].unsqueeze(2).to_broadcast([P, HEADS, HD]), ALU.mult)\
                    .then_inc(s["on_ready"], 1)

            def output(t):
                dve.wait_ge(s["out_ready"], t + 1)
                dve.wait_ge(s["xr_in"], 16 * (t + 1))
                wait(dve, "stored", 16 * t)
                nc.vector.tensor_tensor(o[:], T_ps[1][:, 0:D], xr[:], ALU.add).then_inc(s["o_ready"], 1)

            dve.wait_ge(s["w_in"], 16 * N_IN)
            dve.wait_ge(s["vrows_in"], 16 * BATCH * GH * 2)
            for b in range(BATCH):
                strided_keys(b)

            def tile(t, p, b):
                strided_tops(t)
                maxima(t, 0)
                if not is_first(t):
                    take_PT0(t - 1, NGR - 1)
                    denominators(t - 1, 1 - p)
                for gr in range(1, NGR):
                    maxima(t, gr)
                    if gr == NGR - 1:
                        shift_strided(t)
                    take_PT0(t, gr - 1)
                    if gr == 1 and not is_first(t):
                        normalise(t - 1)
                if not is_first(t):
                    output(t - 1)

            all_tiles(dve, tile)
            take_PT0(LAST, NGR - 1)
            denominators(LAST, 1)
            normalise(LAST)
            output(LAST)

        @block.scalar
        def _(act):
            def take_q(t, p):
                wait(act, "Ss_ready", t - 1)
                wait(act, "qm_ready", KD * (t - 1))
                nc.scalar.copy(q[p][:], qkv["qT"][:, :, bass.ds(t * P, P)]).then_inc(s["q_ready"], 1)

            def exps(t, p, gr):
                act.wait_ge(s["shifts"], t * NGR + gr + 1)
                wait(act, "turned0", t * NGR + gr - 1)
                wait(act, "turned1", t * NGR + gr - 1)
                if gr == 0:
                    wait(act, "dens", t - 1)
                for h in range(GH):
                    hh = gr * GH + h
                    nc.scalar.activation(probs[gr % 2][:, h, :], S_ps[gr % 2][:, h, :], ACT.Exp,
                                         bias=shift[:, hh:hh + 1], scale=0.25,
                                         accum_out=den[p][:, hh:hh + 1]).then_inc(s["exp_done"], 1)

            def exp_strided(t):
                act.wait_ge(s["str_shifted"], t + 1)
                wait(act, "str_turned", t)
                wait(act, "dens", t)
                nc.scalar.activation(probs_s[:], str_in[:], ACT.Exp).then_inc(s["str_exp"], 1)

            def take_PT1(t, gr):
                act.wait_ge(s["turned1"], t * NGR + gr + 1)
                wait(act, "PV_done", t * NGR + gr - 1)
                nc.scalar.copy(PT[gr % 2][:, 1].rearrange("p h c -> p (h c)"), T_ps[1][:])\
                    .then_inc(s["PT1_taken"], 1)

            def take_PTs(t):
                act.wait_ge(s["str_turned"], t + 1)
                wait(act, "O_ready", t)
                nc.scalar.copy(PTs[:].rearrange("p h c -> p (h c)"), T_ps[1][:]).then_inc(s["PTs_taken"], 1)

            def take_OT(t):
                act.wait_ge(s["O_turned"], t + 1)
                wait(act, "out_ready", t)
                nc.scalar.copy(OT[:].rearrange("p k c -> p (k c)"), T_ps[1][:, 0:D]).then_inc(s["OT_taken"], 1)

            def tile(t, p, b):
                exps(t, p, 0)
                if not is_first(t):
                    take_PT1(t - 1, NGR - 1)
                    take_PTs(t - 1)
                if not is_last(t):
                    take_q(t + 1, 1 - p)
                for gr in range(1, NGR):
                    exps(t, p, gr)
                    if gr == NGR - 1:
                        exp_strided(t)
                    take_PT1(t, gr - 1)
                    if gr == 2 and not is_first(t):
                        take_OT(t - 1)

            take_q(0, 0)
            all_tiles(act, tile)
            take_PT1(LAST, NGR - 1)
            take_PTs(LAST)
            take_OT(LAST)

        @block.tensor
        def _(pe):
            def scores_strided(t, p, b):
                pe.wait_ge(s["q_ready"], t + 1)
                wait(pe, "str_shifted", t)
                nc.tensor.matmul(Ss_ps[:], ones[0:1, :], smask[0:1, bass.ds((t - b * QT) * BLK, BLK)],
                                 start=True, stop=False, skip_group_check=True)
                for f in range(KD):
                    m = nc.tensor.matmul(Ss_ps[:, f * D:(f + 1) * D], q[p][:, f, :],
                                         Ks[b][:, f, :, :].rearrange("p h k -> p (h k)"),
                                         start=False, stop=True, skip_group_check=True)
                m.then_inc(s["Ss_ready"], 1)

            def scores(t, p, b, gr):
                first = isinstance(t, int) and t % QT == 0
                if gr == 0:
                    pe.wait_ge(s["qm_ready"], KD * (t + 1))
                wait(pe, "exp_done", GH * (t * NGR + gr - 1))
                for h2 in range(2):
                    nc.tensor.matmul(S_ps[gr % 2][:, 2 * h2:2 * h2 + 2, :].rearrange("p h c -> p (h c)"), identb[:],
                                     wmask[:, 0 if first else 1, :], start=True, stop=False, skip_group_check=True)
                    for h in (2 * h2, 2 * h2 + 1):
                        hh = gr * GH + h
                        m = nc.tensor.matmul(S_ps[gr % 2][:, h, :], qm[p][:, hh, :],
                                             qkv["kT"][:, hh // HPB, bass.ds(t * P + b * P, W2)],
                                             start=False, stop=True, skip_group_check=True)
                m.then_inc(s["S_ready"], 1)

            def turn_P(t, gr, c):
                if c == 0:
                    pe.wait_ge(s["exp_done"], GH * (t * NGR + gr + 1))
                    wait(pe, "PT0_taken", t * NGR + gr)
                else:
                    wait(pe, "PT1_taken", t * NGR + gr)
                    if gr == 0:
                        wait(pe, "PTs_taken", t)
                    if gr == 2:
                        wait(pe, "OT_taken", t)
                    if gr == 3:
                        wait(pe, "o_ready", t)
                for h in range(GH):
                    m = nc.tensor.transpose(T_ps[c][:, h * P:(h + 1) * P], probs[gr % 2][:, h, c * P:(c + 1) * P],
                                            g["ident"][:])
                m.then_inc(s[f"turned{c}"], 1)

            def gather_V(t, b, gr):
                pe.wait_ge(s["PT0_taken"], t * NGR + gr + 1)
                pe.wait_ge(s["PT1_taken"], t * NGR + gr + 1)
                if gr == 0:
                    wait(pe, "on_ready", t)
                for c in range(2):
                    for h in range(GH):
                        hh = gr * GH + h
                        m = nc.tensor.matmul(O_ps[:, hh * HD:(hh + 1) * HD], PT[gr % 2][:, c, h, :],
                                             qkv["v"][:, bass.ds(t + (b + c), 1), hh * HD:(hh + 1) * HD]
                                             .rearrange("p a d -> p (a d)"),
                                             start=(gr == 0 and c == 0 and h == 0), stop=False, skip_group_check=True)
                m.then_inc(s["PV_done"], 1)

            def turn_strided(t):
                pe.wait_ge(s["str_exp"], t + 1)
                pe.wait_ge(s["PT1_taken"], (t + 1) * NGR)
                for gr in range(NGR):
                    m = nc.tensor.transpose(T_ps[1][:, gr * P:(gr + 1) * P], probs_s[:, gr * P:(gr + 1) * P],
                                            g["ident"][:])
                m.then_inc(s["str_turned"], 1)

            def gather_strided(t, b):
                pe.wait_ge(s["PTs_taken"], t + 1)
                for gr in range(NGR):
                    m = nc.tensor.matmul(O_ps[:, gr * GH * HD:(gr + 1) * GH * HD], PTs[:, gr, :], Vs[b][:, gr, :],
                                         start=False, stop=True, skip_group_check=True)
                m.then_inc(s["O_ready"], 1)

            def turn_O(t, last):
                pe.wait_ge(s["on_ready"], t + 1)
                if not last:
                    pe.wait_ge(s["PT1_taken"], (t + 1) * NGR + 2)
                for k in range(KD):
                    m = nc.tensor.transpose(T_ps[1][:, k * P:(k + 1) * P], on[:, k * P:(k + 1) * P], g["ident"][:])
                m.then_inc(s["O_turned"], 1)

            def project_out(t, last):
                pe.wait_ge(s["OT_taken"], t + 1)
                if not last:
                    pe.wait_ge(s["PT1_taken"], (t + 1) * NGR + 3)
                for k in range(KD):
                    m = nc.tensor.matmul(T_ps[1][:, 0:D], OT[:, k, :], wo_T[:, k, :],
                                         start=(k == 0), stop=(k == KD - 1))
                m.then_inc(s["out_ready"], 1)

            pe.wait_ge(s["w_in"], 16 * N_IN)
            pe.wait_ge(s["Ks_ready"], KD * BATCH)
            pe.wait_ge(s["Vs_ready"], BATCH)
            scores_strided(0, 0, 0)
            scores(0, 0, 0, 0)

            def tile(t, p, b):
                last = is_last(t)
                prev_b = b - 1 if isinstance(t, int) and t % QT == 0 else b
                next_b = b + 1 if isinstance(t, int) and t % QT == QT - 1 else b
                for gr in range(NGR):
                    if gr < NGR - 1:
                        scores(t, p, b, gr + 1)
                    elif not last:
                        scores_strided(t + 1, 1 - p, next_b)
                        scores(t + 1, 1 - p, next_b, 0)
                    if not is_first(t):
                        if gr == 0:
                            turn_strided(t - 1)
                        if gr == 2:
                            turn_O(t - 1, False)
                        if gr == 3:
                            project_out(t - 1, False)
                    turn_P(t, gr, 0)
                    if gr:
                        gather_V(t, b, gr - 1)
                    elif not is_first(t):
                        gather_V(t - 1, prev_b, NGR - 1)
                    turn_P(t, gr, 1)
                    if gr == 0 and not is_first(t):
                        gather_strided(t - 1, prev_b)

            all_tiles(pe, tile)
            gather_V(LAST, BATCH - 1, NGR - 1)
            turn_strided(LAST)
            gather_strided(LAST, BATCH - 1)
            turn_O(LAST, True)
            project_out(LAST, True)


def attention(nc, g, a, x_in, x_out):
    with ExitStack() as ctx:
        r = Room(nc, ctx, "qkv_out")
        qkv = dict(qT=r.sb("qT", [P, KD, TOK]), kT=r.sb("kT", [P, KD, BATCH * SPAD]),
                   v=r.sb("v", [P, BATCH * (QT + 1), D]))
        qkv_block(nc, g, a, qkv, x_in)
        attend_block(nc, g, a, qkv, x_in, x_out)



def macaron_program(nc, out, ins):
    def scratch(name, shape):
        return nc.dram_tensor(name, shape, F32).ap()

    Room.sems = []
    a = ins
    stream = [a["x"]] + [scratch(f"x{i}", (TOK, D)) for i in range(1, 6)] + [out.rearrange("b t d -> (b t) d")]
    proj_T = scratch("proj_T", (2 * INNER, BATCH * HPAD))
    bc_T = scratch("bc_T", (2 * STATE, TOK + BLK))
    with ExitStack() as ctx:
        r = Room(nc, ctx, "g")
        g = dict(ident=r.sb("ident", [P, P]), w_up=r.sb("w_up", [P, KD, FH]), w_down=r.sb("w_down", [P, FM, D]),
                 b_up=r.sb("b_up", [P, FM]), half_bias=r.sb("half_bias", [P, D]),
                 neg_A=r.sb("neg_A", [P, IB, STATE]), minus_half=r.sb("minus_half", [P, STATE]),
                 zeros=r.sb("zeros", [P, 2 * BLK]), take=r.sb("take", [P, TOPK * NT], I32),
                 share=r.sb("share", [P, TOPK * NT]))
        fold_block(nc, g, a)
        ffn_block(nc, "ffn0", g, stream[0], stream[1])
        inproj_block(nc, g, a, stream[1], proj_T)
        mamba_block(nc, g, a, stream[1], proj_T, bc_T, stream[2])
        ffn_block(nc, "ffn1", g, stream[2], stream[3])
        recycle_semaphores(nc)
        for m in range(2):
            if m:
                attention(nc, g, a, stream[4], stream[5])
            slots = scratch(f"slots{m}", (NE * CAP, D))
            done = scratch(f"done{m}", (NE * CAP, D))
            route_block(nc, f"route{m}", g, a, stream[3 + 2 * m], slots)
            expert_block(nc, f"expert{m}", g, a, slots, done)
            combine_block(nc, f"combine{m}", g, stream[3 + 2 * m], done, stream[4 + 2 * m])



def layouts(np, v):
    def columns(vec):
        return vec.reshape(-1, P).T

    wqkv = v["L1_attn_w_qkv"]
    return dict(
        x=v["L0_attn_hidden_states"].reshape(TOK, D),
        w_exp=v["L0_ffn_W_exp"], w_con_T=v["L0_ffn_W_con"].T, b_exp=v["L0_ffn_b_exp"][None],
        up_w=v["L0_ffn_up_weights"].transpose(0, 3, 2, 1).reshape(STAGES, 2 * FH),
        down_w=v["L0_ffn_down_weights"][::-1].transpose(0, 2, 3, 1).reshape(STAGES, 2 * FH),
        up_bias=v["L0_ffn_up_bias"][None], b_con=v["L0_ffn_b_con"], down_bias=v["L0_ffn_down_bias"],
        A_log=v["L0_attn_A_log"], in_proj_T=v["L0_attn_in_proj_w"].T,
        conv_w=v["L0_attn_conv_w"].reshape(INNER, TAPS), conv_b=columns(v["L0_attn_conv_b"]),
        x_proj_T=v["L0_attn_x_proj_w"].T, dt_proj_T=v["L0_attn_dt_proj_w"].T,
        dt_bias=columns(v["L0_attn_dt_proj_b"]), D=columns(v["L0_attn_D"]), out_proj_T=v["L0_attn_out_proj_w"].T,
        xd_ln_w=np.concatenate([v["L0_attn_dt_ln_w"], v["L0_attn_b_ln_w"], v["L0_attn_c_ln_w"]])[:, None],
        gate_T=v["L1_ffn_gate_w"].T, fc1_T=v["L1_ffn_fc1_w"].transpose(2, 0, 1).reshape(D, NE * EH),
        fc2=v["L1_ffn_fc2_w"].reshape(NE * EH, D), b1=columns(v["L1_ffn_fc1_b"]), b2=v["L1_ffn_fc2_b"].reshape(-1),
        wq_T=wqkv[0:D].T, wk_T=wqkv[D:2 * D].T, wv_T=wqkv[2 * D:3 * D].T, wo_T=v["L1_attn_w_out"].T)


def constants(np):
    p = np.arange(P)
    f32, bf16 = np.dtype(np.float32), mybir.dt.np(BF16)
    row, col = p[:, None], p[None, :]
    keep = np.ones((P, NBLK + 1), f32)
    keep[:, 0::NBLK // BATCH] = 0
    own = np.where(col <= row, 0, NEG)
    before = np.where((col >= row) | (col % SPARSE == 0), 0, NEG)
    none = np.full((P, P), NEG)
    window = np.concatenate([none, own] * 2 + [before, own] * 2, axis=1)
    strided = np.concatenate([np.tile(np.where(np.arange(NSTR) * SPARSE < P * (i - 1), 0, NEG), HEADS)
                              for i in range(QT)])[None]
    return dict(
        ident=np.eye(P, dtype=f32), keep=keep,
        rank=np.tile(NE - np.arange(NE), (P, 1)).astype(f32),
        first_slot=np.tile(CAP * np.arange(NE), (P, 1)).astype(f32),
        outside=(NE * CAP + np.arange(TOPK * NT)[None] * P + row).astype(f32),
        earlier=(row < col).astype(f32), ones=np.ones((P, P), f32),
        hmask=(row // HD == np.arange(HPB)).astype(f32),
        vmask=(row // NSTR == np.arange(GH * HD) // HD).astype(f32),
        identb=np.eye(P).astype(bf16), ones_row=np.ones((1, P)).astype(bf16),
        window_masks=window.astype(bf16), strided_masks=strided.astype(bf16))


def kernel(**inputs):
    import numpy as np
    import concourse.bacc as bacc
    from concourse.bass_utils import run_bass_kernel_spmd

    nc = bacc.Bacc("TRN2", target_bir_lowering=False, num_devices=1)
    arrays, ins = {}, {}
    for name, value in {**layouts(np, inputs), **constants(np)}.items():
        value = np.ascontiguousarray(value)
        arrays[f"in_{name}_dram"] = value
        ins[name] = nc.dram_tensor(f"in_{name}_dram", value.shape, mybir.dt.from_np(value.dtype),
                                   kind="ExternalInput").ap()
    out = nc.dram_tensor("out_0_dram", (BATCH, SEQ, D), F32, kind="ExternalOutput").ap()
    macaron_program(nc, out, ins)
    result = run_bass_kernel_spmd(nc, [arrays], core_ids=[0])
    return result.results[0]["out_0_dram"]
```

```python
from contextlib import ExitStack

import concourse.bass as bass
from concourse import mybir

F32 = mybir.dt.float32
BF16 = mybir.dt.bfloat16
F32R = mybir.dt.float32r
I32 = mybir.dt.int32
ALU = mybir.AluOpType
ACT = mybir.ActivationFunctionType
AX = mybir.AxisListType

P = 128
BATCH, SEQ, D = 2, 2048, 256
TOK = BATCH * SEQ
KD = D // P
BLK = 512
NBLK = TOK // BLK
TPB = BLK // P
NT = TOK // P
LN_EPS = 1e-5
RMS_EPS = 1e-6
FH = 1024
FM = FH // P
STAGES = 10
INNER, STATE, TAPS, RANK = 512, 16, 4, 64
IB = INNER // P
XD = RANK + 2 * STATE
HPAD = SEQ + TAPS - 1
HEADS, HD = 16, 16
HPB = P // HD
SPARSE = 64
NSTR = SEQ // SPARSE
QT = SEQ // P
NEG = -1.0e30
NE, EH, CAP, TOPK = 8, 1024, 1024, 2
EM = EH // P
HALF = 512
HPE = CAP // HALF


class Room:

    def __init__(self, nc, ctx, tag):
        self.nc, self.ctx, self.tag = nc, ctx, tag

    def sb(self, name, shape, dt=F32):
        return self.ctx.enter_context(self.nc.sbuf_tensor(f"{self.tag}_{name}", shape, dt))

    def ps(self, name, shape, dt=F32):
        return self.ctx.enter_context(self.nc.psum_tensor(f"{self.tag}_{name}", shape, dt))

    def sem(self, name):
        sem = self.nc.alloc_semaphore(f"{self.tag}_{name}")
        Room.sems.append(sem)
        return sem

    sems = []


def recycle_semaphores(nc):
    nc.clear_and_free_semaphores(Room.sems)
    Room.sems = []
    nc.all_engine_barrier()


def tiles(dram, i, n=TPB):
    return dram[bass.ds(i * (n * P), n * P), :].rearrange("(j p) d -> p j d", p=P)



def product(nc, out, lhs, rhs, start, stop):
    nc.tensor.matmul(out, lhs[0], rhs[0], start=start, stop=False)
    nc.tensor.matmul(out, lhs[1], rhs[0], start=False, stop=False)
    return nc.tensor.matmul(out, lhs[0], rhs[1], start=False, stop=stop)


def low_part(engine, low, x, high):
    return engine.tensor_tensor(low, x, high.bitcast(F32), ALU.subtract)



LN_OPS = 3 * TPB + 2


def ln_vector(nc, dve, i, x, xn, stat, mv, s, n=TPB):
    ops = 3 * n + 2
    dve.wait_ge(s["x_loaded"], 16 * (i + 1))
    for j in range(n):
        nc.vector.bn_stats(stat[:, j, :], x[:, j, :]).then_inc(s["ln"], 1)
    dve.wait_ge(s["ln"], i * ops + n)
    nc.vector.tensor_copy(mv[:, n, :], stat[:, n - 1, 0:2]).then_inc(s["ln"], 1)
    for j in range(n):
        nc.vector.bn_aggr(mv[:, j, :], stat[:, j, :]).then_inc(s["ln"], 1)
    dve.wait_ge(s["ln"], i * ops + 2 * n + 1)
    nc.vector.tensor_scalar(mv[:, 0:n, 1], mv[:, 0:n, 1], LN_EPS, None, ALU.add).then_inc(s["ln"], 1)
    dve.wait_ge(s["rstd_ready"], i + 1)
    dve.wait_ge(s["xT_ps_ready"], KD * i)
    for j in range(n):
        nc.vector.tensor_scalar(xn[:, j, :], x[:, j, :], mv[:, j, 0:1], s["rstd"][:, j:j + 1],
                                ALU.subtract, ALU.mult).then_inc(s["ln"], 1)


def ln_gpsimd(nc, pool, i, mv, s, n=TPB):
    pool.wait_ge(s["ln"], i * (3 * n + 2) + 2 * n + 2)
    nc.gpsimd.tensor_tensor(s["rstd"][:, 0:n], mv[:, 0:n, 1], s["minus_half"][:, 0:n], ALU.pow)\
        .then_inc(s["rstd_ready"], 1)


def ln_transpose(nc, pe, i, xn, xT_ps, ident, s, n=TPB):
    pe.wait_ge(s["ln"], (i + 1) * (3 * n + 2))
    pe.wait_ge(s["xT_ready"], KD * i)
    for k in range(KD):
        for j in range(n):
            t = nc.tensor.transpose(xT_ps[k][:, j * P:(j + 1) * P], xn[:, j, k * P:(k + 1) * P], ident[:])
        t.then_inc(s["xT_ps_ready"], 1)


def ln_high(nc, act, i, xT, xT_ps, s, used, count):
    for k in range(KD):
        act.wait_ge(s["xT_ps_ready"], KD * i + k + 1)
        act.wait_ge(used, count)
        nc.scalar.copy(xT[0][:, k, :], xT_ps[k][:]).then_inc(s["xT_high_ready"], 1)


def ln_low(nc, dve, i, xT, xT_ps, s):
    for k in range(KD):
        dve.wait_ge(s["xT_high_ready"], KD * i + k + 1)
        low_part(nc.vector, xT[1][:, k, :], xT_ps[k][:], xT[0][:, k, :]).then_inc(s["xT_ready"], 1)


def ln_room(r, n=TPB, split=True):
    x = r.sb("x", [P, n, D])
    xn = r.sb("xn", [P, n, D])
    stat = r.sb("stat", [P, n, 6])
    mv = r.sb("mv", [P, n + 1, 2])
    xT_ps = [r.ps(f"xT_ps{k}", [P, n * P]) for k in range(KD)]
    if split:
        xT = [r.sb(f"xT_{part}", [P, KD, n * P], F32R) for part in ("high", "low")]
    else:
        xT = r.sb("xT", [P, KD, n * P])
    s = {k: r.sem(k) for k in ("x_loaded", "ln", "rstd_ready", "xT_ps_ready", "xT_high_ready", "xT_ready")}
    s["rstd"] = r.sb("rstd", [P, n])
    return x, xn, stat, mv, xT_ps, xT, s



def fold_block(nc, g, a):
    with ExitStack() as ctx:
        r = Room(nc, ctx, "fold")
        mats = [[r.sb(f"m{m}_{b}", [P, KD, FH]) for b in range(2)] for m in range(2)]
        w = [[r.sb(f"w{m}_{b}", [P, 2 * FH]) for b in range(2)] for m in range(2)]
        prod = [r.sb(f"prod{t}", [P, FH]) for t in range(4)]
        row = [r.sb(f"row{b}", [1, FH]) for b in range(2)]
        rprod = [r.sb(f"rprod{t}", [1, FH]) for t in range(2)]
        up_bias = r.sb("up_bias", [1, FH])
        con_bias = r.sb("con_bias", [P, 2, D])
        alog = r.sb("alog", [P, IB, STATE])
        ps = [r.ps(f"ps{i}", [P, BLK]) for i in range(4)]
        bias_ps = r.ps("bias_ps", [P, FM])
        base_in = r.sem("base_in")
        const_in = r.sem("const_in")
        w_in = [[r.sem(f"w_{n}_in{b}") for b in range(2)] for n in ("up", "down")]
        dv = r.sem("dv")
        rows = r.sem("rows")
        turned = r.sem("turned")
        biased = r.sem("biased")
        taken = r.sem("taken")
        block = ctx.enter_context(nc.Block())
        PER = 2 * KD * 3

        @block.sync
        def _(sp):
            sp.dma_start(mats[0][0][:], a["w_exp"].rearrange("(k p) h -> p k h", p=P)).then_inc(base_in, 16)
            sp.dma_start(mats[1][0][:], a["w_con_T"].rearrange("(k p) h -> p k h", p=P)).then_inc(base_in, 16)
            sp.dma_start(row[0][:], a["b_exp"]).then_inc(base_in, 16)
            for st in range(STAGES):
                for m, name in enumerate(("up_w", "down_w")):
                    if st >= 2:
                        sp.wait_ge(dv, (st - 1) * PER)
                        sp.wait_ge(rows, (st - 1) * 3)
                    sp.dma_start(w[m][st % 2][:], a[name][st, :].partition_broadcast(P)).then_inc(w_in[m][st % 2], 16)
            sp.dma_start(up_bias[:], a["up_bias"]).then_inc(const_in, 16)
            sp.dma_start(g["ident"][:], a["ident"]).then_inc(const_in, 16)
            sp.dma_start(con_bias[:, 0, :], a["b_con"].partition_broadcast(P)).then_inc(const_in, 16)
            sp.dma_start(con_bias[:, 1, :], a["down_bias"].partition_broadcast(P)).then_inc(const_in, 16)
            sp.dma_start(alog[:], a["A_log"].rearrange("(k p) n -> p k n", p=P)).then_inc(const_in, 16)

        def stage(src, dst, wt, s, q0, q1):
            si = src.rearrange("p (n t s) -> p t n s", t=2, s=s)
            do = dst.rearrange("p (n t s) -> p t n s", t=2, s=s)
            wi = wt.rearrange("p (i o n s) -> p i o n s", i=2, o=2, s=s)
            return si, do, wi, [q.rearrange("p (o n s) -> p o n s", o=2, s=s) for q in (q0, q1)]

        @block.vector
        def _(dve):
            dve.wait_ge(base_in, 48)
            for st in range(STAGES):
                for m in range(2):
                    s = 2 ** st if m == 0 else 2 ** (STAGES - 1 - st)
                    dve.wait_ge(w_in[m][st % 2], 16 * (st // 2 + 1))
                    for k in range(KD):
                        n0 = st * PER + (m * KD + k) * 3
                        si, do, wi, q = stage(mats[m][st % 2][:, k, :], mats[m][1 - st % 2][:, k, :],
                                              w[m][st % 2][:], s, prod[2 * k][:], prod[2 * k + 1][:])
                        if n0:
                            dve.wait_ge(dv, n0)
                        for i in range(2):
                            nc.vector.tensor_tensor(q[i], wi[:, i], si[:, i:i + 1].to_broadcast(list(q[i].shape)),
                                                    ALU.mult).then_inc(dv, 1)
                        dve.wait_ge(dv, n0 + 2)
                        nc.vector.tensor_tensor(do, q[0], q[1], ALU.add).then_inc(dv, 1)
            dve.wait_ge(dv, STAGES * PER)
            nc.vector.tensor_copy(g["w_up"][:], mats[0][0][:]).then_inc(dv, 1)
            dve.wait_ge(const_in, 80)
            nc.vector.tensor_tensor(con_bias[:, 0, :], con_bias[:, 0, :], con_bias[:, 1, :], ALU.add).then_inc(dv, 1)
            dve.wait_ge(dv, STAGES * PER + 2)
            nc.vector.tensor_scalar(g["half_bias"][:], con_bias[:, 0, :], 0.5, None, ALU.mult).then_inc(dv, 1)
            dve.wait_ge(biased, 1)
            nc.vector.tensor_copy(g["b_up"][:], bias_ps[:]).then_inc(dv, 1)

        @block.gpsimd
        def _(pool):
            nc.gpsimd.memset(g["minus_half"][:], -0.5)
            nc.gpsimd.memset(g["zeros"][:], 0.0)
            pool.wait_ge(base_in, 48)
            for st in range(STAGES):
                pool.wait_ge(w_in[0][st % 2], 16 * (st // 2 + 1))
                if st:
                    pool.wait_ge(rows, st * 3)
                si, do, wi, q = stage(row[st % 2][:], row[1 - st % 2][:], w[0][st % 2][0:1, :], 2 ** st,
                                      rprod[0][:], rprod[1][:])
                for i in range(2):
                    nc.gpsimd.tensor_tensor(q[i], wi[:, i], si[:, i:i + 1].to_broadcast(list(q[i].shape)),
                                            ALU.mult).then_inc(rows, 1)
                pool.wait_ge(rows, st * 3 + 2)
                nc.gpsimd.tensor_tensor(do, q[0], q[1], ALU.add).then_inc(rows, 1)
            pool.wait_ge(rows, STAGES * 3)
            pool.wait_ge(const_in, 80)
            nc.gpsimd.tensor_tensor(row[1][:], row[0][:], up_bias[:], ALU.add).then_inc(rows, 1)

        @block.tensor
        def _(pe):
            pe.wait_ge(const_in, 80)
            pe.wait_ge(rows, STAGES * 3 + 1)
            for m in range(FM):
                t = nc.tensor.matmul(bias_ps[:, m:m + 1], row[1][0:1, m * P:(m + 1) * P], g["ident"][0:1, 0:1],
                                     start=True, stop=True)
            t.then_inc(biased, 1)
            pe.wait_ge(dv, STAGES * PER)
            for m in range(FM):
                if m >= 4 and m % 2 == 0:
                    pe.wait_ge(taken, m // 2 - 1)
                for k in range(KD):
                    t = nc.tensor.transpose(ps[m // 2 % 2][:, m % 2 * D + k * P:m % 2 * D + (k + 1) * P],
                                            mats[1][0][:, k, m * P:(m + 1) * P], g["ident"][:])
                if m % 2:
                    t.then_inc(turned, 1)

        @block.scalar
        def _(act):
            for m2 in range(FM // 2):
                act.wait_ge(turned, m2 + 1)
                nc.scalar.copy(g["w_down"][:, 2 * m2:2 * m2 + 2, :].rearrange("p m d -> p (m d)"), ps[m2 % 2][:])\
                    .then_inc(taken, 1)
            act.wait_ge(const_in, 80)
            nc.scalar.activation(alog[:], alog[:], ACT.Exp).then_inc(taken, 1)
            act.wait_ge(taken, FM // 2 + 1)
            nc.scalar.mul(g["neg_A"][:], alog[:], -1.0).then_inc(taken, 1)



def ffn_block(nc, tag, g, x_in, x_out):
    with ExitStack() as ctx:
        r = Room(nc, ctx, tag)
        x, xn, stat, mv, xT_ps, xT, s = ln_room(r)
        s["minus_half"] = g["minus_half"]
        xb = r.sb("xb", [P, TPB, D])
        hid = r.sb("hid", [P, FM, BLK])
        hid_high, hid_low = (r.sb(f"hid_{part}", [P, FM, BLK], F32R) for part in ("high", "low"))
        y = r.sb("y", [P, TPB, D])
        up_w = [r.sb(f"up_{part}", [P, KD, FH], F32R) for part in ("high", "low")]
        down_w = [r.sb(f"down_{part}", [P, FM, D], F32R) for part in ("high", "low")]
        w_high, w_low = r.sem("w_high"), r.sem("w_low")
        h_ps = [r.ps(f"h_ps{i}", [P, BLK]) for i in range(3)]
        y_ps = [r.ps(f"y_ps{i}", [P, BLK])[:, 0:D] for i in range(3)]
        xb_ready, h_ps_ready, hid_ready, low_ready, y_ps_ready, y_ready, stored = (
            r.sem(n) for n in ("xb_ready", "h_ps_ready", "hid_ready", "low_ready", "y_ps_ready", "y_ready", "stored"))
        block = ctx.enter_context(nc.Block())
        LAST = NBLK - 1

        @block.sync
        def _(sp):
            def load(i):
                sp.dma_start(x[:], tiles(x_in, i)).then_inc(s["x_loaded"], 16)

            def store(i):
                sp.wait_ge(y_ready, TPB * (i + 1))
                sp.dma_start(tiles(x_out, i), y[:]).then_inc(stored, 16)

            load(0)
            with sp.Fori(0, LAST) as i:
                sp.wait_ge(s["ln"], LN_OPS * (i + 1))
                sp.wait_ge(xb_ready, i + 1)
                load(i + 1)
                store(i)
            store(LAST)
            sp.wait_ge(stored, 16 * NBLK)

        @block.gpsimd
        def _(pool):
            def biased(i):
                pool.wait_ge(s["x_loaded"], 16 * (i + 1))
                pool.wait_ge(y_ready, TPB * i)
                nc.gpsimd.tensor_tensor(xb[:], x[:], g["half_bias"][:].unsqueeze(1).to_broadcast([P, TPB, D]),
                                        ALU.add).then_inc(xb_ready, 1)

            with pool.Fori(0, NBLK) as i:
                ln_gpsimd(nc, pool, i, mv, s)
                biased(i)

        @block.vector
        def _(dve):
            def take_y(i):
                dve.wait_ge(xb_ready, i + 1)
                dve.wait_ge(stored, 16 * i)
                for j in range(TPB):
                    dve.wait_ge(y_ps_ready, TPB * i + j + 1)
                    nc.vector.scalar_tensor_tensor(out=y[:, j, :], in0=y_ps[j % 3], scalar=0.5,
                                                   in1=xb[:, j, :], op0=ALU.mult, op1=ALU.add)\
                        .then_inc(y_ready, 1)

            def hid_lows(i):
                for m in range(FM):
                    dve.wait_ge(hid_ready, 2 * (FM * i + m + 1))
                    low_part(nc.vector, hid_low[:, m, :], hid[:, m, :], hid_high[:, m, :]).then_inc(low_ready, 1)

            for n, name, w in ((1, "w_up", up_w), (2, "w_down", down_w)):
                dve.wait_ge(w_high, n)
                low_part(nc.vector, w[1][:], g[name][:], w[0][:]).then_inc(w_low, 1)
            ln_vector(nc, dve, 0, x, xn, stat, mv, s)
            ln_low(nc, dve, 0, xT, xT_ps, s)
            with dve.Fori(0, LAST) as i:
                ln_vector(nc, dve, i + 1, x, xn, stat, mv, s)
                hid_lows(i)
                ln_low(nc, dve, i + 1, xT, xT_ps, s)
                take_y(i)
            hid_lows(LAST)
            take_y(LAST)

        @block.scalar
        def _(act):
            def take_xT(i):
                ln_high(nc, act, i, xT, xT_ps, s, h_ps_ready, FM * i)

            def gelu(i):
                act.wait_ge(low_ready, FM * i)
                act.wait_ge(y_ps_ready, TPB * i)
                for m in range(FM):
                    act.wait_ge(h_ps_ready, FM * i + m + 1)
                    for h in (hid_high, hid):
                        nc.scalar.activation(h[:, m, :], h_ps[m % 3][:], ACT.Gelu, bias=g["b_up"][:, m:m + 1],
                                             scale=1.0).then_inc(hid_ready, 1)

            for name, w in (("w_up", up_w), ("w_down", down_w)):
                nc.scalar.copy(w[0][:], g[name][:]).then_inc(w_high, 1)
            take_xT(0)
            with act.Fori(0, LAST) as i:
                gelu(i)
                take_xT(i + 1)
            gelu(LAST)

        @block.tensor
        def _(pe):
            def up(i):
                pe.wait_ge(s["xT_ready"], KD * (i + 1))
                for m in range(FM):
                    pe.wait_ge(hid_ready, 2 * (FM * i + max(m - 2, 0)))
                    for k in range(KD):
                        t = product(nc, h_ps[m % 3][:], [w[:, k, m * P:(m + 1) * P] for w in up_w],
                                    [v[:, k, :] for v in xT], k == 0, k == KD - 1)
                    t.then_inc(h_ps_ready, 1)

            def down(i):
                for j in range(TPB):
                    pe.wait_ge(y_ready, TPB * i + max(j - 2, 0))
                    for m in range(FM):
                        if j == 0:
                            pe.wait_ge(low_ready, FM * i + m + 1)
                        t = product(nc, y_ps[j % 3], [h[:, m, j * P:(j + 1) * P] for h in (hid_high, hid_low)],
                                    [w[:, m, :] for w in down_w], m == 0, m == FM - 1)
                    t.then_inc(y_ps_ready, 1)

            ln_transpose(nc, pe, 0, xn, xT_ps, g["ident"], s)
            pe.wait_ge(w_low, 2)
            with pe.Fori(0, LAST) as i:
                up(i)
                ln_transpose(nc, pe, i + 1, xn, xT_ps, g["ident"], s)
                down(i)
            up(LAST)
            down(LAST)



def inproj_block(nc, g, a, x_in, proj_T):
    with ExitStack() as ctx:
        r = Room(nc, ctx, "inp")
        x, xn, stat, mv, xT_ps, xT, s = ln_room(r)
        s["minus_half"] = g["minus_half"]
        NM = 2 * INNER // P
        w = r.sb("w", [P, KD, 2 * INNER])
        ws = [r.sb(f"w_{part}", [P, KD, 2 * INNER], F32R) for part in ("high", "low")]
        o = [r.sb(f"o{i}", [P, IB, BLK]) for i in range(2)]
        p_ps = [r.ps(f"p_ps{i}", [P, BLK]) for i in range(4)]
        w_in, w_high, w_low, p_ps_ready, o_ready, padded = (
            r.sem(n) for n in ("w_in", "w_high", "w_low", "p_ps_ready", "o_ready", "padded"))
        stored = [r.sem(f"stored{h}") for h in range(2)]
        block = ctx.enter_context(nc.Block())
        LAST = NBLK - 1
        BPB = NBLK // BATCH
        PARTS = [(0, BPB, 0), (BPB, LAST, 1)]

        @block.sync
        def _(sp):
            out3 = proj_T.rearrange("(k p) t -> p k t", p=P)

            def load(i):
                sp.dma_start(x[:], tiles(x_in, i)).then_inc(s["x_loaded"], 16)

            def store(i, b):
                for h in range(2):
                    sp.wait_ge(o_ready, NM * i + (h + 1) * IB)
                    sp.dma_start(out3[:, h * IB:(h + 1) * IB, bass.ds(i * BLK + (b * (TAPS - 1) + 1), BLK)], o[h][:])\
                        .then_inc(stored[h], 16)

            load(0)
            sp.dma_start(w[:], a["in_proj_T"].rearrange("(k p) n -> p k n", p=P)).then_inc(w_in, 16)
            for b in range(BATCH):
                z = g["zeros"][:, 0:IB * 2].rearrange("p (k t) -> p k t", k=IB)
                sp.dma_start(out3[:, 0:IB, b * HPAD:b * HPAD + 1], z[:, :, 0:1],
                             allow_slow_non_contiguous=True).then_inc(padded, 16)
                sp.dma_start(out3[:, 0:IB, b * HPAD + SEQ + 1:(b + 1) * HPAD], z).then_inc(padded, 16)
            for lo, hi, b in PARTS:
                with sp.Fori(lo, hi) as i:
                    sp.wait_ge(s["ln"], LN_OPS * (i + 1))
                    load(i + 1)
                    store(i, b)
            store(LAST, 1)
            sp.wait_ge(padded, 16 * 2 * BATCH)
            sp.wait_ge(stored[0], 16 * NBLK)
            sp.wait_ge(stored[1], 16 * NBLK)

        @block.gpsimd
        def _(pool):
            with pool.Fori(0, NBLK) as i:
                ln_gpsimd(nc, pool, i, mv, s)

        @block.vector
        def _(dve):
            ln_vector(nc, dve, 0, x, xn, stat, mv, s)
            dve.wait_ge(w_high, 1)
            low_part(nc.vector, ws[1][:], w[:], ws[0][:]).then_inc(w_low, 1)
            ln_low(nc, dve, 0, xT, xT_ps, s)
            with dve.Fori(1, NBLK) as i:
                ln_vector(nc, dve, i, x, xn, stat, mv, s)
                ln_low(nc, dve, i, xT, xT_ps, s)

        @block.scalar
        def _(act):
            def take_xT(i):
                ln_high(nc, act, i, xT, xT_ps, s, p_ps_ready, NM * i)

            def take(i):
                for m in range(NM):
                    if m % IB == 0:
                        act.wait_ge(stored[m // IB], 16 * i)
                    act.wait_ge(p_ps_ready, NM * i + m + 1)
                    if m < IB:
                        t = nc.scalar.copy(o[0][:, m, :], p_ps[m % 4][:])
                    else:
                        t = nc.scalar.activation(o[1][:, m - IB, :], p_ps[m % 4][:], ACT.Silu)
                    t.then_inc(o_ready, 1)

            act.wait_ge(w_in, 16)
            nc.scalar.copy(ws[0][:], w[:]).then_inc(w_high, 1)
            take_xT(0)
            with act.Fori(0, LAST) as i:
                take(i)
                take_xT(i + 1)
            take(LAST)

        @block.tensor
        def _(pe):
            def project(i):
                pe.wait_ge(s["xT_ready"], KD * (i + 1))
                for m in range(NM):
                    pe.wait_ge(o_ready, NM * i + max(m - 3, 0))
                    for k in range(KD):
                        t = product(nc, p_ps[m % 4][:], [v[:, k, m * P:(m + 1) * P] for v in ws],
                                    [v[:, k, :] for v in xT], k == 0, k == KD - 1)
                    t.then_inc(p_ps_ready, 1)

            pe.wait_ge(w_low, 1)
            ln_transpose(nc, pe, 0, xn, xT_ps, g["ident"], s)
            with pe.Fori(0, LAST) as i:
                project(i)
                ln_transpose(nc, pe, i + 1, xn, xT_ps, g["ident"], s)
            project(LAST)




def mamba_block(nc, g, a, x_in, proj_T, bc_T, x_out):
    with ExitStack() as ctx:
        r = Room(nc, ctx, "mam")
        QS = 4
        NQ = STATE // QS
        NG = NQ * IB
        conv_w = r.sb("conv_w", [P, IB, TAPS])
        conv_b = r.sb("conv_b", [P, IB])
        diag = r.sb("diag", [P, IB, TAPS, P])
        w_x = r.sb("w_x", [P, IB, XD])
        w_dt = r.sb("w_dt", [RANK, INNER])
        b_dt = r.sb("b_dt", [P, IB])
        ln_w = r.sb("ln_w", [XD, 1])
        skip = r.sb("skip", [P, IB])
        keep = r.sb("keep", [P, NBLK + 1])
        w_out = r.sb("w_out", [P, IB, D])
        hs = r.sb("hs", [P, IB, BLK + TAPS - 1])
        u = [r.sb(f"u{b}", [P, IB, BLK]) for b in range(2)]
        dt = [r.sb(f"dt{b}", [P, IB, BLK]) for b in range(2)]
        dtu = [r.sb(f"dtu{b}", [P, IB, BLK]) for b in range(2)]
        soft = r.sb("soft", [P, IB, BLK])
        gate = r.sb("gate", [P, IB, BLK])
        xd = r.sb("xd", [P, TPB, XD])
        xsq = r.sb("xsq", [P, TPB, XD])
        ms = r.sb("ms", [P, 3, TPB])
        rms = r.sb("rms", [P, 3, TPB])
        xdT = r.sb("xdT", [XD, BLK])
        Bq = [r.sb(f"Bq{b}", [P, QS, BLK]) for b in range(2)]
        Cq = [r.sb(f"Cq{b}", [P, QS, BLK]) for b in range(2)]
        dA = [r.sb(f"dA{b}", [P, QS, BLK]) for b in range(2)]
        dBu = [r.sb(f"dBu{b}", [P, QS, BLK]) for b in range(2)]
        h = [r.sb(f"h{b}", [P, QS, BLK]) for b in range(2)]
        h_last = r.sb("h_last", [P, NG, QS])
        xr = r.sb("xr", [P, TPB, D])
        o = r.sb("o", [P, TPB, D])
        y_ps = [r.ps(f"y_ps{k}", [P, BLK]) for k in range(IB)]
        rot_ps = [r.ps(f"rot_ps{k}", [P, BLK]) for k in range(2)]
        xd_ps = r.ps("xd_ps", [P, TPB, P])
        xT_ps = r.ps("xT_ps", [P, BLK])
        names = ("w_in hs_in gate_in x_loaded conv_ps_ready u_ready xd_ps_ready norm rms_ready xT_ps_ready "
                 "xdT_ready bc_stored dt_ps_ready softened dtu_ready dA_ready dBu_ready scanned kept hC_ready "
                 "y_summed y_ready o_ps_ready o_ready stored diags").split()
        s = {n: r.sem(n) for n in names}
        B_in = [r.sem(f"B_in{b}") for b in range(2)]
        C_in = [r.sem(f"C_in{b}") for b in range(2)]
        block = ctx.enter_context(nc.Block())
        LAST = NBLK - 1
        NORM = 9
        SOFT = 2 * IB + 2
        FIN = 2
        W_IN = 16 * 9
        proj3 = proj_T.rearrange("(k p) t -> p k t", p=P)

        def wait(eng, name, value):
            if not (isinstance(value, int) and value <= 0):
                eng.wait_ge(s[name], value)

        def all_steps(eng, step, end):
            step(0, 0, True, False)
            with eng.Fori(0, (NBLK - 2) // 2) as i:
                step(i * 2 + 1, 1, False, False)
                step(i * 2 + 2, 0, False, False)
            step(LAST, LAST % 2, False, True)
            if end:
                end()

        @block.sync
        def _(sp):
            BPB = NBLK // BATCH

            def load_hs(n, b):
                wait(sp, "conv_ps_ready", IB * n)
                sp.dma_start(hs[:], proj3[:, 0:IB, bass.ds(n * BLK + b * (TAPS - 1), BLK + TAPS - 1)])\
                    .then_inc(s["hs_in"], 16)

            def load_quad(c, quad):
                G = c * NG + (quad - 2) * IB
                b = quad % 2
                rows = bc_T[quad * QS:quad * QS + QS, bass.ds(c * BLK + BLK, BLK)]
                wait(sp, "dBu_ready", G + IB)
                sp.dma_start(Bq[b][:], rows.partition_broadcast(P)).then_inc(B_in[b], 16)
                rows = bc_T[STATE + quad * QS:STATE + quad * QS + QS, bass.ds(c * BLK + BLK, BLK)]
                wait(sp, "hC_ready", G + IB)
                sp.dma_start(Cq[b][:], rows.partition_broadcast(P)).then_inc(C_in[b], 16)

            def store_bc(n):
                sp.wait_ge(s["xdT_ready"], n + 1)
                sp.dma_start(bc_T[:, bass.ds(n * BLK + BLK, BLK)], xdT[RANK:XD, :]).then_inc(s["bc_stored"], 16)

            def store_out(c):
                sp.wait_ge(s["o_ready"], TPB * (c + 1))
                sp.dma_start(tiles(x_out, c), o[:]).then_inc(s["stored"], 16)

            def step(c, q, first, last, b, bn):
                if not last:
                    load_hs(c + 1, bn)
                wait(sp, "y_ready", FIN * IB * c)
                sp.dma_start(gate[:], proj3[:, IB:2 * IB, bass.ds(c * BLK + b * (TAPS - 1) + 1, BLK)])\
                    .then_inc(s["gate_in"], 16)
                load_quad(c, 2)
                if not first:
                    store_out(c - 1)
                wait(sp, "o_ready", TPB * c)
                sp.dma_start(xr[:], tiles(x_in, c)).then_inc(s["x_loaded"], 16)
                load_quad(c, 3)
                if not last:
                    store_bc(c + 1)
                    sp.wait_ge(s["bc_stored"], 16 * (c + 2))
                    load_quad(c + 1, 0)
                    load_quad(c + 1, 1)

            for dst, name in ((conv_w, "conv_w"), (w_x, "x_proj_T"), (w_out, "out_proj_T")):
                sp.dma_start(dst[:], a[name].rearrange("(k p) n -> p k n", p=P)).then_inc(s["w_in"], 16)
            for dst, name in ((conv_b, "conv_b"), (b_dt, "dt_bias"), (skip, "D")):
                sp.dma_start(dst[:], a[name]).then_inc(s["w_in"], 16)
            sp.dma_start(w_dt[:], a["dt_proj_T"]).then_inc(s["w_in"], 16)
            sp.dma_start(ln_w[:], a["xd_ln_w"]).then_inc(s["w_in"], 16)
            sp.dma_start(keep[:], a["keep"]).then_inc(s["w_in"], 16)
            load_hs(0, 0)
            store_bc(0)
            sp.wait_ge(s["bc_stored"], 16)
            load_quad(0, 0)
            load_quad(0, 1)
            step(0, 0, True, False, 0, 0)
            with sp.Fori(1, BPB - 1) as c:
                step(c, 0, False, False, 0, 0)
            step(BPB - 1, 0, False, False, 0, 1)
            with sp.Fori(BPB, LAST) as c:
                step(c, 0, False, False, 1, 1)
            step(LAST, 0, False, True, 1, 1)
            store_out(LAST)
            sp.wait_ge(s["stored"], 16 * NBLK)

        @block.gpsimd
        def _(pool):
            def norms(n):
                pool.wait_ge(s["norm"], NORM * n + 7)
                nc.gpsimd.tensor_tensor(rms[:].rearrange("p g j -> p (g j)"), ms[:].rearrange("p g j -> p (g j)"),
                                        g["minus_half"][:, 0:3 * TPB], ALU.pow).then_inc(s["rms_ready"], 1)

            def make_dt(n, p):
                pool.wait_ge(s["softened"], SOFT * (n + 1))
                nc.gpsimd.tensor_tensor(dt[p][:], dt[p][:], soft[:], ALU.add).then_inc(s["dtu_ready"], 1)
                wait(pool, "dBu_ready", NG * (n - 1))
                pool.wait_ge(s["dtu_ready"], 2 * n + 1)
                nc.gpsimd.tensor_tensor(dtu[p][:], dt[p][:], u[p][:], ALU.mult).then_inc(s["dtu_ready"], 1)

            def step(c, q, first, last):
                for gi in range(NG):
                    k, quad, G = gi % IB, gi // IB, c * NG + gi
                    if gi % IB == 0:
                        pool.wait_ge(B_in[quad % 2], 16 * (2 * c + quad // 2 + 1))
                    if gi == 0:
                        pool.wait_ge(s["dtu_ready"], 2 * (c + 1))
                    wait(pool, "scanned", QS * (G - 1))
                    nc.gpsimd.tensor_tensor(dBu[gi % 2][:], Bq[quad % 2][:],
                                            dtu[q][:, k:k + 1, :].to_broadcast([P, QS, BLK]), ALU.mult)\
                        .then_inc(s["dBu_ready"], 1)
                    if gi == 7 and not last:
                        norms(c + 1)
                    if gi == 13 and not last:
                        make_dt(c + 1, 1 - q)

            norms(0)
            make_dt(0, 0)
            all_steps(pool, step, None)

        @block.scalar
        def _(act):
            def make_u(n, p):
                wait(act, "o_ps_ready", TPB * (n - 1))
                for k in range(IB):
                    act.wait_ge(s["conv_ps_ready"], IB * n + k + 1)
                    nc.scalar.activation(u[p][:, k, :], rot_ps[k % 2][:], ACT.Silu, bias=conv_b[:, k:k + 1],
                                         scale=1.0).then_inc(s["u_ready"], 1)

            def take_xdT(n):
                act.wait_ge(s["xT_ps_ready"], n + 1)
                wait(act, "dt_ps_ready", IB * n)
                wait(act, "bc_stored", 16 * n)
                nc.scalar.activation(xdT[:], xT_ps[0:XD, :], ACT.Copy, scale=ln_w[:, 0:1]).then_inc(s["xdT_ready"], 1)

            def softplus(n, p):
                wait(act, "dtu_ready", 2 * n)
                for k in range(IB):
                    act.wait_ge(s["dt_ps_ready"], IB * n + k + 1)
                    nc.scalar.activation(soft[:, k, :], rot_ps[k % 2][:], ACT.Abs, bias=b_dt[:, k:k + 1], scale=1.0)\
                        .then_inc(s["softened"], 1)
                    nc.scalar.activation(dt[p][:, k, :], rot_ps[k % 2][:], ACT.Relu, bias=b_dt[:, k:k + 1], scale=1.0)\
                        .then_inc(s["softened"], 1)
                act.wait_ge(s["softened"], SOFT * n + 2 * IB)
                nc.scalar.activation(soft[:], soft[:], ACT.Exp, scale=-1.0).then_inc(s["softened"], 1)
                act.wait_ge(s["softened"], SOFT * n + 2 * IB + 1)
                nc.scalar.activation(soft[:], soft[:], ACT.Ln, bias=1.0).then_inc(s["softened"], 1)

            def step(c, q, first, last):
                for gi in range(NG):
                    k, quad, G = gi % IB, gi // IB, c * NG + gi
                    if gi == 0:
                        act.wait_ge(s["dtu_ready"], 2 * (c + 1))
                    wait(act, "scanned", QS * (G - 1))
                    for m in range(QS):
                        n = quad * QS + m
                        nc.scalar.activation(dA[gi % 2][:, m, :], dt[q][:, k, :], ACT.Exp,
                                             scale=g["neg_A"][:, k, n:n + 1]).then_inc(s["dA_ready"], 1)
                    if gi == 3 and not last:
                        make_u(c + 1, 1 - q)
                    if gi == 9 and not last:
                        take_xdT(c + 1)
                    if gi == 11 and not last:
                        softplus(c + 1, 1 - q)

            act.wait_ge(s["w_in"], W_IN)
            make_u(0, 0)
            take_xdT(0)
            softplus(0, 0)
            all_steps(act, step, None)

        @block.vector
        def _(dve):
            def norms(n):
                dve.wait_ge(s["xd_ps_ready"], n + 1)
                wait(dve, "xT_ps_ready", n)
                nc.vector.tensor_copy(xd[:], xd_ps[:, :, 0:XD]).then_inc(s["norm"], 1)
                dve.wait_ge(s["norm"], NORM * n + 1)
                nc.vector.tensor_tensor(xsq[:], xd[:], xd[:], ALU.mult).then_inc(s["norm"], 1)
                dve.wait_ge(s["norm"], NORM * n + 2)
                for i, (lo, hi) in enumerate(((0, RANK), (RANK, RANK + STATE), (RANK + STATE, XD))):
                    nc.vector.tensor_reduce(ms[:, i, :], xsq[:, :, lo:hi], AX.X, ALU.add).then_inc(s["norm"], 1)
                dve.wait_ge(s["norm"], NORM * n + 5)
                nc.vector.tensor_scalar(ms[:, 0, :], ms[:, 0, :], 1.0 / RANK, RMS_EPS, ALU.mult, ALU.add)\
                    .then_inc(s["norm"], 1)
                nc.vector.tensor_scalar(ms[:, 1:3, :], ms[:, 1:3, :], 1.0 / STATE, RMS_EPS, ALU.mult, ALU.add)\
                    .then_inc(s["norm"], 1)

            def scale(n):
                dve.wait_ge(s["rms_ready"], n + 1)
                nc.vector.tensor_tensor(xd[:, :, 0:RANK], xd[:, :, 0:RANK],
                                        rms[:, 0, :].unsqueeze(2).to_broadcast([P, TPB, RANK]), ALU.mult)\
                    .then_inc(s["norm"], 1)
                bc = xd[:, :, RANK:XD].rearrange("p j (g n) -> p j g n", g=2)
                nc.vector.tensor_tensor(bc, bc, rms[:, 1:3, :].rearrange("p g j -> p j g").unsqueeze(3)
                                        .to_broadcast([P, TPB, 2, STATE]), ALU.mult).then_inc(s["norm"], 1)

            def finish(c, q, k):
                dve.wait_ge(s["y_summed"], NG * c + NG - IB + k + 1)
                nc.vector.scalar_tensor_tensor(out=u[q][:, k, :], in0=u[q][:, k, :], scalar=skip[:, k:k + 1],
                                               in1=y_ps[k][:], op0=ALU.mult, op1=ALU.add).then_inc(s["y_ready"], 1)
                dve.wait_ge(s["y_ready"], FIN * (IB * c + k) + 1)
                dve.wait_ge(s["gate_in"], 16 * (c + 1))
                nc.vector.tensor_tensor(u[q][:, k, :], u[q][:, k, :], gate[:, k, :], ALU.mult)\
                    .then_inc(s["y_ready"], 1)

            def take_out(c):
                dve.wait_ge(s["x_loaded"], 16 * (c + 1))
                wait(dve, "stored", 16 * c)
                for j in range(TPB):
                    dve.wait_ge(s["o_ps_ready"], TPB * c + j + 1)
                    nc.vector.tensor_tensor(o[:, j, :], rot_ps[j % 2][:, 0:D], xr[:, j, :], ALU.add)\
                        .then_inc(s["o_ready"], 1)

            def step(c, q, first, last):
                for gi in range(NG):
                    k, quad, G = gi % IB, gi // IB, c * NG + gi
                    hb = h[gi % 2]
                    dve.wait_ge(s["dBu_ready"], G + 1)
                    wait(dve, "y_summed", G - 1)
                    wait(dve, "kept", G)
                    for m in range(QS):
                        dve.wait_ge(s["dA_ready"], QS * G + m + 1)
                        nc.vector.tensor_tensor_scan(hb[:, m, :], dA[gi % 2][:, m, :], dBu[gi % 2][:, m, :],
                                                     h_last[:, gi, m:m + 1], ALU.mult, ALU.add)\
                            .then_inc(s["scanned"], 1)
                    dve.wait_ge(s["scanned"], QS * (G + 1))
                    nc.vector.tensor_tensor(h_last[:, gi, :], hb[:, :, BLK - 1], keep[:, bass.ds(c + 1, 1)]
                                            .to_broadcast([P, QS]), ALU.mult).then_inc(s["kept"], 1)
                    dve.wait_ge(s["kept"], G + 1)
                    dve.wait_ge(C_in[quad % 2], 16 * (2 * c + quad // 2 + 1))
                    nc.vector.tensor_tensor(hb[:], hb[:], Cq[quad % 2][:], ALU.mult).then_inc(s["hC_ready"], 1)
                    if gi == 0 and not first:
                        finish(c - 1, 1 - q, IB - 1)
                    if gi == 3 and not first:
                        take_out(c - 1)
                    if gi == 6 and not last:
                        norms(c + 1)
                    if gi == 8 and not last:
                        scale(c + 1)
                    if gi >= NG - 3:
                        finish(c, q, gi - (NG - 3))

            def end():
                finish(LAST, LAST % 2, IB - 1)
                take_out(LAST)

            dve.wait_ge(s["w_in"], W_IN)
            nc.vector.memset(h_last[:], 0.0).then_inc(s["diags"], 1)
            for k in range(IB):
                for tap in range(TAPS):
                    nc.vector.tensor_scalar(diag[:, k, tap, :], g["ident"][:], conv_w[:, k, tap:tap + 1], None,
                                            ALU.mult).then_inc(s["diags"], 1)
            dve.wait_ge(s["diags"], 1 + IB * TAPS)
            norms(0)
            scale(0)
            all_steps(dve, step, end)

        @block.tensor
        def _(pe):
            def convolve(n):
                pe.wait_ge(s["hs_in"], 16 * (n + 1))
                for k in range(IB):
                    if k >= 2:
                        pe.wait_ge(s["u_ready"], IB * n + k - 1)
                    else:
                        wait(pe, "o_ready", TPB * (n - 1))
                    if k < 2:
                        wait(pe, "softened", SOFT * n)
                    for tap in range(TAPS):
                        t = nc.tensor.matmul(rot_ps[k % 2][:], diag[:, k, tap, :], hs[:, k, tap:tap + BLK],
                                             start=(tap == 0), stop=(tap == TAPS - 1))
                    t.then_inc(s["conv_ps_ready"], 1)

            def project_x(n, p):
                pe.wait_ge(s["u_ready"], IB * (n + 1))
                wait(pe, "norm", NORM * (n - 1) + 1)
                for j in range(TPB):
                    for k in range(IB):
                        t = nc.tensor.matmul(xd_ps[:, j, 0:XD], u[p][:, k, j * P:(j + 1) * P], w_x[:, k, :],
                                             start=(k == 0), stop=(k == IB - 1))
                t.then_inc(s["xd_ps_ready"], 1)

            def turn(n):
                pe.wait_ge(s["norm"], NORM * (n + 1))
                wait(pe, "xdT_ready", n)
                for j in range(TPB):
                    t = nc.tensor.transpose(xT_ps[0:XD, j * P:(j + 1) * P], xd[:, j, :], g["ident"][:])
                t.then_inc(s["xT_ps_ready"], 1)

            def project_dt(n):
                pe.wait_ge(s["xdT_ready"], n + 1)
                for k in range(IB):
                    if k < 2:
                        pe.wait_ge(s["u_ready"], IB * n + k + 3)
                    else:
                        pe.wait_ge(s["softened"], SOFT * n + 2 * (k - 1))
                    nc.tensor.matmul(rot_ps[k % 2][:], w_dt[:, k * P:(k + 1) * P], xdT[0:RANK, :],
                                     start=True, stop=True).then_inc(s["dt_ps_ready"], 1)

            def project_out(c, q, last=False):
                pe.wait_ge(s["y_ready"], FIN * IB * (c + 1))
                for j in range(TPB):
                    if not last and j < 2:
                        pe.wait_ge(s["softened"], SOFT * (c + 2))
                    wait(pe, "o_ready", TPB * c + max(j - 1, 0))
                    for k in range(IB):
                        t = nc.tensor.matmul(rot_ps[j % 2][:, 0:D], u[q][:, k, j * P:(j + 1) * P], w_out[:, k, :],
                                             start=(k == 0), stop=(k == IB - 1))
                    t.then_inc(s["o_ps_ready"], 1)

            def step(c, q, first, last):
                for gi in range(NG):
                    k, quad, G = gi % IB, gi // IB, c * NG + gi
                    pe.wait_ge(s["hC_ready"], G + 1)
                    if quad == 0:
                        wait(pe, "y_ready", FIN * (IB * (c - 1) + k) + 1)
                    for m in range(QS):
                        t = nc.tensor.matmul(y_ps[k][:], g["ident"][:], h[gi % 2][:, m, :],
                                             start=(quad == 0 and m == 0), stop=(quad == NQ - 1 and m == QS - 1))
                    t.then_inc(s["y_summed"], 1)
                    if gi == 1 and not first:
                        project_out(c - 1, 1 - q)
                    if gi == 2 and not last:
                        convolve(c + 1)
                    if gi == 5 and not last:
                        project_x(c + 1, 1 - q)
                    if gi == 8 and not last:
                        turn(c + 1)
                    if gi == 10 and not last:
                        project_dt(c + 1)

            pe.wait_ge(s["diags"], 1 + IB * TAPS)
            convolve(0)
            project_x(0, 0)
            turn(0)
            project_dt(0)
            all_steps(pe, step, lambda: project_out(LAST, LAST % 2, True))



def route_block(nc, tag, g, a, x_in, slots_dram):
    with ExitStack() as ctx:
        r = Room(nc, ctx, tag)
        stat = r.sb("stat", [P, NT, 6])
        mv = r.sb("mv", [P, NT + 1, 2])
        rstd = r.sb("rstd", [P, NT])
        xT = [r.sb(f"xT{b}", [P, KD, BLK]) for b in range(2)]
        w = r.sb("w", [P, KD, NE])
        x = r.sb("x", [P, NT, D])
        logits = r.sb("logits", [P, NT, NE])
        e = r.sb("e", [P, NT, NE])
        t = r.sb("t", [P, NT, NE])
        hot = r.sb("hot", [P, TOPK, NT, NE])
        best = r.sb("best", [P, TOPK, NT])
        m = r.sb("m", [P, NT])
        rank = r.sb("rank", [P, NE])
        first_slot = r.sb("first_slot", [P, NE])
        outside = r.sb("outside", [P, TOPK, NT])
        earlier = r.sb("earlier", [P, P])
        ones = r.sb("ones", [P, P])
        total = r.sb("total", [P, TOPK, NT, NE])
        upto = r.sb("upto", [P, TOPK, NT, NE])
        place = r.sb("place", [P, NT, NE])
        loc = r.sb("loc", [P, NT])
        slot = r.sb("slot", [P, NT])
        fits = r.sb("fits", [P, TOPK, NT])
        put = r.sb("put", [P, TOPK, NT], I32)
        xT_ps = [r.ps(f"xT_ps{k}", [P, BLK]) for k in range(KD)]
        l_ps = [r.ps(f"l_ps{b}", [P, TPB, NE]) for b in range(2)]
        count_ps = [r.ps(f"count_ps{j}", [P, 2, NT, NE]) for j in range(TOPK)]
        before_ps, total_ps = ([c[:, n] for c in count_ps] for n in range(2))
        x_loaded = [r.sem(f"x{i}_loaded") for i in range(NBLK)]
        (w_in, stats, rstds, normed, xT_full, xT_taken, l_full, l_taken, cleared, rt, exped, chosen, counted, placed,
         scattered) = (r.sem(n) for n in ("w_in stats rstds normed xT_full xT_taken l_full l_taken cleared rt "
                                          "exped chosen counted placed scattered").split())
        block = ctx.enter_context(nc.Block())
        W_IN = 16 * 6
        NSTAT = 2 * TPB + 2

        def wait(eng, sem, value):
            if not (isinstance(value, int) and value <= 0):
                eng.wait_ge(sem, value)

        @block.sync
        def _(sp):
            for i in range(2):
                sp.dma_start(x[:, i * TPB:(i + 1) * TPB, :], tiles(x_in, i)).then_inc(x_loaded[i], 16)
            for dst, name in ((rank[:], "rank"), (first_slot[:], "first_slot"),
                              (outside[:].rearrange("p j t -> p (j t)"), "outside"),
                              (earlier[:], "earlier"), (ones[:], "ones")):
                sp.dma_start(dst, a[name]).then_inc(w_in, 16)
            sp.dma_start(w[:], a["gate_T"].rearrange("(k p) e -> p k e", p=P)).then_inc(w_in, 16)
            for i in range(2, NBLK):
                sp.dma_start(x[:, i * TPB:(i + 1) * TPB, :], tiles(x_in, i)).then_inc(x_loaded[i], 16)
            rows = slots_dram.rearrange("(c p q) d -> c p q d", p=P, q=4)
            for c in range(rows.shape[0]):
                sp.dma_start(rows[c], g["zeros"][:].unsqueeze(1).to_broadcast([P, 4, D])).then_inc(cleared, 16)

        @block.gpsimd
        def _(pool):
            for i in range(NBLK):
                pool.wait_ge(stats, NSTAT * (i + 1))
                nc.gpsimd.tensor_tensor(rstd[:, i * TPB:(i + 1) * TPB], mv[:, i * TPB:(i + 1) * TPB, 1],
                                        g["minus_half"][:, 0:TPB], ALU.pow).then_inc(rstds, 1)
            pool.wait_ge(cleared, 16 * (NE * CAP // (4 * P)))
            for j in range(TOPK):
                pool.wait_ge(placed, j + 1)
                for i in range(NT):
                    nc.gpsimd.indirect_dma_start(
                        out=slots_dram, out_offset=bass.IndirectOffsetOnAxis(ap=put[:, j, i:i + 1], axis=0),
                        in_=x[:, i, :], in_offset=None, bounds_check=NE * CAP - 1, oob_is_err=False)\
                        .then_inc(scattered, 16)
            pool.wait_ge(scattered, 16 * TOPK * NT)

        @block.vector
        def _(dve):
            def statistics(i):
                mine = range(i * TPB, (i + 1) * TPB)
                dve.wait_ge(x_loaded[i], 16)
                for j in mine:
                    nc.vector.bn_stats(stat[:, j, :], x[:, j, :]).then_inc(stats, 1)
                dve.wait_ge(stats, NSTAT * i + TPB)
                nc.vector.tensor_copy(mv[:, NT, :], stat[:, i * TPB, 0:2]).then_inc(stats, 1)
                for j in mine:
                    nc.vector.bn_aggr(mv[:, j, :], stat[:, j, :]).then_inc(stats, 1)
                dve.wait_ge(stats, NSTAT * i + 2 * TPB + 1)
                var = mv[:, i * TPB:(i + 1) * TPB, 1]
                nc.vector.tensor_scalar(var, var, LN_EPS, None, ALU.add).then_inc(stats, 1)

            def normalise(i):
                dve.wait_ge(rstds, i + 1)
                for j in range(i * TPB, (i + 1) * TPB):
                    ins = nc.vector.tensor_scalar(x[:, j, :], x[:, j, :], mv[:, j, 0:1], rstd[:, j:j + 1],
                                                  ALU.subtract, ALU.mult)
                ins.then_inc(normed, 1)

            def take_logits(i):
                dve.wait_ge(l_full, i + 1)
                nc.vector.tensor_copy(logits[:, i * TPB:(i + 1) * TPB, :], l_ps[i % 2][:]).then_inc(l_taken, 1)

            statistics(0)
            for i in range(NBLK):
                if i + 1 < NBLK:
                    statistics(i + 1)
                normalise(i)
                if i >= 2:
                    take_logits(i - 2)
            take_logits(NBLK - 2)
            take_logits(NBLK - 1)

            n = [0]

            def done(ins):
                ins.then_inc(rt, 1)
                n[0] += 1
                dve.wait_ge(rt, n[0])

            def over(v, k):
                return v.unsqueeze(2).to_broadcast([P, k, NE])

            def choose(j):
                done(nc.vector.tensor_reduce(best[:, j, :], e[:], AX.X, ALU.max))
                done(nc.vector.tensor_tensor(t[:], e[:], over(best[:, j, :], NT), ALU.is_equal))
                done(nc.vector.tensor_tensor(t[:], t[:], rank[:].unsqueeze(1).to_broadcast([P, NT, NE]), ALU.mult))
                done(nc.vector.tensor_reduce(m[:], t[:], AX.X, ALU.max))
                done(nc.vector.tensor_tensor(hot[:, j], t[:], over(m[:], NT), ALU.is_equal))
                nc.vector.sem_inc(chosen, 1)

            def place_all(j):
                dve.wait_ge(counted, 2 * (j + 1))
                done(nc.vector.tensor_copy(total[:, j], total_ps[j]))
                for ex in range(NE):
                    start = upto[:, 0, NT - 1, ex:ex + 1] if j else 0.0
                    ins = nc.vector.tensor_tensor_scan(upto[:, j, :, ex], ones[:, 0:NT], total[:, j, :, ex], start,
                                                       ALU.mult, ALU.add)
                    if ex == NE - 1:
                        done(ins)
                done(nc.vector.tensor_tensor(place[:], upto[:, j], total[:, j], ALU.subtract))
                done(nc.vector.tensor_tensor(place[:], place[:], before_ps[j], ALU.add))
                done(nc.vector.tensor_tensor(place[:], place[:], hot[:, j], ALU.mult))
                done(nc.vector.tensor_reduce(loc[:], place[:], AX.X, ALU.add))
                done(nc.vector.tensor_tensor(place[:], hot[:, j], first_slot[:].unsqueeze(1)
                                             .to_broadcast([P, NT, NE]), ALU.mult))
                done(nc.vector.tensor_reduce(slot[:], place[:], AX.X, ALU.add))
                done(nc.vector.tensor_tensor(slot[:], slot[:], loc[:], ALU.add))
                done(nc.vector.tensor_scalar(fits[:, j], loc[:], float(CAP), None, ALU.is_lt))
                done(nc.vector.tensor_tensor(slot[:], slot[:], fits[:, j], ALU.mult))
                done(nc.vector.tensor_copy(g["take"][:, j * NT:(j + 1) * NT], slot[:]))
                done(nc.vector.tensor_scalar(loc[:], fits[:, j], -1.0, 1.0, ALU.mult, ALU.add))
                done(nc.vector.tensor_tensor(loc[:], loc[:], outside[:, j], ALU.mult))
                done(nc.vector.tensor_tensor(loc[:], loc[:], slot[:], ALU.add))
                nc.vector.tensor_copy(put[:, j], loc[:]).then_inc(placed, 1)

            dve.wait_ge(l_taken, NBLK)
            dve.wait_ge(w_in, W_IN)
            done(nc.vector.tensor_reduce(m[:], logits[:], AX.X, ALU.max))
            done(nc.vector.tensor_tensor(e[:], logits[:], over(m[:], NT), ALU.subtract))
            dve.wait_ge(exped, 1)
            done(nc.vector.tensor_reduce(m[:], e[:], AX.X, ALU.add))
            done(nc.vector.reciprocal(m[:], m[:]))
            done(nc.vector.tensor_tensor(e[:], e[:], over(m[:], NT), ALU.mult))
            choose(0)
            done(nc.vector.scalar_tensor_tensor(out=e[:], in0=hot[:, 0], scalar=-2.0, in1=e[:],
                                                op0=ALU.mult, op1=ALU.add))
            place_all(0)
            choose(1)
            done(nc.vector.tensor_tensor(m[:], best[:, 0, :], best[:, 1, :], ALU.add))
            done(nc.vector.reciprocal(m[:], m[:]))
            dve.wait_ge(placed, 1)
            place_all(1)
            share = g["share"][:].rearrange("p (j t) -> p j t", j=TOPK)
            done(nc.vector.tensor_tensor(share, best[:], m[:].unsqueeze(1).to_broadcast([P, TOPK, NT]), ALU.mult))
            done(nc.vector.scalar_tensor_tensor(out=share, in0=share, scalar=0.5, in1=fits[:],
                                                op0=ALU.mult, op1=ALU.mult))

        @block.scalar
        def _(act):
            for i in range(NBLK):
                wait(act, l_full, i - 1)
                for k in range(KD):
                    act.wait_ge(xT_full, KD * i + k + 1)
                    nc.scalar.copy(xT[i % 2][:, k, :], xT_ps[k][:]).then_inc(xT_taken, 1)
            act.wait_ge(rt, 2)
            nc.scalar.activation(e[:], e[:], ACT.Exp).then_inc(exped, 1)

        @block.tensor
        def _(pe):
            def turn(i):
                pe.wait_ge(normed, i + 1)
                wait(pe, xT_taken, KD * i)
                for k in range(KD):
                    for j in range(TPB):
                        ins = nc.tensor.transpose(xT_ps[k][:, j * P:(j + 1) * P],
                                                  x[:, i * TPB + j, k * P:(k + 1) * P], g["ident"][:])
                    ins.then_inc(xT_full, 1)

            def gate(i):
                pe.wait_ge(xT_taken, KD * (i + 1))
                wait(pe, l_taken, i - 1)
                for j in range(TPB):
                    for k in range(KD):
                        ins = nc.tensor.matmul(l_ps[i % 2][:, j, :], xT[i % 2][:, k, j * P:(j + 1) * P], w[:, k, :],
                                               start=(k == 0), stop=(k == KD - 1))
                ins.then_inc(l_full, 1)

            pe.wait_ge(w_in, W_IN)
            turn(0)
            for i in range(NBLK):
                if i + 1 < NBLK:
                    turn(i + 1)
                gate(i)
            for j in range(TOPK):
                pe.wait_ge(chosen, j + 1)
                nc.tensor.matmul(before_ps[j], earlier[:], hot[:, j], start=True, stop=True).then_inc(counted, 1)
                nc.tensor.matmul(total_ps[j], ones[:], hot[:, j], start=True, stop=True).then_inc(counted, 1)


def expert_block(nc, tag, g, a, slots_dram, done_dram):
    with ExitStack() as ctx:
        r = Room(nc, ctx, tag)
        w1 = r.sb("w1", [P, KD, EH])
        w2 = r.sb("w2", [P, EM, D])
        parts = ("high", "low")
        w1s = [[r.sb(f"w1_{n}{b}", [P, KD, EH], F32R) for n in parts] for b in range(2)]
        w2s = [[r.sb(f"w2_{n}{b}", [P, EM, D], F32R) for n in parts] for b in range(2)]
        b1 = r.sb("b1", [P, EM])
        b2 = r.sb("b2", [P, D])
        x = r.sb("x", [P, TPB, D])
        xT = [r.sb(f"xT_{n}", [P, KD, HALF], F32R) for n in parts]
        hid = r.sb("hid", [P, EM, HALF])
        hid_high, hid_low = (r.sb(f"hid_{n}", [P, EM, HALF], F32R) for n in parts)
        y = r.sb("y", [P, TPB, D])
        xT_ps = [r.ps(f"xT_ps{k}", [P, HALF]) for k in range(KD)]
        h_ps = [r.ps(f"h_ps{i}", [P, HALF]) for i in range(3)]
        y_ps = [r.ps(f"y_ps{i}", [P, BLK])[:, 0:D] for i in range(3)]
        names = ("w1_in w2_in b1_in b2_in w1_high w1_split w2_high w2_split x_in xT_ps_ready xT_high xT_ready "
                 "h_ps_ready hid_ready low_ready y_ps_ready y_ready stored").split()
        s = {n: r.sem(n) for n in names}
        block = ctx.enter_context(nc.Block())
        STEPS = NE * HPE

        def on(eng, name, value):
            if not (isinstance(value, int) and value <= 0):
                eng.wait_ge(s[name], value)

        @block.sync
        def _(sp):
            w1_v = a["fc1_T"].rearrange("(k p) n -> p k n", p=P)
            w2_v = a["fc2"].rearrange("(m p) d -> p m d", p=P)

            def load_w1(e):
                on(sp, "w1_split", e)
                sp.dma_start(w1[:], w1_v[:, :, bass.ds(e * EH, EH)]).then_inc(s["w1_in"], 16)

            def load_w2(e):
                on(sp, "w2_split", e)
                sp.dma_start(w2[:], w2_v[:, bass.ds(e * EM, EM), :]).then_inc(s["w2_in"], 16)

            def load_b1(e):
                on(sp, "hid_ready", 2 * EM * HPE * e)
                sp.dma_start(b1[:], a["b1"][bass.ds(e * P, P), :]).then_inc(s["b1_in"], 16)

            def load_b2(e):
                on(sp, "y_ready", TPB * HPE * e)
                sp.dma_start(b2[:], a["b2"][bass.ds(e * D, D)].partition_broadcast(P)).then_inc(s["b2_in"], 16)

            def load_x(i):
                on(sp, "xT_ps_ready", KD * i)
                sp.dma_start(x[:], tiles(slots_dram, i)).then_inc(s["x_in"], 16)

            def store(i):
                sp.wait_ge(s["y_ready"], TPB * (i + 1))
                sp.dma_start(tiles(done_dram, i), y[:]).then_inc(s["stored"], 16)

            load_x(0)
            load_w1(0)
            load_b1(0)
            load_w2(0)
            load_b2(0)
            with sp.Fori(0, NE - 1) as e:
                load_x(e * HPE + 1)
                load_w1(e + 1)
                load_w2(e + 1)
                store(e * HPE)
                load_x(e * HPE + 2)
                load_b1(e + 1)
                store(e * HPE + 1)
                load_b2(e + 1)
            load_x(STEPS - 1)
            store(STEPS - 2)
            store(STEPS - 1)
            sp.wait_ge(s["stored"], 16 * STEPS)

        @block.gpsimd
        def _(pool):
            def split(e, p, n, raw, halves, used, per):
                pool.wait_ge(s[f"{n}_in"], 16 * (e + 1))
                on(pool, used, per * (e - 1))
                flat = "p a b -> p (a b)"
                high, low, raw = (t[:].rearrange(flat) for t in (*halves[p], raw))
                nc.gpsimd.tensor_tensor(high, raw, g["zeros"][:, 0:1].to_broadcast(list(raw.shape)), ALU.add)\
                    .then_inc(s[f"{n}_high"], 1)
                pool.wait_ge(s[f"{n}_high"], e + 1)
                low_part(nc.gpsimd, low, raw, high).then_inc(s[f"{n}_split"], 1)

            def expert(e, p):
                split(e, p, "w1", w1, w1s, "h_ps_ready", EM * HPE)
                split(e, p, "w2", w2, w2s, "y_ps_ready", TPB * HPE)

            expert(0, 0)
            with pool.Fori(0, NE // 2 - 1) as j:
                expert(j * 2 + 1, 1)
                expert(j * 2 + 2, 0)
            expert(NE - 1, 1)

        @block.tensor
        def _(pe):
            def turn(i):
                pe.wait_ge(s["x_in"], 16 * (i + 1))
                on(pe, "xT_ready", KD * i)
                for k in range(KD):
                    for j in range(TPB):
                        t = nc.tensor.transpose(xT_ps[k][:, j * P:(j + 1) * P], x[:, j, k * P:(k + 1) * P],
                                                g["ident"][:])
                    t.then_inc(s["xT_ps_ready"], 1)

            def up(i, e, p):
                pe.wait_ge(s["xT_ready"], KD * (i + 1))
                pe.wait_ge(s["w1_split"], e + 1)
                for m in range(EM):
                    on(pe, "hid_ready", 2 * (EM * i + max(m - 2, 0)))
                    for k in range(KD):
                        t = product(nc, h_ps[m % 3][:], [w[:, k, m * P:(m + 1) * P] for w in w1s[p]],
                                    [v[:, k, :] for v in xT], k == 0, k == KD - 1)
                    t.then_inc(s["h_ps_ready"], 1)

            def down(i, e, p):
                pe.wait_ge(s["w2_split"], e + 1)
                for j in range(TPB):
                    on(pe, "y_ready", TPB * i + max(j - 2, 0))
                    for m in range(EM):
                        if j == 0:
                            pe.wait_ge(s["low_ready"], EM * i + m + 1)
                        t = product(nc, y_ps[j % 3], [h[:, m, j * P:(j + 1) * P] for h in (hid_high, hid_low)],
                                    [w[:, m, :] for w in w2s[p]], m == 0, m == EM - 1)
                    t.then_inc(s["y_ps_ready"], 1)

            def expert(e, p, last=False):
                up(e * HPE, e, p)
                turn(e * HPE + 1)
                down(e * HPE, e, p)
                up(e * HPE + 1, e, p)
                if not last:
                    turn(e * HPE + 2)
                down(e * HPE + 1, e, p)

            turn(0)
            expert(0, 0)
            with pe.Fori(0, NE // 2 - 1) as j:
                expert(j * 2 + 1, 1)
                expert(j * 2 + 2, 0)
            expert(NE - 1, 1, True)

        @block.scalar
        def _(act):
            def high_xT(i):
                for k in range(KD):
                    act.wait_ge(s["xT_ps_ready"], KD * i + k + 1)
                    on(act, "h_ps_ready", EM * i)
                    nc.scalar.copy(xT[0][:, k, :], xT_ps[k][:]).then_inc(s["xT_high"], 1)

            def relu(i, e):
                on(act, "low_ready", EM * i)
                on(act, "y_ps_ready", TPB * i)
                act.wait_ge(s["b1_in"], 16 * (e + 1))
                for m in range(EM):
                    act.wait_ge(s["h_ps_ready"], EM * i + m + 1)
                    for h in (hid_high, hid):
                        nc.scalar.activation(h[:, m, :], h_ps[m % 3][:], ACT.Relu, bias=b1[:, m:m + 1], scale=1.0)\
                            .then_inc(s["hid_ready"], 1)

            def expert(e, last=False):
                relu(e * HPE, e)
                high_xT(e * HPE + 1)
                relu(e * HPE + 1, e)
                if not last:
                    high_xT(e * HPE + 2)

            high_xT(0)
            with act.Fori(0, NE - 1) as e:
                expert(e)
            expert(NE - 1, True)

        @block.vector
        def _(dve):
            def low_xT(i):
                for k in range(KD):
                    dve.wait_ge(s["xT_high"], KD * i + k + 1)
                    low_part(nc.vector, xT[1][:, k, :], xT_ps[k][:], xT[0][:, k, :]).then_inc(s["xT_ready"], 1)

            def low_hid(i):
                for m in range(EM):
                    dve.wait_ge(s["hid_ready"], 2 * (EM * i + m + 1))
                    low_part(nc.vector, hid_low[:, m, :], hid[:, m, :], hid_high[:, m, :]).then_inc(s["low_ready"], 1)

            def take_y(i, e):
                dve.wait_ge(s["b2_in"], 16 * (e + 1))
                on(dve, "stored", 16 * i)
                for j in range(TPB):
                    dve.wait_ge(s["y_ps_ready"], TPB * i + j + 1)
                    nc.vector.tensor_tensor(y[:, j, :], y_ps[j % 3], b2[:], ALU.add).then_inc(s["y_ready"], 1)

            def expert(e, last):
                low_hid(e * HPE)
                low_xT(e * HPE + 1)
                take_y(e * HPE, e)
                low_hid(e * HPE + 1)
                if not last:
                    low_xT(e * HPE + 2)
                take_y(e * HPE + 1, e)

            low_xT(0)
            with dve.Fori(0, NE - 1) as e:
                expert(e, False)
            expert(NE - 1, True)


def combine_block(nc, tag, g, x_in, done_dram, x_out):
    with ExitStack() as ctx:
        r = Room(nc, ctx, tag)
        NB = 4
        x = [r.sb(f"x{b}", [P, TPB, D]) for b in range(2)]
        got = [[r.sb(f"got{j}_{b}", [P, D]) for b in range(NB)] for j in range(TOPK)]
        x_loaded = [r.sem(f"x_loaded{b}") for b in range(2)]
        stored = [r.sem(f"stored{b}") for b in range(2)]
        fetched = [r.sem(f"fetched{b}") for b in range(NB)]
        added = r.sem("added")
        block = ctx.enter_context(nc.Block())

        @block.sync
        def _(sp):
            def load(i):
                if i >= 2:
                    sp.wait_ge(stored[i % 2], 16 * (i // 2))
                sp.dma_start(x[i % 2][:], tiles(x_in, i)).then_inc(x_loaded[i % 2], 16)

            load(0)
            load(1)
            for i in range(NBLK):
                sp.wait_ge(added, 2 * TPB * (i + 1))
                sp.dma_start(tiles(x_out, i), x[i % 2][:]).then_inc(stored[i % 2], 16)
                if i + 2 < NBLK:
                    load(i + 2)
            for b in range(2):
                sp.wait_ge(stored[b], 16 * (NBLK // 2))

        @block.gpsimd
        def _(pool):
            for i in range(NT):
                if i >= NB:
                    pool.wait_ge(added, 2 * (i - NB + 1))
                for j in range(TOPK):
                    c = j * NT + i
                    nc.gpsimd.indirect_dma_start(
                        out=got[j][i % NB][:], out_offset=None, in_=done_dram,
                        in_offset=bass.IndirectOffsetOnAxis(ap=g["take"][:, c:c + 1], axis=0),
                        bounds_check=NE * CAP - 1, oob_is_err=True).then_inc(fetched[i % NB], 16)

        @block.vector
        def _(dve):
            for i in range(NT):
                b, t = i // TPB % 2, i % TPB
                dve.wait_ge(x_loaded[b], 16 * (i // TPB // 2 + 1))
                dve.wait_ge(fetched[i % NB], 32 * (i // NB + 1))
                for j in range(TOPK):
                    c = j * NT + i
                    if j:
                        dve.wait_ge(added, 2 * i + 1)
                    nc.vector.scalar_tensor_tensor(out=x[b][:, t, :], in0=got[j][i % NB][:],
                                                   scalar=g["share"][:, c:c + 1], in1=x[b][:, t, :],
                                                   op0=ALU.mult, op1=ALU.add).then_inc(added, 1)



SPAD = SEQ + P
GH = 4
NGR = HEADS // GH


def qkv_block(nc, g, a, qkv, x_in):
    with ExitStack() as ctx:
        r = Room(nc, ctx, "qkv")
        x, xn, stat, mv, xT_ps, xT, s = ln_room(r)
        s["minus_half"] = g["minus_half"]
        w = {n: r.sb(n, [P, KD, D]) for n in ("wq_T", "wk_T", "wv_T")}
        ws = {n: [r.sb(f"{n}_{part}", [P, KD, D], F32R) for part in ("high", "low")] for n in w}
        qk_ps = [r.ps(f"qk_ps{i}", [P, BLK]) for i in range(2 * KD)]
        v_ps = [r.ps(f"v_ps{i}", [P, 2, D]) for i in range(TPB // 2)]
        w_in, w_high, w_low, qk_full, qk_taken, v_full, v_taken, padded = (
            r.sem(n) for n in ("w_in", "w_high", "w_low", "qk_full", "qk_taken", "v_full", "v_taken", "padded"))
        block = ctx.enter_context(nc.Block())
        LAST = NBLK - 1
        BPB = NBLK // BATCH
        PARTS = [(0, BPB, 0), (BPB, LAST, 1)]
        NV = TPB // 2

        @block.sync
        def _(sp):
            sp.dma_start(x[:], tiles(x_in, 0)).then_inc(s["x_loaded"], 16)
            for name, t in w.items():
                sp.dma_start(t[:], a[name].rearrange("(k p) n -> p k n", p=P)).then_inc(w_in, 16)
            with sp.Fori(0, LAST) as i:
                sp.wait_ge(s["ln"], LN_OPS * (i + 1))
                sp.dma_start(x[:], tiles(x_in, i + 1)).then_inc(s["x_loaded"], 16)

        @block.gpsimd
        def _(pool):
            for b in range(BATCH):
                nc.gpsimd.memset(qkv["kT"][:, :, b * SPAD:b * SPAD + P], 0.0).then_inc(padded, 1)
                nc.gpsimd.memset(qkv["v"][:, b * (QT + 1), :], 0.0).then_inc(padded, 1)
            with pool.Fori(0, NBLK) as i:
                ln_gpsimd(nc, pool, i, mv, s)
            pool.wait_ge(padded, 2 * BATCH)

        @block.vector
        def _(dve):
            def take_v(i, b):
                for m in range(NV):
                    dve.wait_ge(v_full, NV * i + m + 1)
                    nc.vector.tensor_copy(qkv["v"][:, bass.ds(i * TPB + (b + 1 + 2 * m), 2), :], v_ps[m][:])\
                        .then_inc(v_taken, 1)

            ln_vector(nc, dve, 0, x, xn, stat, mv, s)
            dve.wait_ge(w_high, 3)
            for name, t in w.items():
                low_part(nc.vector, ws[name][1][:], t[:], ws[name][0][:]).then_inc(w_low, 1)
            ln_low(nc, dve, 0, xT, xT_ps, s)
            for lo, hi, b in PARTS:
                with dve.Fori(lo, hi) as i:
                    ln_vector(nc, dve, i + 1, x, xn, stat, mv, s)
                    take_v(i, b)
                    ln_low(nc, dve, i + 1, xT, xT_ps, s)
            take_v(LAST, 1)

        @block.scalar
        def _(act):
            def take_xT(i):
                ln_high(nc, act, i, xT, xT_ps, s, v_full, NV * i)

            def take_qk(i, b):
                for m in range(2 * KD):
                    act.wait_ge(qk_full, 2 * KD * i + m + 1)
                    name, pad = ("qT", 0) if m < KD else ("kT", (b + 1) * P)
                    nc.scalar.copy(qkv[name][:, m % KD, bass.ds(i * BLK + pad, BLK)], qk_ps[m][:])\
                        .then_inc(qk_taken, 1)

            act.wait_ge(w_in, 16 * 3)
            for name, t in w.items():
                nc.scalar.copy(ws[name][0][:], t[:]).then_inc(w_high, 1)
            take_xT(0)
            for lo, hi, b in PARTS:
                with act.Fori(lo, hi) as i:
                    take_qk(i, b)
                    take_xT(i + 1)
            take_qk(LAST, 1)

        @block.tensor
        def _(pe):
            def project(i, first):
                pe.wait_ge(s["xT_ready"], KD * (i + 1))
                for m in range(2 * KD):
                    if not first:
                        pe.wait_ge(qk_taken, 2 * KD * (i - 1) + m + 1)
                    name, f = ("wq_T", "wk_T")[m // KD], m % KD
                    for k in range(KD):
                        t = product(nc, qk_ps[m][:], [v[:, k, f * P:(f + 1) * P] for v in ws[name]],
                                    [v[:, k, :] for v in xT], k == 0, k == KD - 1)
                    t.then_inc(qk_full, 1)
                for m in range(NV):
                    if not first:
                        pe.wait_ge(v_taken, NV * (i - 1) + m + 1)
                    for j in range(2):
                        c = 2 * m + j
                        for k in range(KD):
                            t = product(nc, v_ps[m][:, j, :], [v[:, k, c * P:(c + 1) * P] for v in xT],
                                        [v[:, k, :] for v in ws["wv_T"]], k == 0, k == KD - 1)
                    t.then_inc(v_full, 1)

            pe.wait_ge(w_low, 3)
            ln_transpose(nc, pe, 0, xn, xT_ps, g["ident"], s)
            project(0, True)
            with pe.Fori(1, NBLK) as i:
                ln_transpose(nc, pe, i, xn, xT_ps, g["ident"], s)
                project(i, False)


def attend_block(nc, g, a, qkv, x_in, x_out):
    with ExitStack() as ctx:
        r = Room(nc, ctx, "att")
        W2 = 2 * P
        wo_T = r.sb("wo_T", [P, KD, D])
        hmask = r.sb("hmask", [P, HPB])
        vmask = r.sb("vmask", [P, GH * HD])
        identb = r.sb("identb", [P, P], BF16)
        wmask = r.sb("wmask", [P, 2, 2 * W2], BF16)
        smask = r.sb("smask", [P, QT * NSTR], BF16)
        ones = r.sb("ones", [P, P], BF16)
        xr = r.sb("xr", [P, D])
        q = [r.sb(f"q{b}", [P, KD, P]) for b in range(2)]
        qm = [r.sb(f"qm{b}", [P, HEADS, P]) for b in range(2)]
        Ks = [r.sb(f"Ks{b}", [P, KD, HPB, NSTR]) for b in range(BATCH)]
        vrows = [r.sb(f"vrows{b}", [P, NGR, GH * HD]) for b in range(BATCH)]
        Vs = [r.sb(f"Vs{b}", [P, NGR, GH * HD]) for b in range(BATCH)]
        top_s = r.sb("top_s", [P, HEADS])
        top_w = r.sb("top_w", [P, HEADS])
        shift_s = r.sb("shift_s", [P, HEADS])
        shift = r.sb("shift", [P, HEADS])
        den = [r.sb(f"den{b}", [P, HEADS]) for b in range(2)]
        den_s = r.sb("den_s", [P, HEADS])
        rden = r.sb("rden", [P, HEADS])
        probs = [r.sb(f"probs{b}", [P, GH, W2]) for b in range(2)]
        str_in = r.sb("str_in", [P, HEADS * NSTR])
        probs_s = r.sb("probs_s", [P, HEADS * NSTR])
        PT = [r.sb(f"PT{b}", [P, 2, GH, P]) for b in range(2)]
        PTs = r.sb("PTs", [P, NGR, P])
        on = r.sb("on", [P, D])
        OT = r.sb("OT", [P, KD, P])
        o = r.sb("o", [P, D])
        S_ps = [r.ps(f"S_ps{b}", [P, GH, W2]) for b in range(2)]
        Ss_ps = r.ps("Ss_ps", [P, BLK])
        T_ps = [r.ps(f"T_ps{b}", [P, BLK]) for b in range(2)]
        O_ps = r.ps("O_ps", [P, BLK])
        names = ("w_in vrows_in Ks_ready Vs_ready q_ready qm_ready Ss_ready S_ready top_s_ready shift_s_ready "
                 "tops shifts exp_done str_shifted str_exp str_turned PTs_taken turned0 turned1 PT0_taken "
                 "PT1_taken PV_done O_ready sums dens on_ready O_turned OT_taken out_ready o_ready xr_in "
                 "stored").split()
        s = {n: r.sem(n) for n in names}
        block = ctx.enter_context(nc.Block())
        LAST = NT - 1
        N_IN = 7

        def wait(eng, name, value):
            if not (isinstance(value, int) and value <= 0):
                eng.wait_ge(s[name], value)

        def all_tiles(eng, tile):
            for b in range(BATCH):
                tile(b * QT, 0, b)
                with eng.Fori(0, QT // 2 - 1) as i:
                    tile(i * 2 + (b * QT + 1), 1, b)
                    tile(i * 2 + (b * QT + 2), 0, b)
                tile(b * QT + QT - 1, 1, b)

        def is_first(t):
            return isinstance(t, int) and t == 0

        def is_last(t):
            return isinstance(t, int) and t == LAST

        @block.sync
        def _(sp):
            for b in range(BATCH):
                for c in range(GH):
                    for h in range(2):
                        dst = vrows[b][c * NSTR + h:(c + 1) * NSTR:2, :, :].rearrange("p g d -> p (g d)")
                        sp.dma_start(dst, qkv["v"][h * SPARSE:h * SPARSE + 1, b * (QT + 1) + 1:(b + 1) * (QT + 1), :])\
                            .then_inc(s["vrows_in"], 16)
            for dst, src in ((hmask[:], a["hmask"]), (identb[:], a["identb"]), (ones[0:1, :], a["ones_row"]),
                             (smask[0:1, :], a["strided_masks"]),
                             (wmask[:].rearrange("p a c -> p (a c)"), a["window_masks"]), (vmask[:], a["vmask"]),
                             (wo_T[:], a["wo_T"].rearrange("(k p) n -> p k n", p=P))):
                sp.dma_start(dst, src).then_inc(s["w_in"], 16)

            def tile(t, p, b):
                wait(sp, "o_ready", t)
                sp.dma_start(xr[:], x_in[bass.ds(t * P, P), :]).then_inc(s["xr_in"], 16)
                if not is_first(t):
                    sp.dma_start(x_out[bass.ds((t - 1) * P, P), :], o[:]).then_inc(s["stored"], 16)

            all_tiles(sp, tile)
            sp.wait_ge(s["o_ready"], NT)
            sp.dma_start(x_out[LAST * P:NT * P, :], o[:]).then_inc(s["stored"], 16)
            sp.wait_ge(s["stored"], 16 * NT)

        @block.gpsimd
        def _(pool):
            pool.wait_ge(s["w_in"], 16 * N_IN)

            def mask_q(t, p, b):
                pool.wait_ge(s["q_ready"], t + 1)
                wait(pool, "S_ready", NGR * (t - 1))
                for f in range(KD):
                    nc.gpsimd.tensor_tensor(qm[p][:, f * HPB:(f + 1) * HPB, :],
                                            q[p][:, f:f + 1, :].to_broadcast([P, HPB, P]),
                                            hmask[:].unsqueeze(2).to_broadcast([P, HPB, P]), ALU.mult)\
                        .then_inc(s["qm_ready"], 1)

            all_tiles(pool, mask_q)

        @block.vector
        def _(dve):
            def strided_keys(b):
                kT = qkv["kT"]
                for f in range(KD):
                    keys = kT[:, f, b * SPAD + P:(b + 1) * SPAD:SPARSE]
                    nc.vector.tensor_tensor(Ks[b][:, f, :, :], keys.unsqueeze(1).to_broadcast([P, HPB, NSTR]),
                                            hmask[:].unsqueeze(2).to_broadcast([P, HPB, NSTR]), ALU.mult)\
                        .then_inc(s["Ks_ready"], 1)
                nc.vector.tensor_tensor(Vs[b][:], vrows[b][:], vmask[:].unsqueeze(1).to_broadcast([P, NGR, GH * HD]),
                                        ALU.mult).then_inc(s["Vs_ready"], 1)

            def strided_tops(t):
                dve.wait_ge(s["Ss_ready"], t + 1)
                nc.vector.tensor_reduce(top_s[:], Ss_ps[:].rearrange("p (h k) -> p h k", h=HEADS), AX.X, ALU.max)\
                    .then_inc(s["top_s_ready"], 1)
                dve.wait_ge(s["top_s_ready"], t + 1)
                nc.vector.tensor_scalar(shift_s[:], top_s[:], -0.25, None, ALU.mult).then_inc(s["shift_s_ready"], 1)

            def maxima(t, gr):
                h = slice(gr * GH, (gr + 1) * GH)
                dve.wait_ge(s["S_ready"], t * NGR + gr + 1)
                nc.vector.tensor_reduce(top_w[:, h], S_ps[gr % 2][:], AX.X, ALU.max).then_inc(s["tops"], 1)
                dve.wait_ge(s["tops"], t * NGR + gr + 1)
                dve.wait_ge(s["shift_s_ready"], t + 1)
                wait(dve, "exp_done", GH * ((t - 1) * NGR + gr + 1))
                nc.vector.scalar_tensor_tensor(out=shift[:, h], in0=top_w[:, h], scalar=-0.25, in1=shift_s[:, h],
                                               op0=ALU.mult, op1=ALU.min).then_inc(s["shifts"], 1)

            def shift_strided(t):
                wait(dve, "str_exp", t)
                dve.wait_ge(s["shifts"], (t + 1) * NGR)
                nc.vector.scalar_tensor_tensor(
                    out=str_in[:].rearrange("p (h k) -> p h k", h=HEADS),
                    in0=Ss_ps[:].rearrange("p (h k) -> p h k", h=HEADS), scalar=0.25,
                    in1=shift[:].unsqueeze(2).to_broadcast([P, HEADS, NSTR]),
                    op0=ALU.mult, op1=ALU.add).then_inc(s["str_shifted"], 1)

            def take_PT0(t, gr):
                dve.wait_ge(s["turned0"], t * NGR + gr + 1)
                wait(dve, "PV_done", t * NGR + gr - 1)
                nc.vector.tensor_copy(PT[gr % 2][:, 0].rearrange("p h c -> p (h c)"), T_ps[0][:])\
                    .then_inc(s["PT0_taken"], 1)

            def denominators(t, p):
                dve.wait_ge(s["str_exp"], t + 1)
                nc.vector.tensor_reduce(den_s[:], probs_s[:].rearrange("p (h k) -> p h k", h=HEADS), AX.X, ALU.add)\
                    .then_inc(s["sums"], 1)
                dve.wait_ge(s["sums"], 2 * t + 1)
                dve.wait_ge(s["exp_done"], GH * NGR * (t + 1))
                nc.vector.tensor_tensor(den_s[:], den_s[:], den[p][:], ALU.add).then_inc(s["sums"], 1)
                dve.wait_ge(s["sums"], 2 * t + 2)
                wait(dve, "on_ready", t)
                nc.vector.reciprocal(rden[:], den_s[:]).then_inc(s["dens"], 1)

            def normalise(t):
                dve.wait_ge(s["O_ready"], t + 1)
                dve.wait_ge(s["dens"], t + 1)
                wait(dve, "O_turned", t)
                nc.vector.tensor_tensor(on[:].rearrange("p (h d) -> p h d", h=HEADS),
                                        O_ps[:, 0:D].rearrange("p (h d) -> p h d", h=HEADS),
                                        rden[:].unsqueeze(2).to_broadcast([P, HEADS, HD]), ALU.mult)\
                    .then_inc(s["on_ready"], 1)

            def output(t):
                dve.wait_ge(s["out_ready"], t + 1)
                dve.wait_ge(s["xr_in"], 16 * (t + 1))
                wait(dve, "stored", 16 * t)
                nc.vector.tensor_tensor(o[:], T_ps[1][:, 0:D], xr[:], ALU.add).then_inc(s["o_ready"], 1)

            dve.wait_ge(s["w_in"], 16 * N_IN)
            dve.wait_ge(s["vrows_in"], 16 * BATCH * GH * 2)
            for b in range(BATCH):
                strided_keys(b)

            def tile(t, p, b):
                strided_tops(t)
                maxima(t, 0)
                if not is_first(t):
                    take_PT0(t - 1, NGR - 1)
                    denominators(t - 1, 1 - p)
                for gr in range(1, NGR):
                    maxima(t, gr)
                    if gr == NGR - 1:
                        shift_strided(t)
                    take_PT0(t, gr - 1)
                    if gr == 1 and not is_first(t):
                        normalise(t - 1)
                if not is_first(t):
                    output(t - 1)

            all_tiles(dve, tile)
            take_PT0(LAST, NGR - 1)
            denominators(LAST, 1)
            normalise(LAST)
            output(LAST)

        @block.scalar
        def _(act):
            def take_q(t, p):
                wait(act, "Ss_ready", t - 1)
                wait(act, "qm_ready", KD * (t - 1))
                nc.scalar.copy(q[p][:], qkv["qT"][:, :, bass.ds(t * P, P)]).then_inc(s["q_ready"], 1)

            def exps(t, p, gr):
                act.wait_ge(s["shifts"], t * NGR + gr + 1)
                wait(act, "turned0", t * NGR + gr - 1)
                wait(act, "turned1", t * NGR + gr - 1)
                if gr == 0:
                    wait(act, "dens", t - 1)
                for h in range(GH):
                    hh = gr * GH + h
                    nc.scalar.activation(probs[gr % 2][:, h, :], S_ps[gr % 2][:, h, :], ACT.Exp,
                                         bias=shift[:, hh:hh + 1], scale=0.25,
                                         accum_out=den[p][:, hh:hh + 1]).then_inc(s["exp_done"], 1)

            def exp_strided(t):
                act.wait_ge(s["str_shifted"], t + 1)
                wait(act, "str_turned", t)
                wait(act, "dens", t)
                nc.scalar.activation(probs_s[:], str_in[:], ACT.Exp).then_inc(s["str_exp"], 1)

            def take_PT1(t, gr):
                act.wait_ge(s["turned1"], t * NGR + gr + 1)
                wait(act, "PV_done", t * NGR + gr - 1)
                nc.scalar.copy(PT[gr % 2][:, 1].rearrange("p h c -> p (h c)"), T_ps[1][:])\
                    .then_inc(s["PT1_taken"], 1)

            def take_PTs(t):
                act.wait_ge(s["str_turned"], t + 1)
                wait(act, "O_ready", t)
                nc.scalar.copy(PTs[:].rearrange("p h c -> p (h c)"), T_ps[1][:]).then_inc(s["PTs_taken"], 1)

            def take_OT(t):
                act.wait_ge(s["O_turned"], t + 1)
                wait(act, "out_ready", t)
                nc.scalar.copy(OT[:].rearrange("p k c -> p (k c)"), T_ps[1][:, 0:D]).then_inc(s["OT_taken"], 1)

            def tile(t, p, b):
                exps(t, p, 0)
                if not is_first(t):
                    take_PT1(t - 1, NGR - 1)
                    take_PTs(t - 1)
                if not is_last(t):
                    take_q(t + 1, 1 - p)
                for gr in range(1, NGR):
                    exps(t, p, gr)
                    if gr == NGR - 1:
                        exp_strided(t)
                    take_PT1(t, gr - 1)
                    if gr == 2 and not is_first(t):
                        take_OT(t - 1)

            take_q(0, 0)
            all_tiles(act, tile)
            take_PT1(LAST, NGR - 1)
            take_PTs(LAST)
            take_OT(LAST)

        @block.tensor
        def _(pe):
            def scores_strided(t, p, b):
                pe.wait_ge(s["q_ready"], t + 1)
                wait(pe, "str_shifted", t)
                nc.tensor.matmul(Ss_ps[:], ones[0:1, :], smask[0:1, bass.ds((t - b * QT) * NSTR, NSTR)]
                                 .unsqueeze(1).to_broadcast([1, HEADS, NSTR]),
                                 start=True, stop=False, skip_group_check=True)
                for f in range(KD):
                    m = nc.tensor.matmul(Ss_ps[:, f * D:(f + 1) * D], q[p][:, f, :],
                                         Ks[b][:, f, :, :].rearrange("p h k -> p (h k)"),
                                         start=False, stop=True, skip_group_check=True)
                m.then_inc(s["Ss_ready"], 1)

            def scores(t, p, b, gr):
                first = isinstance(t, int) and t % QT == 0
                if gr == 0:
                    pe.wait_ge(s["qm_ready"], KD * (t + 1))
                wait(pe, "exp_done", GH * (t * NGR + gr - 1))
                for h2 in range(2):
                    nc.tensor.matmul(S_ps[gr % 2][:, 2 * h2:2 * h2 + 2, :].rearrange("p h c -> p (h c)"), identb[:],
                                     wmask[:, 0 if first else 1, :], start=True, stop=False, skip_group_check=True)
                    for h in (2 * h2, 2 * h2 + 1):
                        hh = gr * GH + h
                        m = nc.tensor.matmul(S_ps[gr % 2][:, h, :], qm[p][:, hh, :],
                                             qkv["kT"][:, hh // HPB, bass.ds(t * P + b * P, W2)],
                                             start=False, stop=True, skip_group_check=True)
                m.then_inc(s["S_ready"], 1)

            def turn_P(t, gr, c):
                if c == 0:
                    pe.wait_ge(s["exp_done"], GH * (t * NGR + gr + 1))
                    wait(pe, "PT0_taken", t * NGR + gr)
                else:
                    wait(pe, "PT1_taken", t * NGR + gr)
                    if gr == 0:
                        wait(pe, "PTs_taken", t)
                    if gr == 2:
                        wait(pe, "OT_taken", t)
                    if gr == 3:
                        wait(pe, "o_ready", t)
                for h in range(GH):
                    m = nc.tensor.transpose(T_ps[c][:, h * P:(h + 1) * P], probs[gr % 2][:, h, c * P:(c + 1) * P],
                                            g["ident"][:])
                m.then_inc(s[f"turned{c}"], 1)

            def gather_V(t, b, gr):
                pe.wait_ge(s["PT0_taken"], t * NGR + gr + 1)
                pe.wait_ge(s["PT1_taken"], t * NGR + gr + 1)
                if gr == 0:
                    wait(pe, "on_ready", t)
                for c in range(2):
                    for h in range(GH):
                        hh = gr * GH + h
                        m = nc.tensor.matmul(O_ps[:, hh * HD:(hh + 1) * HD], PT[gr % 2][:, c, h, :],
                                             qkv["v"][:, bass.ds(t + (b + c), 1), hh * HD:(hh + 1) * HD]
                                             .rearrange("p a d -> p (a d)"),
                                             start=(gr == 0 and c == 0 and h == 0), stop=False, skip_group_check=True)
                m.then_inc(s["PV_done"], 1)

            def turn_strided(t):
                pe.wait_ge(s["str_exp"], t + 1)
                pe.wait_ge(s["PT1_taken"], (t + 1) * NGR)
                for gr in range(NGR):
                    m = nc.tensor.transpose(T_ps[1][:, gr * P:(gr + 1) * P], probs_s[:, gr * P:(gr + 1) * P],
                                            g["ident"][:])
                m.then_inc(s["str_turned"], 1)

            def gather_strided(t, b):
                pe.wait_ge(s["PTs_taken"], t + 1)
                for gr in range(NGR):
                    m = nc.tensor.matmul(O_ps[:, gr * GH * HD:(gr + 1) * GH * HD], PTs[:, gr, :], Vs[b][:, gr, :],
                                         start=False, stop=True, skip_group_check=True)
                m.then_inc(s["O_ready"], 1)

            def turn_O(t, last):
                pe.wait_ge(s["on_ready"], t + 1)
                if not last:
                    pe.wait_ge(s["PT1_taken"], (t + 1) * NGR + 2)
                for k in range(KD):
                    m = nc.tensor.transpose(T_ps[1][:, k * P:(k + 1) * P], on[:, k * P:(k + 1) * P], g["ident"][:])
                m.then_inc(s["O_turned"], 1)

            def project_out(t, last):
                pe.wait_ge(s["OT_taken"], t + 1)
                if not last:
                    pe.wait_ge(s["PT1_taken"], (t + 1) * NGR + 3)
                for k in range(KD):
                    m = nc.tensor.matmul(T_ps[1][:, 0:D], OT[:, k, :], wo_T[:, k, :],
                                         start=(k == 0), stop=(k == KD - 1))
                m.then_inc(s["out_ready"], 1)

            pe.wait_ge(s["w_in"], 16 * N_IN)
            pe.wait_ge(s["Ks_ready"], KD * BATCH)
            pe.wait_ge(s["Vs_ready"], BATCH)
            scores_strided(0, 0, 0)
            scores(0, 0, 0, 0)

            def tile(t, p, b):
                last = is_last(t)
                prev_b = b - 1 if isinstance(t, int) and t % QT == 0 else b
                next_b = b + 1 if isinstance(t, int) and t % QT == QT - 1 else b
                for gr in range(NGR):
                    if gr < NGR - 1:
                        scores(t, p, b, gr + 1)
                    elif not last:
                        scores_strided(t + 1, 1 - p, next_b)
                        scores(t + 1, 1 - p, next_b, 0)
                    if not is_first(t):
                        if gr == 0:
                            turn_strided(t - 1)
                        if gr == 2:
                            turn_O(t - 1, False)
                        if gr == 3:
                            project_out(t - 1, False)
                    turn_P(t, gr, 0)
                    if gr:
                        gather_V(t, b, gr - 1)
                    elif not is_first(t):
                        gather_V(t - 1, prev_b, NGR - 1)
                    turn_P(t, gr, 1)
                    if gr == 0 and not is_first(t):
                        gather_strided(t - 1, prev_b)

            all_tiles(pe, tile)
            gather_V(LAST, BATCH - 1, NGR - 1)
            turn_strided(LAST)
            gather_strided(LAST, BATCH - 1)
            turn_O(LAST, True)
            project_out(LAST, True)


def attention(nc, g, a, x_in, x_out):
    with ExitStack() as ctx:
        r = Room(nc, ctx, "qkv_out")
        qkv = dict(qT=r.sb("qT", [P, KD, TOK]), kT=r.sb("kT", [P, KD, BATCH * SPAD]),
                   v=r.sb("v", [P, BATCH * (QT + 1), D]))
        qkv_block(nc, g, a, qkv, x_in)
        attend_block(nc, g, a, qkv, x_in, x_out)



def macaron_program(nc, out, ins):
    def scratch(name, shape):
        return nc.dram_tensor(name, shape, F32).ap()

    Room.sems = []
    a = ins
    stream = [a["x"]] + [scratch(f"x{i}", (TOK, D)) for i in range(1, 6)] + [out.rearrange("b t d -> (b t) d")]
    proj_T = scratch("proj_T", (2 * INNER, BATCH * HPAD))
    bc_T = scratch("bc_T", (2 * STATE, TOK + BLK))
    with ExitStack() as ctx:
        r = Room(nc, ctx, "g")
        g = dict(ident=r.sb("ident", [P, P]), w_up=r.sb("w_up", [P, KD, FH]), w_down=r.sb("w_down", [P, FM, D]),
                 b_up=r.sb("b_up", [P, FM]), half_bias=r.sb("half_bias", [P, D]),
                 neg_A=r.sb("neg_A", [P, IB, STATE]), minus_half=r.sb("minus_half", [P, STATE]),
                 zeros=r.sb("zeros", [P, D]), take=r.sb("take", [P, TOPK * NT], I32),
                 share=r.sb("share", [P, TOPK * NT]))
        fold_block(nc, g, a)
        ffn_block(nc, "ffn0", g, stream[0], stream[1])
        inproj_block(nc, g, a, stream[1], proj_T)
        mamba_block(nc, g, a, stream[1], proj_T, bc_T, stream[2])
        ffn_block(nc, "ffn1", g, stream[2], stream[3])
        recycle_semaphores(nc)
        for m in range(2):
            if m:
                attention(nc, g, a, stream[4], stream[5])
            slots = scratch(f"slots{m}", (NE * CAP, D))
            done = scratch(f"done{m}", (NE * CAP, D))
            route_block(nc, f"route{m}", g, a, stream[3 + 2 * m], slots)
            expert_block(nc, f"expert{m}", g, a, slots, done)
            combine_block(nc, f"combine{m}", g, stream[3 + 2 * m], done, stream[4 + 2 * m])



def layouts(np, v):
    def columns(vec):
        return vec.reshape(-1, P).T

    wqkv = v["L1_attn_w_qkv"]
    return dict(
        x=v["L0_attn_hidden_states"].reshape(TOK, D),
        w_exp=v["L0_ffn_W_exp"], w_con_T=v["L0_ffn_W_con"].T, b_exp=v["L0_ffn_b_exp"][None],
        up_w=v["L0_ffn_up_weights"].transpose(0, 3, 2, 1).reshape(STAGES, 2 * FH),
        down_w=v["L0_ffn_down_weights"][::-1].transpose(0, 2, 3, 1).reshape(STAGES, 2 * FH),
        up_bias=v["L0_ffn_up_bias"][None], b_con=v["L0_ffn_b_con"], down_bias=v["L0_ffn_down_bias"],
        A_log=v["L0_attn_A_log"], in_proj_T=v["L0_attn_in_proj_w"].T,
        conv_w=v["L0_attn_conv_w"].reshape(INNER, TAPS), conv_b=columns(v["L0_attn_conv_b"]),
        x_proj_T=v["L0_attn_x_proj_w"].T, dt_proj_T=v["L0_attn_dt_proj_w"].T,
        dt_bias=columns(v["L0_attn_dt_proj_b"]), D=columns(v["L0_attn_D"]), out_proj_T=v["L0_attn_out_proj_w"].T,
        xd_ln_w=np.concatenate([v["L0_attn_dt_ln_w"], v["L0_attn_b_ln_w"], v["L0_attn_c_ln_w"]])[:, None],
        gate_T=v["L1_ffn_gate_w"].T, fc1_T=v["L1_ffn_fc1_w"].transpose(2, 0, 1).reshape(D, NE * EH),
        fc2=v["L1_ffn_fc2_w"].reshape(NE * EH, D), b1=v["L1_ffn_fc1_b"].reshape(NE, EM, P).transpose(0, 2, 1).reshape(NE * P, EM), b2=v["L1_ffn_fc2_b"].reshape(-1),
        wq_T=wqkv[0:D].T, wk_T=wqkv[D:2 * D].T, wv_T=wqkv[2 * D:3 * D].T, wo_T=v["L1_attn_w_out"].T)


def constants(np):
    p = np.arange(P)
    f32, bf16 = np.dtype(np.float32), mybir.dt.np(BF16)
    row, col = p[:, None], p[None, :]
    keep = np.ones((P, NBLK + 1), f32)
    keep[:, 0::NBLK // BATCH] = 0
    own = np.where(col <= row, 0, NEG)
    before = np.where((col >= row) | (col % SPARSE == 0), 0, NEG)
    none = np.full((P, P), NEG)
    window = np.concatenate([none, own] * 2 + [before, own] * 2, axis=1)
    strided = np.concatenate([np.where(np.arange(NSTR) * SPARSE < P * (i - 1), 0, NEG) for i in range(QT)])[None]
    return dict(
        ident=np.eye(P, dtype=f32), keep=keep,
        rank=np.tile(NE - np.arange(NE), (P, 1)).astype(f32),
        first_slot=np.tile(CAP * np.arange(NE), (P, 1)).astype(f32),
        outside=(NE * CAP + np.arange(TOPK * NT)[None] * P + row).astype(f32),
        earlier=(row < col).astype(f32), ones=np.ones((P, P), f32),
        hmask=(row // HD == np.arange(HPB)).astype(f32),
        vmask=(row // NSTR == np.arange(GH * HD) // HD).astype(f32),
        identb=np.eye(P).astype(bf16), ones_row=np.ones((1, P)).astype(bf16),
        window_masks=window.astype(bf16), strided_masks=strided.astype(bf16))


def kernel(**inputs):
    import numpy as np
    import concourse.bacc as bacc
    from concourse.bass_utils import run_bass_kernel_spmd

    nc = bacc.Bacc("TRN2", target_bir_lowering=False, num_devices=1)
    arrays, ins = {}, {}
    for name, value in {**layouts(np, inputs), **constants(np)}.items():
        value = np.ascontiguousarray(value)
        arrays[f"in_{name}_dram"] = value
        ins[name] = nc.dram_tensor(f"in_{name}_dram", value.shape, mybir.dt.from_np(value.dtype),
                                   kind="ExternalInput").ap()
    out = nc.dram_tensor("out_0_dram", (BATCH, SEQ, D), F32, kind="ExternalOutput").ap()
    macaron_program(nc, out, ins)
    result = run_bass_kernel_spmd(nc, [arrays], core_ids=[0])
    return result.results[0]["out_0_dram"]
```

```python
from contextlib import ExitStack

import concourse.bass as bass
from concourse import mybir

F32 = mybir.dt.float32
BF16 = mybir.dt.bfloat16
F32R = mybir.dt.float32r
I32 = mybir.dt.int32
ALU = mybir.AluOpType
ACT = mybir.ActivationFunctionType
AX = mybir.AxisListType

P = 128
BATCH, SEQ, D = 2, 2048, 256
TOK = BATCH * SEQ
KD = D // P
BLK = 512
NBLK = TOK // BLK
TPB = BLK // P
NT = TOK // P
LN_EPS = 1e-5
RMS_EPS = 1e-6
FH = 1024
FM = FH // P
STAGES = 10
INNER, STATE, TAPS, RANK = 512, 16, 4, 64
IB = INNER // P
XD = RANK + 2 * STATE
HPAD = SEQ + TAPS - 1
HEADS, HD = 16, 16
HPB = P // HD
SPARSE = 64
NSTR = SEQ // SPARSE
QT = SEQ // P
NEG = -1.0e30
NE, EH, CAP, TOPK = 8, 1024, 1024, 2
EM = EH // P
HALF = 512
HPE = CAP // HALF


class Room:

    def __init__(self, nc, ctx, tag):
        self.nc, self.ctx, self.tag = nc, ctx, tag

    def sb(self, name, shape, dt=F32):
        return self.ctx.enter_context(self.nc.sbuf_tensor(f"{self.tag}_{name}", shape, dt))

    def ps(self, name, shape, dt=F32):
        return self.ctx.enter_context(self.nc.psum_tensor(f"{self.tag}_{name}", shape, dt))

    def sem(self, name):
        sem = self.nc.alloc_semaphore(f"{self.tag}_{name}")
        Room.sems.append(sem)
        return sem

    sems = []


def recycle_semaphores(nc):
    nc.clear_and_free_semaphores(Room.sems)
    Room.sems = []
    nc.all_engine_barrier()


def tiles(dram, i, n=TPB):
    return dram[bass.ds(i * (n * P), n * P), :].rearrange("(j p) d -> p j d", p=P)



def product(nc, out, lhs, rhs, start, stop):
    nc.tensor.matmul(out, lhs[0], rhs[0], start=start, stop=False)
    nc.tensor.matmul(out, lhs[1], rhs[0], start=False, stop=False)
    return nc.tensor.matmul(out, lhs[0], rhs[1], start=False, stop=stop)


def low_part(engine, low, x, high):
    return engine.tensor_tensor(low, x, high.bitcast(F32), ALU.subtract)



LN_OPS = 3 * TPB + 2


def ln_vector(nc, dve, i, x, xn, stat, mv, s, n=TPB):
    ops = 3 * n + 2
    dve.wait_ge(s["x_loaded"], 16 * (i + 1))
    for j in range(n):
        nc.vector.bn_stats(stat[:, j, :], x[:, j, :]).then_inc(s["ln"], 1)
    dve.wait_ge(s["ln"], i * ops + n)
    nc.vector.tensor_copy(mv[:, n, :], stat[:, n - 1, 0:2]).then_inc(s["ln"], 1)
    for j in range(n):
        nc.vector.bn_aggr(mv[:, j, :], stat[:, j, :]).then_inc(s["ln"], 1)
    dve.wait_ge(s["ln"], i * ops + 2 * n + 1)
    nc.vector.tensor_scalar(mv[:, 0:n, 1], mv[:, 0:n, 1], LN_EPS, None, ALU.add).then_inc(s["ln"], 1)
    dve.wait_ge(s["rstd_ready"], i + 1)
    dve.wait_ge(s["xT_ps_ready"], KD * i)
    for j in range(n):
        nc.vector.tensor_scalar(xn[:, j, :], x[:, j, :], mv[:, j, 0:1], s["rstd"][:, j:j + 1],
                                ALU.subtract, ALU.mult).then_inc(s["ln"], 1)


def ln_gpsimd(nc, pool, i, mv, s, n=TPB):
    pool.wait_ge(s["ln"], i * (3 * n + 2) + 2 * n + 2)
    nc.gpsimd.tensor_tensor(s["rstd"][:, 0:n], mv[:, 0:n, 1], s["minus_half"][:, 0:n], ALU.pow)\
        .then_inc(s["rstd_ready"], 1)


def ln_transpose(nc, pe, i, xn, xT_ps, ident, s, n=TPB):
    pe.wait_ge(s["ln"], (i + 1) * (3 * n + 2))
    pe.wait_ge(s["xT_ready"], KD * i)
    for k in range(KD):
        for j in range(n):
            t = nc.tensor.transpose(xT_ps[k][:, j * P:(j + 1) * P], xn[:, j, k * P:(k + 1) * P], ident[:])
        t.then_inc(s["xT_ps_ready"], 1)


def ln_high(nc, act, i, xT, xT_ps, s, used, count):
    for k in range(KD):
        act.wait_ge(s["xT_ps_ready"], KD * i + k + 1)
        act.wait_ge(used, count)
        nc.scalar.copy(xT[0][:, k, :], xT_ps[k][:]).then_inc(s["xT_high_ready"], 1)


def ln_low(nc, dve, i, xT, xT_ps, s):
    for k in range(KD):
        dve.wait_ge(s["xT_high_ready"], KD * i + k + 1)
        low_part(nc.vector, xT[1][:, k, :], xT_ps[k][:], xT[0][:, k, :]).then_inc(s["xT_ready"], 1)


def ln_room(r, n=TPB, split=True):
    x = r.sb("x", [P, n, D])
    xn = r.sb("xn", [P, n, D])
    stat = r.sb("stat", [P, n, 6])
    mv = r.sb("mv", [P, n + 1, 2])
    xT_ps = [r.ps(f"xT_ps{k}", [P, n * P]) for k in range(KD)]
    if split:
        xT = [r.sb(f"xT_{part}", [P, KD, n * P], F32R) for part in ("high", "low")]
    else:
        xT = r.sb("xT", [P, KD, n * P])
    s = {k: r.sem(k) for k in ("x_loaded", "ln", "rstd_ready", "xT_ps_ready", "xT_high_ready", "xT_ready")}
    s["rstd"] = r.sb("rstd", [P, n])
    return x, xn, stat, mv, xT_ps, xT, s



LOCAL = 7
FAR = STAGES - LOCAL


def fold_block(nc, g, a):
    with ExitStack() as ctx:
        r = Room(nc, ctx, "fold")
        local = [[r.sb(f"local{m}_{b}", [P, FH]) for b in range(2)] for m in range(2)]
        w = [[r.sb(f"w{m}_{b}", [P, 2 * FH]) for b in range(2)] for m in range(2)]
        w_far = [r.sb(f"w_far{b}", [P, 2 * FH]) for b in range(FAR)]
        prod = [[r.sb(f"prod{m}_{t}", [P, FH]) for t in range(2)] for m in range(2)]
        exp_T = r.sb("exp_T", [P, FM, D])
        con = [r.sb(f"con{b}", [P, FM, D]) for b in range(2)]
        up = [r.sb(f"up{b}", [P, KD, FH]) for b in range(2)]
        cols = [r.sb(f"cols{m}", [P, FAR, 2, 2, FM // 2]) for m in range(2)]
        bias = r.sb("bias", [P, 2, FM])
        bcol = [r.sb(f"bcol{b}", [P, FM]) for b in range(2)]
        bprod = [r.sb(f"bprod{t}", [P, FM // 2]) for t in range(2)]
        con_bias = r.sb("con_bias", [P, 2, D])
        alog = r.sb("alog", [P, IB, STATE])
        up_ps = [r.ps(f"up_ps{i}", [P, BLK]) for i in range(2 * KD)]
        con_ps = [r.ps(f"con_ps{i}", [P, 2, D]) for i in range(2)]
        bias_ps = r.ps("bias_ps", [P, FM])
        base_in, const_in = r.sem("base_in"), r.sem("const_in")
        w_in = [[r.sem(f"w_{n}_in{b}") for b in range(2)] for n in ("up", "down")]
        far_in = r.sem("far_in")
        idents = [r.sem(f"{n}_idents") for n in ("up", "down")]
        locals_ = [r.sem(f"{n}_local") for n in ("up", "down")]
        up_ps_ready, up_taken, far, scaled, con_done, bias_ready, bsteps, con_ready, con_taken, misc = (
            r.sem(n) for n in ("up_ps_ready up_taken far scaled con_done bias_ready bsteps con_ready "
                               "con_taken misc").split())
        block = ctx.enter_context(nc.Block())
        RESULT = (LOCAL - 1) % 2

        def blocks(distance, m):
            n, j = divmod(m, distance)
            return [n * 2 * distance + t * distance + j for t in range(2)]

        @block.sync
        def _(sp):
            sp.dma_start(g["ident"][:], a["ident"]).then_inc(base_in, 16)
            for st in range(LOCAL):
                for m, name in enumerate(("up_w", "down_w")):
                    if st >= 2:
                        sp.wait_ge(locals_[m], 3 * (st - 1))
                    sp.dma_start(w[m][st % 2][:], a[name][st + m * FAR, :].partition_broadcast(P))\
                        .then_inc(w_in[m][st % 2], 16)
                if st == 0:
                    sp.dma_start(con[0][:], a["w_con"].rearrange("(m p) d -> p m d", p=P)).then_inc(const_in, 16)
                    sp.dma_start(exp_T[:], a["w_exp_T"].rearrange("(m p) d -> p m d", p=P)).then_inc(const_in, 16)
                    for m, name in enumerate(("up_cols", "down_cols")):
                        sp.dma_start(cols[m][:].rearrange("p s i o m -> p (s i o m)"), a[name])\
                            .then_inc(const_in, 16)
                    for n, name in enumerate(("b_exp", "up_bias")):
                        sp.dma_start(bias[:, n, :], a[name]).then_inc(const_in, 16)
                    for n, name in enumerate(("b_con", "down_bias")):
                        sp.dma_start(con_bias[:, n, :], a[name].partition_broadcast(P)).then_inc(const_in, 16)
                    sp.dma_start(alog[:], a["A_log"].rearrange("(k p) n -> p k n", p=P)).then_inc(const_in, 16)
            for n in range(FAR):
                sp.dma_start(w_far[n][:], a["up_w"][LOCAL + n, :].partition_broadcast(P)).then_inc(far_in, 16)

        def stage(eng, src, dst, wt, s, q0, q1, sem, n0):
            si = src.rearrange("p (n t s) -> p t n s", t=2, s=s)
            do = dst.rearrange("p (n t s) -> p t n s", t=2, s=s)
            wi = wt.rearrange("p (i o n s) -> p i o n s", i=2, o=2, s=s)
            q = [v.rearrange("p (o n s) -> p o n s", o=2, s=s) for v in (q0, q1)]
            for i in range(2):
                eng.tensor_tensor(q[i], wi[:, i], si[:, i:i + 1].to_broadcast(list(q[i].shape)), ALU.mult)\
                    .then_inc(sem, 1)
            return do, q

        def local_stages(queue, eng, m):
            queue.wait_ge(base_in, 16)
            ident = g["ident"][:].unsqueeze(1).to_broadcast([P, FM, P])
            eng.tensor_tensor(local[m][1][:].rearrange("p (m c) -> p m c", m=FM), ident, ident, ALU.mult)\
                .then_inc(idents[m], 1)
            queue.wait_ge(idents[m], 1)
            for st in range(LOCAL):
                queue.wait_ge(w_in[m][st % 2], 16 * (st // 2 + 1))
                if st:
                    queue.wait_ge(locals_[m], 3 * st)
                src, dst = local[m][1 - st % 2][:], local[m][st % 2][:]
                s = 2 ** st if m == 0 else 2 ** (LOCAL - 1 - st)
                do, q = stage(eng, src, dst, w[m][st % 2][:], s, prod[m][0][:], prod[m][1][:], locals_[m], 3 * st)
                queue.wait_ge(locals_[m], 3 * st + 2)
                eng.tensor_tensor(do, q[0], q[1], ALU.add).then_inc(locals_[m], 1)

        @block.gpsimd
        def _(pool):
            nc.gpsimd.memset(g["minus_half"][:], -0.5)
            nc.gpsimd.memset(g["zeros"][:], 0.0)
            local_stages(pool, nc.gpsimd, 1)

        @block.scalar
        def _(act):
            act.wait_ge(const_in, 16 * 9)
            for st in range(FAR):
                src, dst = con[st % 2], con[1 - st % 2]
                if st:
                    act.wait_ge(con_done, FM * st)
                for m in range(FM // 2):
                    ins = blocks(FM // 2 >> st, m)
                    for o in range(2):
                        nc.scalar.mul(dst[:, ins[o], :], src[:, ins[0], :], cols[1][:, st, 0, o, m:m + 1])\
                            .then_inc(scaled, 1)
            nc.scalar.activation(alog[:], alog[:], ACT.Exp).then_inc(misc, 1)
            act.wait_ge(misc, 1)
            nc.scalar.mul(g["neg_A"][:], alog[:], -1.0).then_inc(misc, 1)
            for k in range(KD):
                for h in range(2):
                    i = 2 * k + h
                    act.wait_ge(up_ps_ready, i + 1)
                    nc.scalar.copy(up[0][:, k, h * BLK:(h + 1) * BLK], up_ps[i][:]).then_inc(up_taken, 1)
            for m2 in range(FM // 2):
                act.wait_ge(con_ready, m2 + 1)
                nc.scalar.copy(g["w_down"][:, 2 * m2:2 * m2 + 2, :], con_ps[m2 % 2][:]).then_inc(con_taken, 1)

        @block.vector
        def _(dve):
            local_stages(dve, nc.vector, 0)
            for st in range(FAR):
                src, dst = con[st % 2], con[1 - st % 2]
                for m in range(FM // 2):
                    ins = blocks(FM // 2 >> st, m)
                    for o in range(2):
                        dve.wait_ge(scaled, FM * st + 2 * m + o + 1)
                        nc.vector.scalar_tensor_tensor(
                            out=dst[:, ins[o], :], in0=src[:, ins[1], :], scalar=cols[1][:, st, 1, o, m:m + 1],
                            in1=dst[:, ins[o], :], op0=ALU.mult, op1=ALU.add).then_inc(con_done, 1)
            n = 0
            for st in range(FAR):
                dve.wait_ge(far_in, 16 * FAR)
                for k in range(KD):
                    src = up[st % 2]
                    dst = g["w_up"] if st == FAR - 1 else up[1 - st % 2]
                    dve.wait_ge(up_taken, 2 * (k + 1))
                    if n:
                        dve.wait_ge(far, n)
                    do, q = stage(nc.vector, src[:, k, :], dst[:, k, :], w_far[st][:], P << st,
                                  prod[0][0][:], prod[0][1][:], far, n)
                    dve.wait_ge(far, n + 2)
                    nc.vector.tensor_tensor(do, q[0], q[1], ALU.add).then_inc(far, 1)
                    n += 3
            dve.wait_ge(bias_ready, 1)
            steps = 0

            def done(ins):
                nonlocal steps
                ins.then_inc(bsteps, 1)
                steps += 1
                dve.wait_ge(bsteps, steps)

            done(nc.vector.tensor_copy(bcol[0][:], bias_ps[:]))
            for st in range(FAR):
                d = 1 << st
                src, dst = (v[:].rearrange("p (n t j) -> p t n j", t=2, j=d) for v in (bcol[st % 2], bcol[1 - st % 2]))
                for o in range(2):
                    q = [v[:].rearrange("p (n j) -> p n j", j=d) for v in bprod]
                    for i in range(2):
                        done(nc.vector.tensor_tensor(q[i], src[:, i],
                                                     cols[0][:, st, i, o, :].rearrange("p (n j) -> p n j", j=d),
                                                     ALU.mult))
                    done(nc.vector.tensor_tensor(dst[:, o], q[0], q[1], ALU.add))
            done(nc.vector.tensor_tensor(g["b_up"][:], bcol[FAR % 2][:], bias[:, 1, :], ALU.add))
            done(nc.vector.tensor_tensor(con_bias[:, 0, :], con_bias[:, 0, :], con_bias[:, 1, :], ALU.add))
            done(nc.vector.tensor_scalar(g["half_bias"][:], con_bias[:, 0, :], 0.5, None, ALU.mult))

        @block.tensor
        def _(pe):
            pe.wait_ge(const_in, 16 * 9)
            pe.wait_ge(locals_[0], 3 * LOCAL)
            M = local[0][RESULT]
            for k in range(KD):
                for h in range(2):
                    for j in range(FM // 2):
                        m = h * (FM // 2) + j
                        t = nc.tensor.matmul(up_ps[2 * k + h][:, j * P:(j + 1) * P], exp_T[:, m, k * P:(k + 1) * P],
                                             M[:, m * P:(m + 1) * P], start=True, stop=True)
                    t.then_inc(up_ps_ready, 1)
            for m in range(FM):
                t = nc.tensor.matmul(bias_ps[:, m:m + 1], M[:, m * P:(m + 1) * P], bias[:, 0, m:m + 1],
                                     start=True, stop=True)
            t.then_inc(bias_ready, 1)
            pe.wait_ge(locals_[1], 3 * LOCAL)
            pe.wait_ge(con_done, FM * FAR)
            M, W = local[1][RESULT], con[FAR % 2]
            for m in range(FM):
                if m >= 4 and m % 2 == 0:
                    pe.wait_ge(con_taken, m // 2 - 1)
                t = nc.tensor.matmul(con_ps[m // 2 % 2][:, m % 2, :], M[:, m * P:(m + 1) * P], W[:, m, :],
                                     start=True, stop=True)
                if m % 2:
                    t.then_inc(con_ready, 1)



def ffn_block(nc, tag, g, x_in, x_out):
    with ExitStack() as ctx:
        r = Room(nc, ctx, tag)
        x, xn, stat, mv, xT_ps, xT, s = ln_room(r)
        s["minus_half"] = g["minus_half"]
        xb = r.sb("xb", [P, TPB, D])
        hid = r.sb("hid", [P, FM, BLK])
        hid_high, hid_low = (r.sb(f"hid_{part}", [P, FM, BLK], F32R) for part in ("high", "low"))
        y = r.sb("y", [P, TPB, D])
        up_w = [r.sb(f"up_{part}", [P, KD, FH], F32R) for part in ("high", "low")]
        down_w = [r.sb(f"down_{part}", [P, FM, D], F32R) for part in ("high", "low")]
        w_high, w_low = r.sem("w_high"), r.sem("w_low")
        h_ps = [r.ps(f"h_ps{i}", [P, BLK]) for i in range(3)]
        y_ps = [r.ps(f"y_ps{i}", [P, BLK])[:, 0:D] for i in range(3)]
        xb_ready, h_ps_ready, hid_ready, low_ready, y_ps_ready, y_ready, stored = (
            r.sem(n) for n in ("xb_ready", "h_ps_ready", "hid_ready", "low_ready", "y_ps_ready", "y_ready", "stored"))
        block = ctx.enter_context(nc.Block())
        LAST = NBLK - 1

        @block.sync
        def _(sp):
            def load(i):
                sp.dma_start(x[:], tiles(x_in, i)).then_inc(s["x_loaded"], 16)

            def store(i):
                sp.wait_ge(y_ready, TPB * (i + 1))
                sp.dma_start(tiles(x_out, i), y[:]).then_inc(stored, 16)

            load(0)
            with sp.Fori(0, LAST) as i:
                sp.wait_ge(s["ln"], LN_OPS * (i + 1))
                sp.wait_ge(xb_ready, i + 1)
                load(i + 1)
                store(i)
            store(LAST)
            sp.wait_ge(stored, 16 * NBLK)

        @block.gpsimd
        def _(pool):
            def biased(i):
                pool.wait_ge(s["x_loaded"], 16 * (i + 1))
                pool.wait_ge(y_ready, TPB * i)
                nc.gpsimd.tensor_tensor(xb[:], x[:], g["half_bias"][:].unsqueeze(1).to_broadcast([P, TPB, D]),
                                        ALU.add).then_inc(xb_ready, 1)

            with pool.Fori(0, NBLK) as i:
                ln_gpsimd(nc, pool, i, mv, s)
                biased(i)

        @block.vector
        def _(dve):
            def take_y(i):
                dve.wait_ge(xb_ready, i + 1)
                dve.wait_ge(stored, 16 * i)
                for j in range(TPB):
                    dve.wait_ge(y_ps_ready, TPB * i + j + 1)
                    nc.vector.scalar_tensor_tensor(out=y[:, j, :], in0=y_ps[j % 3], scalar=0.5,
                                                   in1=xb[:, j, :], op0=ALU.mult, op1=ALU.add)\
                        .then_inc(y_ready, 1)

            def hid_lows(i):
                for m in range(FM):
                    dve.wait_ge(hid_ready, 2 * (FM * i + m + 1))
                    low_part(nc.vector, hid_low[:, m, :], hid[:, m, :], hid_high[:, m, :]).then_inc(low_ready, 1)

            ln_vector(nc, dve, 0, x, xn, stat, mv, s)
            dve.wait_ge(w_high, 1)
            low_part(nc.vector, up_w[1][:], g["w_up"][:], up_w[0][:]).then_inc(w_low, 1)
            ln_low(nc, dve, 0, xT, xT_ps, s)
            dve.wait_ge(w_high, 2)
            low_part(nc.vector, down_w[1][:], g["w_down"][:], down_w[0][:]).then_inc(w_low, 1)
            with dve.Fori(0, LAST) as i:
                ln_vector(nc, dve, i + 1, x, xn, stat, mv, s)
                hid_lows(i)
                ln_low(nc, dve, i + 1, xT, xT_ps, s)
                take_y(i)
            hid_lows(LAST)
            take_y(LAST)

        @block.scalar
        def _(act):
            def take_xT(i):
                ln_high(nc, act, i, xT, xT_ps, s, h_ps_ready, FM * i)

            def gelu(i):
                act.wait_ge(low_ready, FM * i)
                act.wait_ge(y_ps_ready, TPB * i)
                for m in range(FM):
                    act.wait_ge(h_ps_ready, FM * i + m + 1)
                    for h in (hid_high, hid):
                        nc.scalar.activation(h[:, m, :], h_ps[m % 3][:], ACT.Gelu, bias=g["b_up"][:, m:m + 1],
                                             scale=1.0).then_inc(hid_ready, 1)

            for name, w in (("w_up", up_w), ("w_down", down_w)):
                nc.scalar.copy(w[0][:], g[name][:]).then_inc(w_high, 1)
            take_xT(0)
            with act.Fori(0, LAST) as i:
                gelu(i)
                take_xT(i + 1)
            gelu(LAST)

        @block.tensor
        def _(pe):
            def up(i):
                pe.wait_ge(s["xT_ready"], KD * (i + 1))
                for m in range(FM):
                    pe.wait_ge(hid_ready, 2 * (FM * i + max(m - 2, 0)))
                    for k in range(KD):
                        t = product(nc, h_ps[m % 3][:], [w[:, k, m * P:(m + 1) * P] for w in up_w],
                                    [v[:, k, :] for v in xT], k == 0, k == KD - 1)
                    t.then_inc(h_ps_ready, 1)

            def down(i):
                for j in range(TPB):
                    pe.wait_ge(y_ready, TPB * i + max(j - 2, 0))
                    for m in range(FM):
                        if j == 0:
                            pe.wait_ge(low_ready, FM * i + m + 1)
                        t = product(nc, y_ps[j % 3], [h[:, m, j * P:(j + 1) * P] for h in (hid_high, hid_low)],
                                    [w[:, m, :] for w in down_w], m == 0, m == FM - 1)
                    t.then_inc(y_ps_ready, 1)

            ln_transpose(nc, pe, 0, xn, xT_ps, g["ident"], s)
            pe.wait_ge(w_low, 2)
            with pe.Fori(0, LAST) as i:
                up(i)
                ln_transpose(nc, pe, i + 1, xn, xT_ps, g["ident"], s)
                down(i)
            up(LAST)
            down(LAST)



def inproj_block(nc, g, a, x_in, proj_T):
    with ExitStack() as ctx:
        r = Room(nc, ctx, "inp")
        x, xn, stat, mv, xT_ps, xT, s = ln_room(r)
        s["minus_half"] = g["minus_half"]
        NM = 2 * INNER // P
        w = r.sb("w", [P, KD, 2 * INNER])
        ws = [r.sb(f"w_{part}", [P, KD, 2 * INNER], F32R) for part in ("high", "low")]
        o = [r.sb(f"o{i}", [P, IB, BLK]) for i in range(2)]
        p_ps = [r.ps(f"p_ps{i}", [P, BLK]) for i in range(4)]
        w_in, w_high, w_low, p_ps_ready, o_ready, padded = (
            r.sem(n) for n in ("w_in", "w_high", "w_low", "p_ps_ready", "o_ready", "padded"))
        stored = [r.sem(f"stored{h}") for h in range(2)]
        block = ctx.enter_context(nc.Block())
        LAST = NBLK - 1
        BPB = NBLK // BATCH
        PARTS = [(0, BPB, 0), (BPB, LAST, 1)]

        @block.sync
        def _(sp):
            out3 = proj_T.rearrange("(k p) t -> p k t", p=P)

            def load(i):
                sp.dma_start(x[:], tiles(x_in, i)).then_inc(s["x_loaded"], 16)

            def store(i, b):
                for h in range(2):
                    sp.wait_ge(o_ready, NM * i + (h + 1) * IB)
                    sp.dma_start(out3[:, h * IB:(h + 1) * IB, bass.ds(i * BLK + (b * (TAPS - 1) + 1), BLK)], o[h][:])\
                        .then_inc(stored[h], 16)

            load(0)
            sp.dma_start(w[:], a["in_proj_T"].rearrange("(k p) n -> p k n", p=P)).then_inc(w_in, 16)
            for b in range(BATCH):
                z = g["zeros"][:, 0:IB * 2].rearrange("p (k t) -> p k t", k=IB)
                sp.dma_start(out3[:, 0:IB, b * HPAD:b * HPAD + 1], z[:, :, 0:1],
                             allow_slow_non_contiguous=True).then_inc(padded, 16)
                sp.dma_start(out3[:, 0:IB, b * HPAD + SEQ + 1:(b + 1) * HPAD], z).then_inc(padded, 16)
            for lo, hi, b in PARTS:
                with sp.Fori(lo, hi) as i:
                    sp.wait_ge(s["ln"], LN_OPS * (i + 1))
                    load(i + 1)
                    store(i, b)
            store(LAST, 1)
            sp.wait_ge(padded, 16 * 2 * BATCH)
            sp.wait_ge(stored[0], 16 * NBLK)
            sp.wait_ge(stored[1], 16 * NBLK)

        @block.gpsimd
        def _(pool):
            with pool.Fori(0, NBLK) as i:
                ln_gpsimd(nc, pool, i, mv, s)

        @block.vector
        def _(dve):
            ln_vector(nc, dve, 0, x, xn, stat, mv, s)
            dve.wait_ge(w_high, 1)
            low_part(nc.vector, ws[1][:], w[:], ws[0][:]).then_inc(w_low, 1)
            ln_low(nc, dve, 0, xT, xT_ps, s)
            with dve.Fori(1, NBLK) as i:
                ln_vector(nc, dve, i, x, xn, stat, mv, s)
                ln_low(nc, dve, i, xT, xT_ps, s)

        @block.scalar
        def _(act):
            def take_xT(i):
                ln_high(nc, act, i, xT, xT_ps, s, p_ps_ready, NM * i)

            def take(i):
                for m in range(NM):
                    if m % IB == 0:
                        act.wait_ge(stored[m // IB], 16 * i)
                    act.wait_ge(p_ps_ready, NM * i + m + 1)
                    if m < IB:
                        t = nc.scalar.copy(o[0][:, m, :], p_ps[m % 4][:])
                    else:
                        t = nc.scalar.activation(o[1][:, m - IB, :], p_ps[m % 4][:], ACT.Silu)
                    t.then_inc(o_ready, 1)

            act.wait_ge(w_in, 16)
            nc.scalar.copy(ws[0][:], w[:]).then_inc(w_high, 1)
            take_xT(0)
            with act.Fori(0, LAST) as i:
                take(i)
                take_xT(i + 1)
            take(LAST)

        @block.tensor
        def _(pe):
            def project(i):
                pe.wait_ge(s["xT_ready"], KD * (i + 1))
                for m in range(NM):
                    pe.wait_ge(o_ready, NM * i + max(m - 3, 0))
                    for k in range(KD):
                        t = product(nc, p_ps[m % 4][:], [v[:, k, m * P:(m + 1) * P] for v in ws],
                                    [v[:, k, :] for v in xT], k == 0, k == KD - 1)
                    t.then_inc(p_ps_ready, 1)

            pe.wait_ge(w_low, 1)
            ln_transpose(nc, pe, 0, xn, xT_ps, g["ident"], s)
            with pe.Fori(0, LAST) as i:
                project(i)
                ln_transpose(nc, pe, i + 1, xn, xT_ps, g["ident"], s)
            project(LAST)




def mamba_block(nc, g, a, x_in, proj_T, bc_T, x_out):
    with ExitStack() as ctx:
        r = Room(nc, ctx, "mam")
        QS = 4
        NQ = STATE // QS
        NG = NQ * IB
        conv_w = r.sb("conv_w", [P, IB, TAPS])
        conv_b = r.sb("conv_b", [P, IB])
        diag = r.sb("diag", [P, IB, TAPS, P])
        w_x = r.sb("w_x", [P, IB, XD])
        w_dt = r.sb("w_dt", [RANK, INNER])
        b_dt = r.sb("b_dt", [P, IB])
        ln_w = r.sb("ln_w", [XD, 1])
        skip = r.sb("skip", [P, IB])
        keep = r.sb("keep", [P, NBLK + 1])
        w_out = r.sb("w_out", [P, IB, D])
        hs = r.sb("hs", [P, IB, BLK + TAPS - 1])
        xsq = hs[:].rearrange("p k t -> p (k t)")[:, 0:TPB * XD].rearrange("p (j f) -> p j f", j=TPB)
        soft = hs[:, :, 0:BLK]
        u = [r.sb(f"u{b}", [P, IB, BLK]) for b in range(2)]
        dt = [r.sb(f"dt{b}", [P, IB, BLK]) for b in range(2)]
        dtu = r.sb("dtu", [P, IB, BLK])
        gate = [r.sb(f"gate{b}", [P, IB, BLK]) for b in range(2)]
        xd = r.sb("xd", [P, TPB, XD])
        ms = r.sb("ms", [P, 3, TPB])
        rms = r.sb("rms", [P, 3, TPB])
        xdT = r.sb("xdT", [XD, BLK])
        Bq = [r.sb(f"Bq{b}", [P, QS, BLK]) for b in range(2)]
        Cq = [r.sb(f"Cq{b}", [P, QS, BLK]) for b in range(2)]
        dA = [r.sb(f"dA{b}", [P, QS, BLK]) for b in range(2)]
        dBu = [r.sb(f"dBu{b}", [P, QS, BLK]) for b in range(2)]
        NH = 4
        h = [r.sb(f"h{b}", [P, QS, BLK]) for b in range(NH)]
        h_last = r.sb("h_last", [P, NG, QS])
        xr = r.sb("xr", [P, TPB, D])
        y_ps = [r.ps(f"y_ps{k}", [P, BLK]) for k in range(IB)]
        rot_ps = [r.ps(f"rot_ps{k}", [P, BLK]) for k in range(2)]
        xd_ps = r.ps("xd_ps", [P, TPB, P])
        xT_ps = r.ps("xT_ps", [P, BLK])
        names = ("w_in hs_in x_loaded conv_ps_ready u_ready xd_ps_ready norm rms_ready xT_ps_ready "
                 "xdT_ready bc_stored dt_ps_ready softened dtu_ready dA_ready dBu_ready scanned kept hC_ready "
                 "y_summed y_ready o_ps_ready o_ready stored diags").split()
        s = {n: r.sem(n) for n in names}
        gate_in = [r.sem(f"gate_in{b}") for b in range(2)]
        B_in = [r.sem(f"B_in{b}") for b in range(2)]
        C_in = [r.sem(f"C_in{b}") for b in range(2)]
        block = ctx.enter_context(nc.Block())
        LAST = NBLK - 1
        NORM = 9
        SOFT = 2 * IB + 2
        FIN = 2
        W_IN = 16 * 9
        out_ps = [xd_ps[:].rearrange("p j f -> p (j f)")[:, j * D:(j + 1) * D] for j in range(2)]
        AT = dict(conv=(0, 1, 2, 3), out=(10, 14), silu=(3, 5), x_proj=4, norms=6, pool_norms=8, scale=7, turn=7,
                  xdT=9, dt_proj=(8, 9), soften=(10, 11), soft_exp=11, soft_log=11, take_out=(12, 15))
        proj3 = proj_T.rearrange("(k p) t -> p k t", p=P)

        def wait(eng, name, value):
            if not (isinstance(value, int) and value <= 0):
                eng.wait_ge(s[name], value)

        def all_steps(eng, step, end):
            step(0, 0, True, False)
            with eng.Fori(0, (NBLK - 2) // 2) as i:
                step(i * 2 + 1, 1, False, False)
                step(i * 2 + 2, 0, False, False)
            step(LAST, LAST % 2, False, True)
            if end:
                end()

        @block.sync
        def _(sp):
            BPB = NBLK // BATCH

            def load_hs(n, b):
                wait(sp, "dtu_ready", 2 * IB * n)
                sp.dma_start(hs[:], proj3[:, 0:IB, bass.ds(n * BLK + b * (TAPS - 1), BLK + TAPS - 1)])\
                    .then_inc(s["hs_in"], 16)

            def load_quad(c, quad):
                G = c * NG + (quad - 2) * IB
                b = quad % 2
                rows = bc_T[quad * QS:quad * QS + QS, bass.ds(c * BLK + BLK, BLK)]
                wait(sp, "dBu_ready", G + IB)
                sp.dma_start(Bq[b][:], rows.partition_broadcast(P)).then_inc(B_in[b], 16)
                rows = bc_T[STATE + quad * QS:STATE + quad * QS + QS, bass.ds(c * BLK + BLK, BLK)]
                wait(sp, "hC_ready", G + IB)
                sp.dma_start(Cq[b][:], rows.partition_broadcast(P)).then_inc(C_in[b], 16)

            def store_bc(n):
                sp.wait_ge(s["xdT_ready"], n + 1)
                sp.dma_start(bc_T[:, bass.ds(n * BLK + BLK, BLK)], xdT[RANK:XD, :]).then_inc(s["bc_stored"], 16)

            def store_out(c):
                sp.wait_ge(s["o_ready"], TPB * (c + 1))
                sp.dma_start(tiles(x_out, c), xr[:]).then_inc(s["stored"], 16)

            def step(c):
                b = c // BPB
                if c == 0:
                    load_hs(1, 1 // BPB)
                wait(sp, "o_ps_ready", TPB * (c - 1))
                sp.dma_start(gate[c % 2][:], proj3[:, IB:2 * IB, bass.ds(c * BLK + b * (TAPS - 1) + 1, BLK)])\
                    .then_inc(gate_in[c % 2], 16)
                load_quad(c, 2)
                load_quad(c, 3)
                if c < LAST:
                    store_bc(c + 1)
                    sp.wait_ge(s["bc_stored"], 16 * (c + 2))
                    load_quad(c + 1, 0)
                if c:
                    store_out(c - 1)
                    sp.wait_ge(s["stored"], 16 * c)
                sp.dma_start(xr[:], tiles(x_in, c)).then_inc(s["x_loaded"], 16)
                if c < LAST - 1:
                    load_hs(c + 2, (c + 2) // BPB)
                if c < LAST:
                    load_quad(c + 1, 1)

            for dst, name in ((conv_w, "conv_w"), (w_x, "x_proj_T"), (w_out, "out_proj_T")):
                sp.dma_start(dst[:], a[name].rearrange("(k p) n -> p k n", p=P)).then_inc(s["w_in"], 16)
            for dst, name in ((conv_b, "conv_b"), (b_dt, "dt_bias"), (skip, "D")):
                sp.dma_start(dst[:], a[name]).then_inc(s["w_in"], 16)
            sp.dma_start(w_dt[:], a["dt_proj_T"]).then_inc(s["w_in"], 16)
            sp.dma_start(ln_w[:], a["xd_ln_w"]).then_inc(s["w_in"], 16)
            sp.dma_start(keep[:], a["keep"]).then_inc(s["w_in"], 16)
            load_hs(0, 0)
            store_bc(0)
            sp.wait_ge(s["bc_stored"], 16)
            load_quad(0, 0)
            load_quad(0, 1)
            for c in range(NBLK):
                step(c)
            store_out(LAST)
            sp.wait_ge(s["stored"], 16 * NBLK)

        @block.gpsimd
        def _(pool):
            def norms(n):
                pool.wait_ge(s["norm"], NORM * n + 7)
                nc.gpsimd.tensor_tensor(rms[:].rearrange("p g j -> p (g j)"), ms[:].rearrange("p g j -> p (g j)"),
                                        g["minus_half"][:, 0:3 * TPB], ALU.pow).then_inc(s["rms_ready"], 1)

            def make_dt(n, p, k):
                if k == 0:
                    pool.wait_ge(s["softened"], SOFT * (n + 1))
                nc.gpsimd.tensor_tensor(dt[p][:, k, :], dt[p][:, k, :], soft[:, k, :], ALU.add)\
                    .then_inc(s["dtu_ready"], 1)
                pool.wait_ge(s["dtu_ready"], 2 * (IB * n + k) + 1)
                wait(pool, "dBu_ready", NG * (n - 1) + NG - IB + k + 1)
                nc.gpsimd.tensor_tensor(dtu[:, k, :], dt[p][:, k, :], u[p][:, k, :], ALU.mult)\
                    .then_inc(s["dtu_ready"], 1)

            def step(c, q, first, last):
                for gi in range(NG):
                    k, quad, G = gi % IB, gi // IB, c * NG + gi
                    if gi % IB == 0:
                        pool.wait_ge(B_in[quad % 2], 16 * (2 * c + quad // 2 + 1))
                    if quad == 0:
                        pool.wait_ge(s["dtu_ready"], 2 * (IB * c + k + 1))
                    wait(pool, "scanned", QS * (G - 1))
                    nc.gpsimd.tensor_tensor(dBu[gi % 2][:], Bq[quad % 2][:],
                                            dtu[:, k:k + 1, :].to_broadcast([P, QS, BLK]), ALU.mult)\
                        .then_inc(s["dBu_ready"], 1)
                    if gi == AT["pool_norms"] and not last:
                        norms(c + 1)
                    if gi >= NG - IB and not last:
                        make_dt(c + 1, 1 - q, gi - (NG - IB))

            norms(0)
            for k in range(IB):
                make_dt(0, 0, k)
            all_steps(pool, step, None)

        @block.scalar
        def _(act):
            def make_u(n, p, half):
                if half == 0:
                    wait(act, "y_ready", FIN * IB * (n - 1))
                for k in (2 * half, 2 * half + 1):
                    act.wait_ge(s["conv_ps_ready"], IB * n + k + 1)
                    nc.scalar.activation(u[p][:, k, :], rot_ps[k % 2][:], ACT.Silu, bias=conv_b[:, k:k + 1],
                                         scale=1.0).then_inc(s["u_ready"], 1)

            def take_xdT(n):
                act.wait_ge(s["xT_ps_ready"], n + 1)
                wait(act, "dt_ps_ready", IB * n)
                wait(act, "bc_stored", 16 * n)
                nc.scalar.activation(xdT[:], xT_ps[0:XD, :], ACT.Copy, scale=ln_w[:, 0:1]).then_inc(s["xdT_ready"], 1)

            def soften(n, p, half):
                if half == 0:
                        act.wait_ge(s["norm"], NORM * n + 5)
                for k in (2 * half, 2 * half + 1):
                    act.wait_ge(s["dt_ps_ready"], IB * n + k + 1)
                    nc.scalar.activation(soft[:, k, :], rot_ps[k % 2][:], ACT.Abs, bias=b_dt[:, k:k + 1], scale=1.0)\
                        .then_inc(s["softened"], 1)
                    nc.scalar.activation(dt[p][:, k, :], rot_ps[k % 2][:], ACT.Relu, bias=b_dt[:, k:k + 1], scale=1.0)\
                        .then_inc(s["softened"], 1)

            def soft_exp(n):
                act.wait_ge(s["softened"], SOFT * n + 2 * IB)
                nc.scalar.activation(soft[:], soft[:], ACT.Exp, scale=-1.0).then_inc(s["softened"], 1)

            def soft_log(n):
                act.wait_ge(s["softened"], SOFT * n + 2 * IB + 1)
                nc.scalar.activation(soft[:], soft[:], ACT.Ln, bias=1.0).then_inc(s["softened"], 1)

            def step(c, q, first, last):
                for gi in range(NG):
                    k, quad, G = gi % IB, gi // IB, c * NG + gi
                    if quad == 0:
                        act.wait_ge(s["dtu_ready"], 2 * (IB * c + k) + 1)
                    wait(act, "scanned", QS * (G - 1))
                    for m in range(QS):
                        n = quad * QS + m
                        nc.scalar.activation(dA[gi % 2][:, m, :], dt[q][:, k, :], ACT.Exp,
                                             scale=g["neg_A"][:, k, n:n + 1]).then_inc(s["dA_ready"], 1)
                    if last:
                        continue
                    for half in range(2):
                        if gi == AT["silu"][half]:
                            make_u(c + 1, 1 - q, half)
                        if gi == AT["soften"][half]:
                            soften(c + 1, 1 - q, half)
                    if gi == AT["xdT"]:
                        take_xdT(c + 1)
                    if gi == AT["soft_exp"]:
                        soft_exp(c + 1)
                    if gi == AT["soft_log"]:
                        soft_log(c + 1)

            act.wait_ge(s["w_in"], W_IN)
            make_u(0, 0, 0)
            make_u(0, 0, 1)
            take_xdT(0)
            soften(0, 0, 0)
            soften(0, 0, 1)
            soft_exp(0)
            soft_log(0)
            all_steps(act, step, None)

        @block.vector
        def _(dve):
            def norms(n):
                dve.wait_ge(s["xd_ps_ready"], n + 1)
                wait(dve, "xT_ps_ready", n)
                nc.vector.tensor_copy(xd[:], xd_ps[:, :, 0:XD]).then_inc(s["norm"], 1)
                dve.wait_ge(s["norm"], NORM * n + 1)
                nc.vector.tensor_tensor(xsq, xd[:], xd[:], ALU.mult).then_inc(s["norm"], 1)
                dve.wait_ge(s["norm"], NORM * n + 2)
                for i, (lo, hi) in enumerate(((0, RANK), (RANK, RANK + STATE), (RANK + STATE, XD))):
                    nc.vector.tensor_reduce(ms[:, i, :], xsq[:, :, lo:hi], AX.X, ALU.add).then_inc(s["norm"], 1)
                dve.wait_ge(s["norm"], NORM * n + 5)
                nc.vector.tensor_scalar(ms[:, 0, :], ms[:, 0, :], 1.0 / RANK, RMS_EPS, ALU.mult, ALU.add)\
                    .then_inc(s["norm"], 1)
                nc.vector.tensor_scalar(ms[:, 1:3, :], ms[:, 1:3, :], 1.0 / STATE, RMS_EPS, ALU.mult, ALU.add)\
                    .then_inc(s["norm"], 1)

            def scale(n):
                dve.wait_ge(s["rms_ready"], n + 1)
                nc.vector.tensor_tensor(xd[:, :, 0:RANK], xd[:, :, 0:RANK],
                                        rms[:, 0, :].unsqueeze(2).to_broadcast([P, TPB, RANK]), ALU.mult)\
                    .then_inc(s["norm"], 1)
                bc = xd[:, :, RANK:XD].rearrange("p j (g n) -> p j g n", g=2)
                nc.vector.tensor_tensor(bc, bc, rms[:, 1:3, :].rearrange("p g j -> p j g").unsqueeze(3)
                                        .to_broadcast([P, TPB, 2, STATE]), ALU.mult).then_inc(s["norm"], 1)

            def finish(c, q, k, half):
                dve.wait_ge(s["y_summed"], NG * c + NG - IB + k + 1)
                nc.vector.scalar_tensor_tensor(out=u[q][:, k, :], in0=u[q][:, k, :], scalar=skip[:, k:k + 1],
                                               in1=y_ps[k][:], op0=ALU.mult, op1=ALU.add).then_inc(s["y_ready"], 1)
                dve.wait_ge(s["y_ready"], FIN * (IB * c + k) + 1)
                dve.wait_ge(gate_in[q], 16 * (half + 1))
                nc.vector.tensor_tensor(gate[q][:, k, :], u[q][:, k, :], gate[q][:, k, :], ALU.mult)\
                    .then_inc(s["y_ready"], 1)

            def take_out(c, pair):
                dve.wait_ge(s["x_loaded"], 16 * (c + 1))
                dve.wait_ge(s["o_ps_ready"], TPB * c + 2 * pair + 2)
                for j in (2 * pair, 2 * pair + 1):
                    nc.vector.tensor_tensor(xr[:, j, :], out_ps[j % 2], xr[:, j, :], ALU.add)\
                        .then_inc(s["o_ready"], 1)

            def step(c, q, first, last, half):
                for gi in range(NG):
                    k, quad, G = gi % IB, gi // IB, c * NG + gi
                    hb = h[gi % NH]
                    dve.wait_ge(s["dBu_ready"], G + 1)
                    wait(dve, "y_summed", G - NH + 1)
                    wait(dve, "kept", G)
                    for m in range(QS):
                        dve.wait_ge(s["dA_ready"], QS * G + m + 1)
                        nc.vector.tensor_tensor_scan(hb[:, m, :], dA[gi % 2][:, m, :], dBu[gi % 2][:, m, :],
                                                     h_last[:, gi, m:m + 1], ALU.mult, ALU.add)\
                            .then_inc(s["scanned"], 1)
                    dve.wait_ge(s["scanned"], QS * (G + 1))
                    nc.vector.tensor_tensor(h_last[:, gi, :], hb[:, :, BLK - 1], keep[:, bass.ds(c + 1, 1)]
                                            .to_broadcast([P, QS]), ALU.mult).then_inc(s["kept"], 1)
                    dve.wait_ge(s["kept"], G + 1)
                    dve.wait_ge(C_in[quad % 2], 16 * (2 * c + quad // 2 + 1))
                    nc.vector.tensor_tensor(hb[:], hb[:], Cq[quad % 2][:], ALU.mult).then_inc(s["hC_ready"], 1)
                    if gi == 0 and not first:
                        finish(c - 1, 1 - q, IB - 1, half if q else half - 1)
                    for pair in range(2):
                        if gi == AT["take_out"][pair] and not first:
                            take_out(c - 1, pair)
                    if gi == AT["norms"] and not last:
                        norms(c + 1)
                    if gi == AT["scale"] and not last:
                        scale(c + 1)
                    if gi >= NG - 3:
                        finish(c, q, gi - (NG - 3), half)

            def steps():
                step(0, 0, True, False, 0)
                with dve.Fori(0, (NBLK - 2) // 2) as i:
                    step(i * 2 + 1, 1, False, False, i)
                    step(i * 2 + 2, 0, False, False, i + 1)
                step(LAST, LAST % 2, False, True, LAST // 2)
                finish(LAST, LAST % 2, IB - 1, LAST // 2)
                take_out(LAST, 0)
                take_out(LAST, 1)

            dve.wait_ge(s["w_in"], W_IN)
            nc.vector.memset(h_last[:], 0.0).then_inc(s["diags"], 1)
            for k in range(IB):
                for tap in range(TAPS):
                    nc.vector.tensor_scalar(diag[:, k, tap, :], g["ident"][:], conv_w[:, k, tap:tap + 1], None,
                                            ALU.mult).then_inc(s["diags"], 1)
            dve.wait_ge(s["diags"], 1 + IB * TAPS)
            norms(0)
            scale(0)
            steps()

        @block.tensor
        def _(pe):
            def convolve(n, k):
                pe.wait_ge(s["hs_in"], 16 * (n + 1))
                if k >= 2:
                    pe.wait_ge(s["u_ready"], IB * n + k - 1)
                else:
                    wait(pe, "softened", SOFT * n)
                for tap in range(TAPS):
                    t = nc.tensor.matmul(rot_ps[k % 2][:], diag[:, k, tap, :], hs[:, k, tap:tap + BLK],
                                         start=(tap == 0), stop=(tap == TAPS - 1))
                t.then_inc(s["conv_ps_ready"], 1)

            def project_x(n, p):
                pe.wait_ge(s["u_ready"], IB * (n + 1))
                wait(pe, "norm", NORM * (n - 1) + 1)
                wait(pe, "o_ready", TPB * (n - 2))
                for j in range(TPB):
                    for k in range(IB):
                        t = nc.tensor.matmul(xd_ps[:, j, 0:XD], u[p][:, k, j * P:(j + 1) * P], w_x[:, k, :],
                                             start=(k == 0), stop=(k == IB - 1))
                t.then_inc(s["xd_ps_ready"], 1)

            def turn(n):
                pe.wait_ge(s["norm"], NORM * (n + 1))
                wait(pe, "xdT_ready", n)
                for j in range(TPB):
                    t = nc.tensor.transpose(xT_ps[0:XD, j * P:(j + 1) * P], xd[:, j, :], g["ident"][:])
                t.then_inc(s["xT_ps_ready"], 1)

            def project_dt(n, half):
                pe.wait_ge(s["xdT_ready"], n + 1)
                for k in (2 * half, 2 * half + 1):
                    if k < 2:
                        pe.wait_ge(s["u_ready"], IB * n + k + 3)
                    else:
                        pe.wait_ge(s["softened"], SOFT * n + 2 * (k - 1))
                    nc.tensor.matmul(rot_ps[k % 2][:], w_dt[:, k * P:(k + 1) * P], xdT[0:RANK, :],
                                     start=True, stop=True).then_inc(s["dt_ps_ready"], 1)

            def project_out(c, q, pair, last=False):
                pe.wait_ge(s["y_ready"], FIN * IB * (c + 1))
                pe.wait_ge(s["norm"], NORM * (LAST if last else c + 2) + 1)
                wait(pe, "o_ready", TPB * c + 2 * pair)
                for j in (2 * pair, 2 * pair + 1):
                    for k in range(IB):
                        t = nc.tensor.matmul(out_ps[j % 2], gate[q][:, k, j * P:(j + 1) * P], w_out[:, k, :],
                                             start=(k == 0), stop=(k == IB - 1))
                    t.then_inc(s["o_ps_ready"], 1)

            def step(c, q, first, last):
                for gi in range(NG):
                    k, quad, G = gi % IB, gi // IB, c * NG + gi
                    pe.wait_ge(s["hC_ready"], G + 1)
                    if quad == 0:
                        wait(pe, "y_ready", FIN * (IB * (c - 1) + k) + 1)
                    for m in range(QS):
                        t = nc.tensor.matmul(y_ps[k][:], g["ident"][:], h[gi % NH][:, m, :],
                                             start=(quad == 0 and m == 0), stop=(quad == NQ - 1 and m == QS - 1))
                    t.then_inc(s["y_summed"], 1)
                    for pair in range(2):
                        if gi == AT["out"][pair] and not first:
                            project_out(c - 1, 1 - q, pair, last)
                    if last:
                        continue
                    if gi in AT["conv"]:
                        convolve(c + 1, AT["conv"].index(gi))
                    if gi == AT["x_proj"]:
                        project_x(c + 1, 1 - q)
                    if gi == AT["turn"]:
                        turn(c + 1)
                    for half in range(2):
                        if gi == AT["dt_proj"][half]:
                            project_dt(c + 1, half)

            pe.wait_ge(s["diags"], 1 + IB * TAPS)
            for k in range(IB):
                convolve(0, k)
            project_x(0, 0)
            turn(0)
            project_dt(0, 0)
            project_dt(0, 1)
            all_steps(pe, step, None)
            project_out(LAST, LAST % 2, 0, True)
            project_out(LAST, LAST % 2, 1, True)



def route_block(nc, tag, g, a, x_in, slots_dram):
    with ExitStack() as ctx:
        r = Room(nc, ctx, tag)
        stat = r.sb("stat", [P, NT, 6])
        mv = r.sb("mv", [P, NT + 1, 2])
        rstd = r.sb("rstd", [P, NT])
        xT = [r.sb(f"xT{b}", [P, KD, BLK]) for b in range(2)]
        w = r.sb("w", [P, KD, NE])
        x = r.sb("x", [P, NT, D])
        logits = r.sb("logits", [P, NT, NE])
        e = r.sb("e", [P, NT, NE])
        t = r.sb("t", [P, NT, NE])
        hot = r.sb("hot", [P, TOPK, NT, NE])
        best = r.sb("best", [P, TOPK, NT])
        m = r.sb("m", [P, NT])
        rank = r.sb("rank", [P, NE])
        first_slot = r.sb("first_slot", [P, NE])
        outside = r.sb("outside", [P, TOPK, NT])
        earlier = r.sb("earlier", [P, P])
        ones = r.sb("ones", [P, P])
        total = r.sb("total", [P, TOPK, NT, NE])
        upto = r.sb("upto", [P, TOPK, NT, NE])
        place = r.sb("place", [P, NT, NE])
        loc = r.sb("loc", [P, NT])
        slot = r.sb("slot", [P, NT])
        fits = r.sb("fits", [P, TOPK, NT])
        put = r.sb("put", [P, TOPK, NT], I32)
        xT_ps = [r.ps(f"xT_ps{k}", [P, BLK]) for k in range(KD)]
        l_ps = [r.ps(f"l_ps{b}", [P, TPB, NE]) for b in range(2)]
        count_ps = [r.ps(f"count_ps{j}", [P, 2, NT, NE]) for j in range(TOPK)]
        before_ps, total_ps = ([c[:, n] for c in count_ps] for n in range(2))
        x_loaded = [r.sem(f"x{i}_loaded") for i in range(NBLK)]
        (w_in, stats, rstds, normed, xT_full, xT_taken, l_full, l_taken, cleared, rt, exped, chosen, counted, placed,
         scattered) = (r.sem(n) for n in ("w_in stats rstds normed xT_full xT_taken l_full l_taken cleared rt "
                                          "exped chosen counted placed scattered").split())
        block = ctx.enter_context(nc.Block())
        W_IN = 16 * 6
        NSTAT = 2 * TPB + 2

        def wait(eng, sem, value):
            if not (isinstance(value, int) and value <= 0):
                eng.wait_ge(sem, value)

        @block.sync
        def _(sp):
            for i in range(2):
                sp.dma_start(x[:, i * TPB:(i + 1) * TPB, :], tiles(x_in, i)).then_inc(x_loaded[i], 16)
            for dst, name in ((rank[:], "rank"), (first_slot[:], "first_slot"),
                              (outside[:].rearrange("p j t -> p (j t)"), "outside"),
                              (earlier[:], "earlier"), (ones[:], "ones")):
                sp.dma_start(dst, a[name]).then_inc(w_in, 16)
            sp.dma_start(w[:], a["gate_T"].rearrange("(k p) e -> p k e", p=P)).then_inc(w_in, 16)
            for i in range(2, NBLK):
                sp.dma_start(x[:, i * TPB:(i + 1) * TPB, :], tiles(x_in, i)).then_inc(x_loaded[i], 16)
            rows = slots_dram.rearrange("(c p q) d -> c p q d", p=P, q=4)
            for c in range(rows.shape[0]):
                sp.dma_start(rows[c], g["zeros"][:].unsqueeze(1).to_broadcast([P, 4, D])).then_inc(cleared, 16)

        @block.gpsimd
        def _(pool):
            for i in range(NBLK):
                pool.wait_ge(stats, NSTAT * (i + 1))
                nc.gpsimd.tensor_tensor(rstd[:, i * TPB:(i + 1) * TPB], mv[:, i * TPB:(i + 1) * TPB, 1],
                                        g["minus_half"][:, 0:TPB], ALU.pow).then_inc(rstds, 1)
            pool.wait_ge(cleared, 16 * (NE * CAP // (4 * P)))
            for j in range(TOPK):
                pool.wait_ge(placed, j + 1)
                for i in range(NT):
                    nc.gpsimd.indirect_dma_start(
                        out=slots_dram, out_offset=bass.IndirectOffsetOnAxis(ap=put[:, j, i:i + 1], axis=0),
                        in_=x[:, i, :], in_offset=None, bounds_check=NE * CAP - 1, oob_is_err=False)\
                        .then_inc(scattered, 16)
            pool.wait_ge(scattered, 16 * TOPK * NT)

        @block.vector
        def _(dve):
            def statistics(i):
                mine = range(i * TPB, (i + 1) * TPB)
                dve.wait_ge(x_loaded[i], 16)
                for j in mine:
                    nc.vector.bn_stats(stat[:, j, :], x[:, j, :]).then_inc(stats, 1)
                dve.wait_ge(stats, NSTAT * i + TPB)
                nc.vector.tensor_copy(mv[:, NT, :], stat[:, i * TPB, 0:2]).then_inc(stats, 1)
                for j in mine:
                    nc.vector.bn_aggr(mv[:, j, :], stat[:, j, :]).then_inc(stats, 1)
                dve.wait_ge(stats, NSTAT * i + 2 * TPB + 1)
                var = mv[:, i * TPB:(i + 1) * TPB, 1]
                nc.vector.tensor_scalar(var, var, LN_EPS, None, ALU.add).then_inc(stats, 1)

            def normalise(i):
                dve.wait_ge(rstds, i + 1)
                for j in range(i * TPB, (i + 1) * TPB):
                    ins = nc.vector.tensor_scalar(x[:, j, :], x[:, j, :], mv[:, j, 0:1], rstd[:, j:j + 1],
                                                  ALU.subtract, ALU.mult)
                ins.then_inc(normed, 1)

            def take_logits(i):
                dve.wait_ge(l_full, i + 1)
                nc.vector.tensor_copy(logits[:, i * TPB:(i + 1) * TPB, :], l_ps[i % 2][:]).then_inc(l_taken, 1)

            statistics(0)
            for i in range(NBLK):
                if i + 1 < NBLK:
                    statistics(i + 1)
                normalise(i)
                if i >= 2:
                    take_logits(i - 2)
            take_logits(NBLK - 2)
            take_logits(NBLK - 1)

            n = [0]

            def done(ins):
                ins.then_inc(rt, 1)
                n[0] += 1
                dve.wait_ge(rt, n[0])

            def over(v, k):
                return v.unsqueeze(2).to_broadcast([P, k, NE])

            def choose(j):
                done(nc.vector.tensor_reduce(best[:, j, :], e[:], AX.X, ALU.max))
                done(nc.vector.tensor_tensor(t[:], e[:], over(best[:, j, :], NT), ALU.is_equal))
                done(nc.vector.tensor_tensor(t[:], t[:], rank[:].unsqueeze(1).to_broadcast([P, NT, NE]), ALU.mult))
                done(nc.vector.tensor_reduce(m[:], t[:], AX.X, ALU.max))
                done(nc.vector.tensor_tensor(hot[:, j], t[:], over(m[:], NT), ALU.is_equal))
                nc.vector.sem_inc(chosen, 1)

            def place_all(j):
                dve.wait_ge(counted, 2 * (j + 1))
                done(nc.vector.tensor_copy(total[:, j], total_ps[j]))
                for ex in range(NE):
                    start = upto[:, 0, NT - 1, ex:ex + 1] if j else 0.0
                    ins = nc.vector.tensor_tensor_scan(upto[:, j, :, ex], ones[:, 0:NT], total[:, j, :, ex], start,
                                                       ALU.mult, ALU.add)
                    if ex == NE - 1:
                        done(ins)
                done(nc.vector.tensor_tensor(place[:], upto[:, j], total[:, j], ALU.subtract))
                done(nc.vector.tensor_tensor(place[:], place[:], before_ps[j], ALU.add))
                done(nc.vector.tensor_tensor(place[:], place[:], hot[:, j], ALU.mult))
                done(nc.vector.tensor_reduce(loc[:], place[:], AX.X, ALU.add))
                done(nc.vector.tensor_tensor(place[:], hot[:, j], first_slot[:].unsqueeze(1)
                                             .to_broadcast([P, NT, NE]), ALU.mult))
                done(nc.vector.tensor_reduce(slot[:], place[:], AX.X, ALU.add))
                done(nc.vector.tensor_tensor(slot[:], slot[:], loc[:], ALU.add))
                done(nc.vector.tensor_scalar(fits[:, j], loc[:], float(CAP), None, ALU.is_lt))
                done(nc.vector.tensor_tensor(slot[:], slot[:], fits[:, j], ALU.mult))
                done(nc.vector.tensor_copy(g["take"][:, j * NT:(j + 1) * NT], slot[:]))
                done(nc.vector.tensor_scalar(loc[:], fits[:, j], -1.0, 1.0, ALU.mult, ALU.add))
                done(nc.vector.tensor_tensor(loc[:], loc[:], outside[:, j], ALU.mult))
                done(nc.vector.tensor_tensor(loc[:], loc[:], slot[:], ALU.add))
                nc.vector.tensor_copy(put[:, j], loc[:]).then_inc(placed, 1)

            dve.wait_ge(l_taken, NBLK)
            dve.wait_ge(w_in, W_IN)
            done(nc.vector.tensor_reduce(m[:], logits[:], AX.X, ALU.max))
            done(nc.vector.tensor_tensor(e[:], logits[:], over(m[:], NT), ALU.subtract))
            dve.wait_ge(exped, 1)
            done(nc.vector.tensor_reduce(m[:], e[:], AX.X, ALU.add))
            done(nc.vector.reciprocal(m[:], m[:]))
            done(nc.vector.tensor_tensor(e[:], e[:], over(m[:], NT), ALU.mult))
            choose(0)
            done(nc.vector.scalar_tensor_tensor(out=e[:], in0=hot[:, 0], scalar=-2.0, in1=e[:],
                                                op0=ALU.mult, op1=ALU.add))
            place_all(0)
            choose(1)
            done(nc.vector.tensor_tensor(m[:], best[:, 0, :], best[:, 1, :], ALU.add))
            done(nc.vector.reciprocal(m[:], m[:]))
            dve.wait_ge(placed, 1)
            place_all(1)
            share = g["share"][:].rearrange("p (j t) -> p j t", j=TOPK)
            done(nc.vector.tensor_tensor(share, best[:], m[:].unsqueeze(1).to_broadcast([P, TOPK, NT]), ALU.mult))
            done(nc.vector.scalar_tensor_tensor(out=share, in0=share, scalar=0.5, in1=fits[:],
                                                op0=ALU.mult, op1=ALU.mult))

        @block.scalar
        def _(act):
            for i in range(NBLK):
                wait(act, l_full, i - 1)
                for k in range(KD):
                    act.wait_ge(xT_full, KD * i + k + 1)
                    nc.scalar.copy(xT[i % 2][:, k, :], xT_ps[k][:]).then_inc(xT_taken, 1)
            act.wait_ge(rt, 2)
            nc.scalar.activation(e[:], e[:], ACT.Exp).then_inc(exped, 1)

        @block.tensor
        def _(pe):
            def turn(i):
                pe.wait_ge(normed, i + 1)
                wait(pe, xT_taken, KD * i)
                for k in range(KD):
                    for j in range(TPB):
                        ins = nc.tensor.transpose(xT_ps[k][:, j * P:(j + 1) * P],
                                                  x[:, i * TPB + j, k * P:(k + 1) * P], g["ident"][:])
                    ins.then_inc(xT_full, 1)

            def gate(i):
                pe.wait_ge(xT_taken, KD * (i + 1))
                wait(pe, l_taken, i - 1)
                for j in range(TPB):
                    for k in range(KD):
                        ins = nc.tensor.matmul(l_ps[i % 2][:, j, :], xT[i % 2][:, k, j * P:(j + 1) * P], w[:, k, :],
                                               start=(k == 0), stop=(k == KD - 1))
                ins.then_inc(l_full, 1)

            pe.wait_ge(w_in, W_IN)
            turn(0)
            for i in range(NBLK):
                if i + 1 < NBLK:
                    turn(i + 1)
                gate(i)
            for j in range(TOPK):
                pe.wait_ge(chosen, j + 1)
                nc.tensor.matmul(before_ps[j], earlier[:], hot[:, j], start=True, stop=True).then_inc(counted, 1)
                nc.tensor.matmul(total_ps[j], ones[:], hot[:, j], start=True, stop=True).then_inc(counted, 1)


def expert_block(nc, tag, g, a, slots_dram, done_dram):
    with ExitStack() as ctx:
        r = Room(nc, ctx, tag)
        w1 = r.sb("w1", [P, KD, EH])
        w2 = r.sb("w2", [P, EM, D])
        parts = ("high", "low")
        w1s = [[r.sb(f"w1_{n}{b}", [P, KD, EH], F32R) for n in parts] for b in range(2)]
        w2s = [[r.sb(f"w2_{n}{b}", [P, EM, D], F32R) for n in parts] for b in range(2)]
        b1 = r.sb("b1", [P, EM])
        b2 = r.sb("b2", [P, D])
        x = r.sb("x", [P, TPB, D])
        xT = [r.sb(f"xT_{n}", [P, KD, HALF], F32R) for n in parts]
        hid = r.sb("hid", [P, EM, HALF])
        hid_high, hid_low = (r.sb(f"hid_{n}", [P, EM, HALF], F32R) for n in parts)
        y = r.sb("y", [P, TPB, D])
        xT_ps = [r.ps(f"xT_ps{k}", [P, HALF]) for k in range(KD)]
        h_ps = [r.ps(f"h_ps{i}", [P, HALF]) for i in range(3)]
        y_ps = [r.ps(f"y_ps{i}", [P, BLK])[:, 0:D] for i in range(3)]
        names = ("w1_in w2_in b1_in b2_in w1_high w1_split w2_high w2_split x_in xT_ps_ready xT_high xT_ready "
                 "h_ps_ready hid_ready low_ready y_ps_ready y_ready stored").split()
        s = {n: r.sem(n) for n in names}
        block = ctx.enter_context(nc.Block())
        STEPS = NE * HPE

        def on(eng, name, value):
            if not (isinstance(value, int) and value <= 0):
                eng.wait_ge(s[name], value)

        @block.sync
        def _(sp):
            w1_v = a["fc1_T"].rearrange("(k p) n -> p k n", p=P)
            w2_v = a["fc2"].rearrange("(m p) d -> p m d", p=P)

            def load_w1(e):
                on(sp, "w1_split", e)
                sp.dma_start(w1[:], w1_v[:, :, bass.ds(e * EH, EH)]).then_inc(s["w1_in"], 16)

            def load_w2(e):
                on(sp, "w2_split", e)
                sp.dma_start(w2[:], w2_v[:, bass.ds(e * EM, EM), :]).then_inc(s["w2_in"], 16)

            def load_b1(e):
                on(sp, "hid_ready", 2 * EM * HPE * e)
                sp.dma_start(b1[:], a["b1"][bass.ds(e * P, P), :]).then_inc(s["b1_in"], 16)

            def load_b2(e):
                on(sp, "y_ready", TPB * HPE * e)
                sp.dma_start(b2[:], a["b2"][bass.ds(e * D, D)].partition_broadcast(P)).then_inc(s["b2_in"], 16)

            def load_x(i):
                on(sp, "xT_ps_ready", KD * i)
                sp.dma_start(x[:], tiles(slots_dram, i)).then_inc(s["x_in"], 16)

            def store(i):
                sp.wait_ge(s["y_ready"], TPB * (i + 1))
                sp.dma_start(tiles(done_dram, i), y[:]).then_inc(s["stored"], 16)

            load_w1(0)
            load_x(0)
            load_b1(0)
            load_w2(0)
            load_b2(0)
            with sp.Fori(0, NE - 1) as e:
                load_x(e * HPE + 1)
                load_w1(e + 1)
                load_w2(e + 1)
                store(e * HPE)
                load_x(e * HPE + 2)
                load_b1(e + 1)
                store(e * HPE + 1)
                load_b2(e + 1)
            load_x(STEPS - 1)
            store(STEPS - 2)
            store(STEPS - 1)
            sp.wait_ge(s["stored"], 16 * STEPS)

        @block.gpsimd
        def _(pool):
            def split(e, p, n, raw, halves, used, per):
                pool.wait_ge(s[f"{n}_in"], 16 * (e + 1))
                on(pool, used, per * (e - 1))
                flat = "p a b -> p (a b)"
                high, low, raw = (t[:].rearrange(flat) for t in (*halves[p], raw))
                nc.gpsimd.tensor_tensor(high, raw, g["zeros"][:, 0:1].to_broadcast(list(raw.shape)), ALU.add)\
                    .then_inc(s[f"{n}_high"], 1)
                pool.wait_ge(s[f"{n}_high"], e + 1)
                low_part(nc.gpsimd, low, raw, high).then_inc(s[f"{n}_split"], 1)

            def expert(e, p):
                split(e, p, "w1", w1, w1s, "h_ps_ready", EM * HPE)
                split(e, p, "w2", w2, w2s, "y_ps_ready", TPB * HPE)

            split(0, 0, "w2", w2, w2s, "y_ps_ready", TPB * HPE)
            with pool.Fori(0, NE // 2 - 1) as j:
                expert(j * 2 + 1, 1)
                expert(j * 2 + 2, 0)
            expert(NE - 1, 1)

        @block.tensor
        def _(pe):
            def turn(i):
                pe.wait_ge(s["x_in"], 16 * (i + 1))
                on(pe, "xT_ready", KD * i)
                for k in range(KD):
                    for j in range(TPB):
                        t = nc.tensor.transpose(xT_ps[k][:, j * P:(j + 1) * P], x[:, j, k * P:(k + 1) * P],
                                                g["ident"][:])
                    t.then_inc(s["xT_ps_ready"], 1)

            def up(i, e, p):
                pe.wait_ge(s["xT_ready"], KD * (i + 1))
                pe.wait_ge(s["w1_split"], e + 1)
                for m in range(EM):
                    on(pe, "hid_ready", 2 * (EM * i + max(m - 2, 0)))
                    for k in range(KD):
                        t = product(nc, h_ps[m % 3][:], [w[:, k, m * P:(m + 1) * P] for w in w1s[p]],
                                    [v[:, k, :] for v in xT], k == 0, k == KD - 1)
                    t.then_inc(s["h_ps_ready"], 1)

            def down(i, e, p):
                pe.wait_ge(s["w2_split"], e + 1)
                for j in range(TPB):
                    on(pe, "y_ready", TPB * i + max(j - 2, 0))
                    for m in range(EM):
                        if j == 0:
                            pe.wait_ge(s["low_ready"], EM * i + m + 1)
                        t = product(nc, y_ps[j % 3], [h[:, m, j * P:(j + 1) * P] for h in (hid_high, hid_low)],
                                    [w[:, m, :] for w in w2s[p]], m == 0, m == EM - 1)
                    t.then_inc(s["y_ps_ready"], 1)

            def expert(e, p, last=False):
                up(e * HPE, e, p)
                turn(e * HPE + 1)
                down(e * HPE, e, p)
                up(e * HPE + 1, e, p)
                if not last:
                    turn(e * HPE + 2)
                down(e * HPE + 1, e, p)

            turn(0)
            expert(0, 0)
            with pe.Fori(0, NE // 2 - 1) as j:
                expert(j * 2 + 1, 1)
                expert(j * 2 + 2, 0)
            expert(NE - 1, 1, True)

        @block.scalar
        def _(act):
            def high_xT(i):
                for k in range(KD):
                    act.wait_ge(s["xT_ps_ready"], KD * i + k + 1)
                    on(act, "h_ps_ready", EM * i)
                    nc.scalar.copy(xT[0][:, k, :], xT_ps[k][:]).then_inc(s["xT_high"], 1)

            def relu(i, e):
                on(act, "low_ready", EM * i)
                on(act, "y_ps_ready", TPB * i)
                act.wait_ge(s["b1_in"], 16 * (e + 1))
                for m in range(EM):
                    act.wait_ge(s["h_ps_ready"], EM * i + m + 1)
                    for h in (hid_high, hid):
                        nc.scalar.activation(h[:, m, :], h_ps[m % 3][:], ACT.Relu, bias=b1[:, m:m + 1], scale=1.0)\
                            .then_inc(s["hid_ready"], 1)

            def expert(e, last=False):
                relu(e * HPE, e)
                high_xT(e * HPE + 1)
                relu(e * HPE + 1, e)
                if not last:
                    high_xT(e * HPE + 2)

            act.wait_ge(s["w1_in"], 16)
            nc.scalar.copy(w1s[0][0][:], w1[:]).then_inc(s["w1_high"], 1)
            high_xT(0)
            with act.Fori(0, NE - 1) as e:
                expert(e)
            expert(NE - 1, True)

        @block.vector
        def _(dve):
            def low_xT(i):
                for k in range(KD):
                    dve.wait_ge(s["xT_high"], KD * i + k + 1)
                    low_part(nc.vector, xT[1][:, k, :], xT_ps[k][:], xT[0][:, k, :]).then_inc(s["xT_ready"], 1)

            def low_hid(i):
                for m in range(EM):
                    dve.wait_ge(s["hid_ready"], 2 * (EM * i + m + 1))
                    low_part(nc.vector, hid_low[:, m, :], hid[:, m, :], hid_high[:, m, :]).then_inc(s["low_ready"], 1)

            def take_y(i, e):
                dve.wait_ge(s["b2_in"], 16 * (e + 1))
                on(dve, "stored", 16 * i)
                for j in range(TPB):
                    dve.wait_ge(s["y_ps_ready"], TPB * i + j + 1)
                    nc.vector.tensor_tensor(y[:, j, :], y_ps[j % 3], b2[:], ALU.add).then_inc(s["y_ready"], 1)

            def expert(e, last):
                low_hid(e * HPE)
                low_xT(e * HPE + 1)
                take_y(e * HPE, e)
                low_hid(e * HPE + 1)
                if not last:
                    low_xT(e * HPE + 2)
                take_y(e * HPE + 1, e)

            dve.wait_ge(s["w1_high"], 1)
            low_part(nc.vector, w1s[0][1][:], w1[:], w1s[0][0][:]).then_inc(s["w1_split"], 1)
            low_xT(0)
            with dve.Fori(0, NE - 1) as e:
                expert(e, False)
            expert(NE - 1, True)


def combine_block(nc, tag, g, x_in, done_dram, x_out):
    with ExitStack() as ctx:
        r = Room(nc, ctx, tag)
        NB = 4
        x = [r.sb(f"x{b}", [P, TPB, D]) for b in range(2)]
        got = [[r.sb(f"got{j}_{b}", [P, D]) for b in range(NB)] for j in range(TOPK)]
        x_loaded = [r.sem(f"x_loaded{b}") for b in range(2)]
        stored = [r.sem(f"stored{b}") for b in range(2)]
        fetched = [r.sem(f"fetched{b}") for b in range(NB)]
        added = r.sem("added")
        block = ctx.enter_context(nc.Block())

        @block.sync
        def _(sp):
            def load(i):
                if i >= 2:
                    sp.wait_ge(stored[i % 2], 16 * (i // 2))
                sp.dma_start(x[i % 2][:], tiles(x_in, i)).then_inc(x_loaded[i % 2], 16)

            load(0)
            load(1)
            for i in range(NBLK):
                sp.wait_ge(added, 2 * TPB * (i + 1))
                sp.dma_start(tiles(x_out, i), x[i % 2][:]).then_inc(stored[i % 2], 16)
                if i + 2 < NBLK:
                    load(i + 2)
            for b in range(2):
                sp.wait_ge(stored[b], 16 * (NBLK // 2))

        @block.gpsimd
        def _(pool):
            for i in range(NT):
                if i >= NB:
                    pool.wait_ge(added, 2 * (i - NB + 1))
                for j in range(TOPK):
                    c = j * NT + i
                    nc.gpsimd.indirect_dma_start(
                        out=got[j][i % NB][:], out_offset=None, in_=done_dram,
                        in_offset=bass.IndirectOffsetOnAxis(ap=g["take"][:, c:c + 1], axis=0),
                        bounds_check=NE * CAP - 1, oob_is_err=True).then_inc(fetched[i % NB], 16)

        @block.vector
        def _(dve):
            for i in range(NT):
                b, t = i // TPB % 2, i % TPB
                dve.wait_ge(x_loaded[b], 16 * (i // TPB // 2 + 1))
                dve.wait_ge(fetched[i % NB], 32 * (i // NB + 1))
                for j in range(TOPK):
                    c = j * NT + i
                    if j:
                        dve.wait_ge(added, 2 * i + 1)
                    nc.vector.scalar_tensor_tensor(out=x[b][:, t, :], in0=got[j][i % NB][:],
                                                   scalar=g["share"][:, c:c + 1], in1=x[b][:, t, :],
                                                   op0=ALU.mult, op1=ALU.add).then_inc(added, 1)



SPAD = SEQ + P
GH = 4
NGR = HEADS // GH


def qkv_block(nc, g, a, qkv, x_in, done_dram, x_out, q_parts, k_parts):
    with ExitStack() as ctx:
        r = Room(nc, ctx, "qkv")
        x, xn, stat, mv, xT_ps, xT, s = ln_room(r)
        s["minus_half"] = g["minus_half"]
        w = {n: r.sb(n, [P, KD, D]) for n in ("wq_T", "wk_T", "wv_T")}
        ws = {n: [r.sb(f"{n}_{part}", [P, KD, D], F32R) for part in ("high", "low")] for n in w}
        qk_ps = [r.ps(f"qk_ps{i}", [P, BLK]) for i in range(2 * KD)]
        v_ps = [r.ps(f"v_ps{i}", [P, 2, D]) for i in range(TPB // 2)]
        got = [[[r.sb(f"got{b}_{j}_{c}", [P, D]) for c in range(TPB)] for j in range(TOPK)] for b in range(2)]
        share = r.sb("share", [P, TOPK, TPB])
        fetched = [r.sem(f"fetched{b}") for b in range(2)]
        combined, x_stored, shares = (r.sem(n) for n in ("combined", "x_stored", "shares"))
        norm_sems = dict(s, x_loaded=combined)
        high, low = (r.sb(n, [P, 2 * KD, BLK], F32R) for n in ("high", "low"))
        stored = [r.sem(f"{n}_stored") for n in ("q", "k")]
        pad_stored, qk_low = r.sem("pad_stored"), r.sem("qk_low")
        w_in, w_high, w_low, qk_full, qk_taken, v_full, v_taken, padded = (
            r.sem(n) for n in ("w_in", "w_high", "w_low", "qk_full", "qk_taken", "v_full", "v_taken", "padded"))
        block = ctx.enter_context(nc.Block())
        LAST = NBLK - 1
        BPB = NBLK // BATCH
        PARTS = [(0, BPB, 0), (BPB, LAST, 1)]
        NV = TPB // 2

        @block.sync
        def _(sp):
            sp.dma_start(x[:], tiles(x_in, 0)).then_inc(s["x_loaded"], 16)
            for name, t in w.items():
                sp.dma_start(t[:], a[name].rearrange("(k p) n -> p k n", p=P)).then_inc(w_in, 16)
            for b in range(BATCH):
                for c in range(2 * D // P):
                    sp.dma_start(k_parts[c * P:(c + 1) * P, b * SPAD:b * SPAD + P],
                                 g["zeros"][:, 0:P]).then_inc(pad_stored, 16)

            def store(i, b):
                for n, dram, pad, order in ((0, q_parts, 0, (high, low, high)), (1, k_parts, (b + 1) * P, (high, low))):
                    sp.wait_ge(qk_low, 2 * KD * i + (n + 1) * KD)
                    rows = dram.rearrange("(f h s d) t -> f s h d t", f=KD, s=len(order), d=HD)
                    for f in range(KD):
                        for j, part in enumerate(order):
                            sp.dma_start(rows[f, j][:, :, bass.ds(i * BLK + pad, BLK)], part[:, n * KD + f, :].bitcast(F32))\
                                .then_inc(stored[n], 16)

            def store_x(i):
                sp.wait_ge(combined, 16 * (i + 1))
                sp.dma_start(tiles(x_out, i), x[:]).then_inc(x_stored, 16)

            store_x(0)
            for lo, hi, b in PARTS:
                with sp.Fori(lo, hi) as i:
                    store_x(i + 1)
                    store(i, b)
            store(LAST, 1)
            sp.wait_ge(x_stored, 16 * NBLK)
            sp.wait_ge(pad_stored, 16 * BATCH * 2 * D // P)
            for n in range(2):
                sp.wait_ge(stored[n], 16 * NBLK * KD * (3 - n))

        @block.gpsimd
        def _(pool):
            for b in range(BATCH):
                nc.gpsimd.memset(qkv["v"][:, b * (QT + 1), :], 0.0).then_inc(padded, 1)
            def fetch(i):
                if i >= 2:
                    pool.wait_ge(combined, 16 * (i - 1))
                for c in range(TPB):
                    for j in range(TOPK):
                        n = j * NT + i * TPB + c
                        nc.gpsimd.indirect_dma_start(
                            out=got[i % 2][j][c][:], out_offset=None, in_=done_dram,
                            in_offset=bass.IndirectOffsetOnAxis(ap=g["take"][:, n:n + 1], axis=0),
                            bounds_check=NE * CAP - 1, oob_is_err=True).then_inc(fetched[i % 2], 16)

            fetch(0)
            fetch(1)
            for i in range(NBLK):
                ln_gpsimd(nc, pool, i, mv, s)
                if i + 2 < NBLK:
                    fetch(i + 2)
            pool.wait_ge(padded, BATCH)

        @block.vector
        def _(dve):
            def lows(i):
                for m in range(2 * KD):
                    dve.wait_ge(qk_taken, 2 * KD * i + m + 1)
                    dve.wait_ge(stored[m // KD], 16 * KD * (3 - m // KD) * i)
                    low_part(nc.vector, low[:, m, :], qk_ps[m][:], high[:, m, :]).then_inc(qk_low, 1)

            def take_v(i, b):
                for m in range(NV):
                    dve.wait_ge(v_full, NV * i + m + 1)
                    nc.vector.tensor_copy(qkv["v"][:, bass.ds(i * TPB + (b + 1 + 2 * m), 2), :], v_ps[m][:])\
                        .then_inc(v_taken, 1)

            def combine(i, p, half):
                dve.wait_ge(s["x_loaded"], 16 * (i + 1))
                dve.wait_ge(fetched[p], 16 * TOPK * TPB * (half + 1))
                for j in range(TOPK):
                    if j:
                        dve.wait_ge(combined, 16 * i + 8)
                    for c in range(TPB):
                        nc.vector.scalar_tensor_tensor(
                            out=x[:, c, :], in0=got[p][j][c][:], scalar=share[:, j, c:c + 1], in1=x[:, c, :],
                            op0=ALU.mult, op1=ALU.add).then_inc(combined, 2)

            def prepare(i):
                wanted = g["share"][:].rearrange("p (j t) -> p j t", j=TOPK)[:, :, bass.ds(i * TPB, TPB)]
                nc.vector.tensor_copy(share[:], wanted).then_inc(shares, 1)
                dve.wait_ge(shares, i + 1)

            prepare(0)
            combine(0, 0, 0)
            ln_vector(nc, dve, 0, x, xn, stat, mv, norm_sems)
            dve.wait_ge(w_high, 3)
            for name, t in w.items():
                low_part(nc.vector, ws[name][1][:], t[:], ws[name][0][:]).then_inc(w_low, 1)
            ln_low(nc, dve, 0, xT, xT_ps, s)
            def step(i, b, p, half):
                prepare(i + 1)
                combine(i + 1, p, half)
                ln_vector(nc, dve, i + 1, x, xn, stat, mv, norm_sems)
                lows(i)
                take_v(i, b)
                ln_low(nc, dve, i + 1, xT, xT_ps, s)

            with dve.Fori(0, BPB // 2) as h:
                step(h * 2, 0, 1, h)
                step(h * 2 + 1, 0, 0, h + 1)
            for i in range(BPB, LAST):
                step(i, 1, (i + 1) % 2, (i + 1) // 2)
            lows(LAST)
            take_v(LAST, 1)

        @block.scalar
        def _(act):
            def take_xT(i):
                ln_high(nc, act, i, xT, xT_ps, s, v_full, NV * i)

            def take_qk(i, b):
                for m in range(2 * KD):
                    act.wait_ge(qk_full, 2 * KD * i + m + 1)
                    if m < KD:
                        nc.scalar.copy(qkv["qT"][:, m, bass.ds(i * BLK, BLK)], qk_ps[m][:])
                    else:
                        nc.scalar.copy(qkv["kS"][:, m - KD, bass.ds(i * (BLK // SPARSE), BLK // SPARSE)],
                                       qk_ps[m][:, 0:BLK:SPARSE])
                    act.wait_ge(stored[m // KD], 16 * KD * (3 - m // KD) * i)
                    nc.scalar.copy(high[:, m, :], qk_ps[m][:]).then_inc(qk_taken, 1)

            def load_x(i):
                act.wait_ge(s["ln"], LN_OPS * i)
                act.wait_ge(x_stored, 16 * i)
                act.dma_start(x[:], tiles(x_in, i)).then_inc(s["x_loaded"], 16)

            act.wait_ge(w_in, 16 * 3)
            for name, t in w.items():
                nc.scalar.copy(ws[name][0][:], t[:]).then_inc(w_high, 1)
            take_xT(0)
            load_x(1)
            with act.Fori(0, BPB) as i:
                take_qk(i, 0)
                take_xT(i + 1)
                load_x(i + 2)
            with act.Fori(BPB, LAST - 1) as i:
                take_qk(i, 1)
                take_xT(i + 1)
                load_x(i + 2)
            take_qk(LAST - 1, 1)
            take_xT(LAST)
            take_qk(LAST, 1)

        @block.tensor
        def _(pe):
            def project(i, first):
                pe.wait_ge(s["xT_ready"], KD * (i + 1))
                for m in range(2 * KD):
                    if not first:
                        pe.wait_ge(qk_low, 2 * KD * (i - 1) + m + 1)
                    name, f = ("wq_T", "wk_T")[m // KD], m % KD
                    for k in range(KD):
                        t = product(nc, qk_ps[m][:], [v[:, k, f * P:(f + 1) * P] for v in ws[name]],
                                    [v[:, k, :] for v in xT], k == 0, k == KD - 1)
                    t.then_inc(qk_full, 1)
                for m in range(NV):
                    if not first:
                        pe.wait_ge(v_taken, NV * (i - 1) + m + 1)
                    for j in range(2):
                        c = 2 * m + j
                        for k in range(KD):
                            t = product(nc, v_ps[m][:, j, :], [v[:, k, c * P:(c + 1) * P] for v in xT],
                                        [v[:, k, :] for v in ws["wv_T"]], k == 0, k == KD - 1)
                    t.then_inc(v_full, 1)

            pe.wait_ge(w_low, 3)
            ln_transpose(nc, pe, 0, xn, xT_ps, g["ident"], s)
            project(0, True)
            with pe.Fori(1, NBLK) as i:
                ln_transpose(nc, pe, i, xn, xT_ps, g["ident"], s)
                project(i, False)


def attend_block(nc, g, a, qkv, q_parts, k_parts, x_in, x_out):
    with ExitStack() as ctx:
        r = Room(nc, ctx, "att")
        W2 = 2 * P
        wo_T = r.sb("wo_T", [P, KD, D])
        hmask = r.sb("hmask", [P, HPB])
        vmask = r.sb("vmask", [P, GH * HD])
        identb = r.sb("identb", [P, P], BF16)
        wmask = r.sb("wmask", [P, 2, 2 * W2], BF16)
        smask = r.sb("smask", [P, QT * NSTR], BF16)
        ones = r.sb("ones", [P, P], BF16)
        xr = r.sb("xr", [P, D])
        q = [r.sb(f"q{b}", [P, KD, P]) for b in range(2)]
        qz = [r.sb(f"qz{b}", [P, HEADS // 2, 2, P], F32R) for b in range(2)]
        Kw = [r.sb(f"Kw{b}", [P, HEADS // 2, W2], F32R) for b in range(2)]
        Ks = [r.sb(f"Ks{b}", [P, KD, HPB, NSTR]) for b in range(BATCH)]
        vrows = [r.sb(f"vrows{b}", [P, NGR, GH * HD]) for b in range(BATCH)]
        Vs = [r.sb(f"Vs{b}", [P, NGR, GH * HD]) for b in range(BATCH)]
        top_s = r.sb("top_s", [P, HEADS])
        top_w = r.sb("top_w", [P, HEADS])
        shift_s = r.sb("shift_s", [P, HEADS])
        shift = r.sb("shift", [P, HEADS])
        den = [r.sb(f"den{b}", [P, HEADS]) for b in range(2)]
        den_s = r.sb("den_s", [P, HEADS])
        rden = r.sb("rden", [P, HEADS])
        probs = [r.sb(f"probs{b}", [P, GH, W2]) for b in range(NGR)]
        str_in = r.sb("str_in", [P, HEADS * NSTR])
        probs_s = r.sb("probs_s", [P, HEADS * NSTR])
        PT = [r.sb(f"PT{b}", [P, 2, GH, P]) for b in range(2)]
        PTs = r.sb("PTs", [P, NGR, P])
        on = r.sb("on", [P, D])
        OT = r.sb("OT", [P, KD, P])
        o = r.sb("o", [P, D])
        S_ps = [r.ps(f"S_ps{b}", [P, GH, W2]) for b in range(2)]
        Ss_ps = r.ps("Ss_ps", [P, BLK])
        T_ps = [r.ps(f"T_ps{b}", [P, BLK]) for b in range(2)]
        O_ps = r.ps("O_ps", [P, BLK])
        names = ("w_in vrows_in Ks_ready Vs_ready q_ready zeroed Ss_ready S_ready top_s_ready shift_s_ready "
                 "tops shifts exp_done str_shifted str_exp str_turned PTs_taken turned0 turned1 PT0_taken "
                 "PT1_taken PV_done O_ready sums dens on_ready O_turned OT_taken out_ready o_ready xr_in "
                 "stored").split()
        s = {n: r.sem(n) for n in names}
        qk_in = [r.sem(f"qk_in{b}") for b in range(2)]
        block = ctx.enter_context(nc.Block())
        LAST = NT - 1
        N_IN = 7
        QK_IN = 16 * 8

        def wait(eng, name, value):
            if not (isinstance(value, int) and value <= 0):
                eng.wait_ge(s[name], value)

        def all_tiles(eng, tile):
            for b in range(BATCH):
                tile(b * QT, 0, b)
                with eng.Fori(0, QT // 2 - 1) as i:
                    tile(i * 2 + (b * QT + 1), 1, b)
                    tile(i * 2 + (b * QT + 2), 0, b)
                tile(b * QT + QT - 1, 1, b)

        def is_first(t):
            return isinstance(t, int) and t == 0

        def is_last(t):
            return isinstance(t, int) and t == LAST

        @block.sync
        def _(sp):
            for dst, src in ((hmask[:], a["hmask"]), (identb[:], a["identb"]), (ones[0:1, :], a["ones_row"]),
                             (smask[0:1, :], a["strided_masks"]),
                             (wmask[:].rearrange("p a c -> p (a c)"), a["window_masks"]), (vmask[:], a["vmask"]),
                             (wo_T[:], a["wo_T"].rearrange("(k p) n -> p k n", p=P))):
                sp.dma_start(dst, src).then_inc(s["w_in"], 16)

            def load_qk(t, p, b):
                wait(sp, "S_ready", NGR * (t - 1))
                for o in range(2):
                    for half in range(2):
                        rows = slice(o * 64 + half * 32, o * 64 + half * 32 + 32)
                        k = k_parts.rearrange("(j o r) t -> o r j t", o=2, r=2 * HD)[o]
                        sp.dma_start(Kw[p][rows, :, :].bitcast(F32), k[:, :, bass.ds(t * P + b * P, W2)]).then_inc(qk_in[p], 16)
                        q3 = q_parts.rearrange("(j o r) t -> o r j t", o=2, r=3 * HD)[o]
                        sp.dma_start(qz[p][rows, :, o, :].bitcast(F32), q3[half * HD:half * HD + 2 * HD, :, bass.ds(t * P, P)])\
                            .then_inc(qk_in[p], 16)

            sp.wait_ge(s["zeroed"], 2)
            load_qk(0, 0, 0)
            for b in range(BATCH):
                for c in range(GH):
                    for h in range(2):
                        dst = vrows[b][c * NSTR + h:(c + 1) * NSTR:2, :, :].rearrange("p g d -> p (g d)")
                        sp.dma_start(dst, qkv["v"][h * SPARSE:h * SPARSE + 1, b * (QT + 1) + 1:(b + 1) * (QT + 1), :])\
                            .then_inc(s["vrows_in"], 16)

            def tile(t, p, b):
                if not is_last(t):
                    load_qk(t + 1, 1 - p, b + 1 if isinstance(t, int) and t % QT == QT - 1 else b)
                wait(sp, "o_ready", t)
                sp.dma_start(xr[:], x_in[bass.ds(t * P, P), :]).then_inc(s["xr_in"], 16)
                if not is_first(t):
                    sp.dma_start(x_out[bass.ds((t - 1) * P, P), :], o[:]).then_inc(s["stored"], 16)

            all_tiles(sp, tile)
            sp.wait_ge(s["o_ready"], NT)
            sp.dma_start(x_out[LAST * P:NT * P, :], o[:]).then_inc(s["stored"], 16)
            sp.wait_ge(s["stored"], 16 * NT)

        @block.gpsimd
        def _(pool):
            for p in range(2):
                nc.gpsimd.memset(qz[p][:].rearrange("p j o q -> p (j o q)").bitcast(F32), 0.0).then_inc(s["zeroed"], 1)

        @block.vector
        def _(dve):
            def strided_keys(b):
                for f in range(KD):
                    keys = qkv["kS"][:, f, b * NSTR:(b + 1) * NSTR]
                    nc.vector.tensor_tensor(Ks[b][:, f, :, :], keys.unsqueeze(1).to_broadcast([P, HPB, NSTR]),
                                            hmask[:].unsqueeze(2).to_broadcast([P, HPB, NSTR]), ALU.mult)\
                        .then_inc(s["Ks_ready"], 1)

            def strided_values(b):
                nc.vector.tensor_tensor(Vs[b][:], vrows[b][:], vmask[:].unsqueeze(1).to_broadcast([P, NGR, GH * HD]),
                                        ALU.mult).then_inc(s["Vs_ready"], 1)

            def strided_tops(t):
                dve.wait_ge(s["Ss_ready"], t + 1)
                nc.vector.tensor_reduce(top_s[:], Ss_ps[:].rearrange("p (h k) -> p h k", h=HEADS), AX.X, ALU.max)\
                    .then_inc(s["top_s_ready"], 1)
                dve.wait_ge(s["top_s_ready"], t + 1)
                nc.vector.tensor_scalar(shift_s[:], top_s[:], -0.25, None, ALU.mult).then_inc(s["shift_s_ready"], 1)

            def maxima(t, gr):
                h = slice(gr * GH, (gr + 1) * GH)
                dve.wait_ge(s["S_ready"], t * NGR + gr + 1)
                nc.vector.tensor_reduce(top_w[:, h], S_ps[gr % 2][:], AX.X, ALU.max).then_inc(s["tops"], 1)
                dve.wait_ge(s["tops"], t * NGR + gr + 1)
                dve.wait_ge(s["shift_s_ready"], t + 1)
                wait(dve, "exp_done", GH * ((t - 1) * NGR + gr + 1))
                nc.vector.scalar_tensor_tensor(out=shift[:, h], in0=top_w[:, h], scalar=-0.25, in1=shift_s[:, h],
                                               op0=ALU.mult, op1=ALU.min).then_inc(s["shifts"], 1)

            def shift_strided(t):
                wait(dve, "str_exp", t)
                dve.wait_ge(s["shifts"], (t + 1) * NGR)
                nc.vector.scalar_tensor_tensor(
                    out=str_in[:].rearrange("p (h k) -> p h k", h=HEADS),
                    in0=Ss_ps[:].rearrange("p (h k) -> p h k", h=HEADS), scalar=0.25,
                    in1=shift[:].unsqueeze(2).to_broadcast([P, HEADS, NSTR]),
                    op0=ALU.mult, op1=ALU.add).then_inc(s["str_shifted"], 1)

            def take_PT0(t, gr):
                dve.wait_ge(s["turned0"], t * NGR + gr + 1)
                wait(dve, "PV_done", t * NGR + gr - 1)
                nc.vector.tensor_copy(PT[gr % 2][:, 0].rearrange("p h c -> p (h c)"), T_ps[0][:])\
                    .then_inc(s["PT0_taken"], 1)

            def denominators(t, p):
                dve.wait_ge(s["str_exp"], t + 1)
                nc.vector.tensor_reduce(den_s[:], probs_s[:].rearrange("p (h k) -> p h k", h=HEADS), AX.X, ALU.add)\
                    .then_inc(s["sums"], 1)
                dve.wait_ge(s["sums"], 2 * t + 1)
                dve.wait_ge(s["exp_done"], GH * NGR * (t + 1))
                nc.vector.tensor_tensor(den_s[:], den_s[:], den[p][:], ALU.add).then_inc(s["sums"], 1)
                dve.wait_ge(s["sums"], 2 * t + 2)
                wait(dve, "on_ready", t)
                nc.vector.reciprocal(rden[:], den_s[:]).then_inc(s["dens"], 1)

            def normalise(t):
                dve.wait_ge(s["O_ready"], t + 1)
                dve.wait_ge(s["dens"], t + 1)
                wait(dve, "O_turned", t)
                nc.vector.tensor_tensor(on[:].rearrange("p (h d) -> p h d", h=HEADS),
                                        O_ps[:, 0:D].rearrange("p (h d) -> p h d", h=HEADS),
                                        rden[:].unsqueeze(2).to_broadcast([P, HEADS, HD]), ALU.mult)\
                    .then_inc(s["on_ready"], 1)

            def output(t):
                dve.wait_ge(s["out_ready"], t + 1)
                dve.wait_ge(s["xr_in"], 16 * (t + 1))
                wait(dve, "stored", 16 * t)
                nc.vector.tensor_tensor(o[:], T_ps[1][:, 0:D], xr[:], ALU.add).then_inc(s["o_ready"], 1)

            dve.wait_ge(s["w_in"], 16 * N_IN)
            for b in range(BATCH):
                strided_keys(b)

            strided_tops(0)
            maxima(0, 0)

            def tile(t, p, b):
                for gr in range(NGR):
                    if gr < NGR - 1:
                        maxima(t, gr + 1)
                    elif not is_last(t):
                        strided_tops(t + 1)
                        maxima(t + 1, 0)
                    if gr == 2:
                        shift_strided(t)
                        if is_first(t):
                            dve.wait_ge(s["vrows_in"], 16 * BATCH * GH * 2)
                            for seq in range(BATCH):
                                strided_values(seq)
                    if gr:
                        take_PT0(t, gr - 1)
                    elif not is_first(t):
                        take_PT0(t - 1, NGR - 1)
                        denominators(t - 1, 1 - p)
                    if gr == 1 and not is_first(t):
                        normalise(t - 1)
                    if gr == 3 and not is_first(t):
                        output(t - 1)

            all_tiles(dve, tile)
            take_PT0(LAST, NGR - 1)
            denominators(LAST, 1)
            normalise(LAST)
            output(LAST)

        @block.scalar
        def _(act):
            def take_q(t, p):
                wait(act, "Ss_ready", t - 1)
                nc.scalar.copy(q[p][:], qkv["qT"][:, :, bass.ds(t * P, P)]).then_inc(s["q_ready"], 1)

            def exps(t, p, gr):
                act.wait_ge(s["shifts"], t * NGR + gr + 1)
                wait(act, "turned0", (t - 1) * NGR + gr + 1)
                wait(act, "turned1", (t - 1) * NGR + gr + 1)
                if gr == 0:
                    wait(act, "dens", t - 1)
                for h in range(GH):
                    hh = gr * GH + h
                    nc.scalar.activation(probs[gr][:, h, :], S_ps[gr % 2][:, h, :], ACT.Exp,
                                         bias=shift[:, hh:hh + 1], scale=0.25,
                                         accum_out=den[p][:, hh:hh + 1]).then_inc(s["exp_done"], 1)

            def exp_strided(t):
                act.wait_ge(s["str_shifted"], t + 1)
                wait(act, "str_turned", t)
                wait(act, "dens", t)
                nc.scalar.activation(probs_s[:], str_in[:], ACT.Exp).then_inc(s["str_exp"], 1)

            def take_PT1(t, gr):
                act.wait_ge(s["turned1"], t * NGR + gr + 1)
                wait(act, "PV_done", t * NGR + gr - 1)
                nc.scalar.copy(PT[gr % 2][:, 1].rearrange("p h c -> p (h c)"), T_ps[1][:])\
                    .then_inc(s["PT1_taken"], 1)

            def take_PTs(t):
                act.wait_ge(s["str_turned"], t + 1)
                wait(act, "O_ready", t)
                nc.scalar.copy(PTs[:].rearrange("p h c -> p (h c)"), T_ps[1][:]).then_inc(s["PTs_taken"], 1)

            def take_OT(t):
                act.wait_ge(s["O_turned"], t + 1)
                wait(act, "out_ready", t)
                nc.scalar.copy(OT[:].rearrange("p k c -> p (k c)"), T_ps[1][:, 0:D]).then_inc(s["OT_taken"], 1)

            def tile(t, p, b):
                for gr in range(NGR):
                    if not is_first(t):
                        if gr == 1:
                            take_PTs(t - 1)
                        if gr == 3:
                            take_OT(t - 1)
                    if gr < NGR - 1:
                        exps(t, p, gr + 1)
                    elif not is_last(t):
                        exps(t + 1, 1 - p, 0)
                    if gr == 2:
                        exp_strided(t)
                    if gr:
                        take_PT1(t, gr - 1)
                    elif not is_first(t):
                        take_PT1(t - 1, NGR - 1)
                    if gr == 0 and not is_last(t):
                        take_q(t + 1, 1 - p)

            take_q(0, 0)
            exps(0, 0, 0)
            all_tiles(act, tile)
            take_PT1(LAST, NGR - 1)
            take_PTs(LAST)
            take_OT(LAST)

        @block.tensor
        def _(pe):
            def scores_strided(t, p, b):
                pe.wait_ge(s["q_ready"], t + 1)
                wait(pe, "str_shifted", t)
                nc.tensor.matmul(Ss_ps[:], ones[0:1, :], smask[0:1, bass.ds((t - b * QT) * NSTR, NSTR)]
                                 .unsqueeze(1).to_broadcast([1, HEADS, NSTR]),
                                 start=True, stop=False, skip_group_check=True)
                for f in range(KD):
                    m = nc.tensor.matmul(Ss_ps[:, f * D:(f + 1) * D], q[p][:, f, :],
                                         Ks[b][:, f, :, :].rearrange("p h k -> p (h k)"),
                                         start=False, stop=True, skip_group_check=True)
                m.then_inc(s["Ss_ready"], 1)

            def scores(t, p, b, half, gr):
                first = isinstance(t, int) and t % QT == 0
                if gr == 0:
                    pe.wait_ge(qk_in[p], QK_IN * (half + 1))
                wait(pe, "exp_done", GH * (t * NGR + gr - 1))
                for h2 in range(2):
                    nc.tensor.matmul(S_ps[gr % 2][:, 2 * h2:2 * h2 + 2, :].rearrange("p h c -> p (h c)"), identb[:],
                                     wmask[:, 0 if first else 1, :], start=True, stop=False, skip_group_check=True)
                    for h in (2 * h2, 2 * h2 + 1):
                        hh = gr * GH + h
                        m = nc.tensor.matmul(S_ps[gr % 2][:, h, :], qz[p][:, hh // 2, hh % 2, :], Kw[p][:, hh // 2, :],
                                             start=False, stop=True, skip_group_check=True)
                m.then_inc(s["S_ready"], 1)

            def turn_P(t, gr, c):
                if c == 0:
                    pe.wait_ge(s["exp_done"], GH * (t * NGR + gr + 1))
                    wait(pe, "PT0_taken", t * NGR + gr)
                else:
                    wait(pe, "PT1_taken", t * NGR + gr)
                    if gr == 0:
                        wait(pe, "PTs_taken", t)
                    if gr == 2:
                        wait(pe, "o_ready", t)
                for h in range(GH):
                    m = nc.tensor.transpose(T_ps[c][:, h * P:(h + 1) * P], probs[gr][:, h, c * P:(c + 1) * P],
                                            g["ident"][:])
                m.then_inc(s[f"turned{c}"], 1)

            def gather_V(t, b, gr):
                pe.wait_ge(s["PT0_taken"], t * NGR + gr + 1)
                pe.wait_ge(s["PT1_taken"], t * NGR + gr + 1)
                if gr == 0:
                    wait(pe, "on_ready", t)
                for c in range(2):
                    for h in range(GH):
                        hh = gr * GH + h
                        m = nc.tensor.matmul(O_ps[:, hh * HD:(hh + 1) * HD], PT[gr % 2][:, c, h, :],
                                             qkv["v"][:, bass.ds(t + (b + c), 1), hh * HD:(hh + 1) * HD]
                                             .rearrange("p a d -> p (a d)"),
                                             start=(gr == 0 and c == 0 and h == 0), stop=False, skip_group_check=True)
                m.then_inc(s["PV_done"], 1)

            def turn_strided(t):
                pe.wait_ge(s["str_exp"], t + 1)
                pe.wait_ge(s["PT1_taken"], (t + 1) * NGR)
                for gr in range(NGR):
                    m = nc.tensor.transpose(T_ps[1][:, gr * P:(gr + 1) * P], probs_s[:, gr * P:(gr + 1) * P],
                                            g["ident"][:])
                m.then_inc(s["str_turned"], 1)

            def gather_strided(t, b):
                pe.wait_ge(s["PTs_taken"], t + 1)
                pe.wait_ge(s["Vs_ready"], BATCH)
                for gr in range(NGR):
                    m = nc.tensor.matmul(O_ps[:, gr * GH * HD:(gr + 1) * GH * HD], PTs[:, gr, :], Vs[b][:, gr, :],
                                         start=False, stop=True, skip_group_check=True)
                m.then_inc(s["O_ready"], 1)

            def turn_O(t, last):
                pe.wait_ge(s["on_ready"], t + 1)
                if not last:
                    pe.wait_ge(s["PT1_taken"], (t + 1) * NGR + 2)
                for k in range(KD):
                    m = nc.tensor.transpose(T_ps[1][:, k * P:(k + 1) * P], on[:, k * P:(k + 1) * P], g["ident"][:])
                m.then_inc(s["O_turned"], 1)

            def project_out(t):
                pe.wait_ge(s["OT_taken"], t + 1)
                for k in range(KD):
                    m = nc.tensor.matmul(T_ps[1][:, 0:D], OT[:, k, :], wo_T[:, k, :],
                                         start=(k == 0), stop=(k == KD - 1))
                m.then_inc(s["out_ready"], 1)

            pe.wait_ge(s["w_in"], 16 * N_IN)
            pe.wait_ge(s["Ks_ready"], KD * BATCH)
            scores_strided(0, 0, 0)
            scores(0, 0, 0, 0, 0)

            def tile(t, p, b, half):
                last = is_last(t)
                prev_b = b - 1 if isinstance(t, int) and t % QT == 0 else b
                next_b = b + 1 if isinstance(t, int) and t % QT == QT - 1 else b
                for gr in range(NGR):
                    if gr < NGR - 1:
                        scores(t, p, b, half, gr + 1)
                    elif not last:
                        scores_strided(t + 1, 1 - p, next_b)
                        scores(t + 1, 1 - p, next_b, half + p, 0)
                    before = [(t, b, gr - n) if gr >= n else (t - 1, prev_b, gr - n + NGR) for n in (1, 2)]
                    turned, used = [None if is_first(t) and gr < n else v for n, v in zip((1, 2), before)]
                    if gr == 1 and not is_first(t):
                        turn_strided(t - 1)
                    if gr == 3 and not is_first(t):
                        turn_O(t - 1, False)
                    if turned:
                        turn_P(turned[0], turned[2], 0)
                    if gr == 3 and not is_first(t):
                        project_out(t - 1)
                    if used:
                        gather_V(*used)
                    if gr == 1 and not is_first(t):
                        gather_strided(t - 1, prev_b)
                    if turned:
                        turn_P(turned[0], turned[2], 1)

            for b in range(BATCH):
                n = b * QT // 2
                tile(b * QT, 0, b, n)
                with pe.Fori(0, QT // 2 - 1) as i:
                    tile(i * 2 + (b * QT + 1), 1, b, i + n)
                    tile(i * 2 + (b * QT + 2), 0, b, i + (n + 1))
                tile(b * QT + QT - 1, 1, b, n + QT // 2 - 1)
            turn_P(LAST, NGR - 1, 0)
            gather_V(LAST, BATCH - 1, NGR - 2)
            turn_P(LAST, NGR - 1, 1)
            turn_strided(LAST)
            gather_V(LAST, BATCH - 1, NGR - 1)
            gather_strided(LAST, BATCH - 1)
            turn_O(LAST, True)
            project_out(LAST)


def attention(nc, g, a, x_in, done_dram, x_mid, x_out):
    with ExitStack() as ctx:
        r = Room(nc, ctx, "qkv_out")
        qkv = dict(qT=r.sb("qT", [P, KD, TOK]), kS=r.sb("kS", [P, KD, BATCH * NSTR]),
                   v=r.sb("v", [P, BATCH * (QT + 1), D]))
        q_parts = nc.dram_tensor("q_parts", (3 * D, TOK), F32).ap()
        k_parts = nc.dram_tensor("k_parts", (2 * D, BATCH * SPAD), F32).ap()
        qkv_block(nc, g, a, qkv, x_in, done_dram, x_mid, q_parts, k_parts)
        attend_block(nc, g, a, qkv, q_parts, k_parts, x_mid, x_out)



def macaron_program(nc, out, ins):
    def scratch(name, shape):
        return nc.dram_tensor(name, shape, F32).ap()

    Room.sems = []
    a = ins
    stream = [a["x"]] + [scratch(f"x{i}", (TOK, D)) for i in range(1, 6)] + [out.rearrange("b t d -> (b t) d")]
    proj_T = scratch("proj_T", (2 * INNER, BATCH * HPAD))
    bc_T = scratch("bc_T", (2 * STATE, TOK + BLK))
    with ExitStack() as ctx:
        r = Room(nc, ctx, "g")
        g = dict(ident=r.sb("ident", [P, P]), w_up=r.sb("w_up", [P, KD, FH]), w_down=r.sb("w_down", [P, FM, D]),
                 b_up=r.sb("b_up", [P, FM]), half_bias=r.sb("half_bias", [P, D]),
                 neg_A=r.sb("neg_A", [P, IB, STATE]), minus_half=r.sb("minus_half", [P, STATE]),
                 zeros=r.sb("zeros", [P, D]), take=r.sb("take", [P, TOPK * NT], I32),
                 share=r.sb("share", [P, TOPK * NT]))
        fold_block(nc, g, a)
        ffn_block(nc, "ffn0", g, stream[0], stream[1])
        inproj_block(nc, g, a, stream[1], proj_T)
        mamba_block(nc, g, a, stream[1], proj_T, bc_T, stream[2])
        ffn_block(nc, "ffn1", g, stream[2], stream[3])
        recycle_semaphores(nc)
        for m in range(2):
            if m:
                attention(nc, g, a, stream[3], done, stream[4], stream[5])
            slots = scratch(f"slots{m}", (NE * CAP, D))
            done = scratch(f"done{m}", (NE * CAP, D))
            route_block(nc, f"route{m}", g, a, stream[3 + 2 * m], slots)
            expert_block(nc, f"expert{m}", g, a, slots, done)
        combine_block(nc, "combine", g, stream[5], done, stream[6])



def layouts(np, v):
    def columns(vec):
        return vec.reshape(-1, P).T

    def far_columns(w):
        return w.reshape(FAR, 2, 2, FM // 2, P).transpose(4, 0, 1, 2, 3).reshape(P, -1)

    wqkv = v["L1_attn_w_qkv"]
    up_w = v["L0_ffn_up_weights"].transpose(0, 3, 2, 1)
    down_w = v["L0_ffn_down_weights"][::-1].transpose(0, 2, 3, 1)
    return dict(
        x=v["L0_attn_hidden_states"].reshape(TOK, D),
        w_exp_T=v["L0_ffn_W_exp"].T, w_con=v["L0_ffn_W_con"], b_exp=columns(v["L0_ffn_b_exp"]),
        up_w=up_w.reshape(STAGES, 2 * FH), down_w=down_w.reshape(STAGES, 2 * FH),
        up_cols=far_columns(up_w[LOCAL:]), down_cols=far_columns(down_w[:FAR]),
        up_bias=columns(v["L0_ffn_up_bias"]), b_con=v["L0_ffn_b_con"], down_bias=v["L0_ffn_down_bias"],
        A_log=v["L0_attn_A_log"], in_proj_T=v["L0_attn_in_proj_w"].T,
        conv_w=v["L0_attn_conv_w"].reshape(INNER, TAPS), conv_b=columns(v["L0_attn_conv_b"]),
        x_proj_T=v["L0_attn_x_proj_w"].T, dt_proj_T=v["L0_attn_dt_proj_w"].T,
        dt_bias=columns(v["L0_attn_dt_proj_b"]), D=columns(v["L0_attn_D"]), out_proj_T=v["L0_attn_out_proj_w"].T,
        xd_ln_w=np.concatenate([v["L0_attn_dt_ln_w"], v["L0_attn_b_ln_w"], v["L0_attn_c_ln_w"]])[:, None],
        gate_T=v["L1_ffn_gate_w"].T, fc1_T=v["L1_ffn_fc1_w"].transpose(2, 0, 1).reshape(D, NE * EH),
        fc2=v["L1_ffn_fc2_w"].reshape(NE * EH, D), b2=v["L1_ffn_fc2_b"].reshape(-1),
        b1=v["L1_ffn_fc1_b"].reshape(NE, EM, P).transpose(0, 2, 1).reshape(NE * P, EM),
        wq_T=wqkv[0:D].T, wk_T=wqkv[D:2 * D].T, wv_T=wqkv[2 * D:3 * D].T, wo_T=v["L1_attn_w_out"].T)


def constants(np):
    p = np.arange(P)
    f32, bf16 = np.dtype(np.float32), mybir.dt.np(BF16)
    row, col = p[:, None], p[None, :]
    keep = np.ones((P, NBLK + 1), f32)
    keep[:, 0::NBLK // BATCH] = 0
    own = np.where(col <= row, 0, NEG)
    before = np.where((col >= row) | (col % SPARSE == 0), 0, NEG)
    none = np.full((P, P), NEG)
    window = np.concatenate([none, own] * 2 + [before, own] * 2, axis=1)
    strided = np.concatenate([np.where(np.arange(NSTR) * SPARSE < P * (i - 1), 0, NEG) for i in range(QT)])[None]
    return dict(
        ident=np.eye(P, dtype=f32), keep=keep,
        rank=np.tile(NE - np.arange(NE), (P, 1)).astype(f32),
        first_slot=np.tile(CAP * np.arange(NE), (P, 1)).astype(f32),
        outside=(NE * CAP + np.arange(TOPK * NT)[None] * P + row).astype(f32),
        earlier=(row < col).astype(f32), ones=np.ones((P, P), f32),
        hmask=(row // HD == np.arange(HPB)).astype(f32),
        vmask=(row // NSTR == np.arange(GH * HD) // HD).astype(f32),
        identb=np.eye(P).astype(bf16), ones_row=np.ones((1, P)).astype(bf16),
        window_masks=window.astype(bf16), strided_masks=strided.astype(bf16))


def kernel(**inputs):
    import numpy as np
    import concourse.bacc as bacc
    from concourse.bass_utils import run_bass_kernel_spmd

    nc = bacc.Bacc("TRN2", target_bir_lowering=False, num_devices=1)
    arrays, ins = {}, {}
    for name, value in {**layouts(np, inputs), **constants(np)}.items():
        value = np.ascontiguousarray(value)
        arrays[f"in_{name}_dram"] = value
        ins[name] = nc.dram_tensor(f"in_{name}_dram", value.shape, mybir.dt.from_np(value.dtype),
                                   kind="ExternalInput").ap()
    out = nc.dram_tensor("out_0_dram", (BATCH, SEQ, D), F32, kind="ExternalOutput").ap()
    macaron_program(nc, out, ins)
    result = run_bass_kernel_spmd(nc, [arrays], core_ids=[0])
    return result.results[0]["out_0_dram"]
```
